# Optimizing a Trainium2 kernel written in Bass

```python
import numpy as np
import jax
import jax.numpy as jnp

def _softmax(x, axis=-1):
    return jax.nn.softmax(x, axis=axis)

def _gelu(x):
    return jax.nn.gelu(x, approximate=True)

def _silu(x):
    return jax.nn.silu(x)

def _sigmoid(x):
    return jax.nn.sigmoid(x)

def _layernorm(x, axis=-1, eps=1e-05):
    m = jnp.mean(x, axis=axis, keepdims=True)
    v = jnp.var(x, axis=axis, keepdims=True)
    return (x - m) / jnp.sqrt(v + eps)

def _scatter_add(tgt, idx, src, axis=0):
    return tgt.at[idx].add(src)

def _segment_sum(src, seg, n):
    return jax.ops.segment_sum(src, seg, n)
kernel_name = 'mk_gnn_preln_d2_gnn_r8_c17546'

def setup_inputs(seed: int=0):
    np.random.seed(seed)
    _w = jnp.asarray

    def _rec_inputs():
        import jax
        import jax.numpy as jnp
        _gk = jax.random.key(seed)
        x = -8.776e-05 + 1 * jax.random.normal(jax.random.fold_in(_gk, 1), (6250, 256), jnp.float32)
        src = jax.random.randint(jax.random.fold_in(_gk, 2), (100000,), 0, 6250, jnp.int32)
        dst = jax.random.randint(jax.random.fold_in(_gk, 3), (100000,), 0, 6250, jnp.int32)
        _o = jnp.argsort(dst, stable=True)
        src = src[_o]
        dst = dst[_o]
        edge_attr_64 = 0.000151818 + 1.00006 * jax.random.normal(jax.random.fold_in(_gk, 12), (100000, 64), jnp.float32)
        edge_type_6 = jax.random.randint(jax.random.fold_in(_gk, 14), (100000,), 0, 6, jnp.int32)
        edge_weight = jax.random.uniform(jax.random.fold_in(_gk, 15), (100000,), jnp.float32, 0.0, 4.99999)
        node_type_3 = jax.random.randint(jax.random.fold_in(_gk, 16), (6250,), 0, 3, jnp.int32)
        return (x, src, dst, edge_attr_64, edge_type_6, edge_weight, node_type_3)
    x, src, dst, edge_attr_64, edge_type_6, edge_weight, node_type_3 = _rec_inputs()

    def _L0_gnn_setup():
        import jax, jax.numpy as jnp
        import numpy as np
        H = 256
        R = 64
        N = 2500
        E = 40000
        CUTOFF_LO = 0.0
        CUTOFF_UP = 5.0
        LN_EPS = 1e-05

        def _layernorm(x, g, b):
            mu = jnp.mean(x, axis=-1, keepdims=True)
            var = jnp.var(x, axis=-1, keepdims=True)
            return (x - mu) * jax.lax.rsqrt(var + LN_EPS) * g + b

        def _cosine_cutoff(r):
            c = 0.5 * (jnp.cos(r * (jnp.pi / CUTOFF_UP)) + 1.0)
            return c * (r < CUTOFF_UP).astype(r.dtype)
        key = jax.random.key(seed)
        ks = jax.random.split(key, 16)

        def xavier(k, shape):
            fan_in, fan_out = (shape[1], shape[0])
            lim = np.sqrt(6.0 / (fan_in + fan_out))
            return jax.random.uniform(k, shape, jnp.float32, -lim, lim)
        x = jax.random.normal(ks[0], (N, H), jnp.float32)
        edge_index = jax.random.randint(ks[1], (2, E), 0, N, jnp.int64)
        edge_weight = jax.random.uniform(ks[2], (E,), jnp.float32, 0.0, CUTOFF_UP)
        edge_attr = jax.random.normal(ks[3], (E, R), jnp.float32)
        return {'x': x, 'edge_index': edge_index, 'edge_weight': edge_weight, 'edge_attr': edge_attr, 'ln_g': jnp.ones((H,), jnp.float32), 'ln_b': jnp.zeros((H,), jnp.float32), 'Wq': xavier(ks[4], (H, H)), 'bq': jnp.zeros((H,), jnp.float32), 'Wk': xavier(ks[5], (H, H)), 'bk': jnp.zeros((H,), jnp.float32), 'Wv': xavier(ks[6], (H, H)), 'bv': jnp.zeros((H,), jnp.float32), 'Wo': xavier(ks[7], (H, H)), 'bo': jnp.zeros((H,), jnp.float32), 'Wdk': xavier(ks[8], (H, R)), 'bdk': jnp.zeros((H,), jnp.float32), 'Wdv': xavier(ks[9], (H, R)), 'bdv': jnp.zeros((H,), jnp.float32)}
    _L0_gnn_all = _L0_gnn_setup()
    _L0_gnn_in = {k: v for k, v in _L0_gnn_all.items() if k in ('ln_g', 'ln_b', 'Wq', 'bq', 'Wk', 'bk', 'Wv', 'bv', 'Wo', 'bo', 'Wdk', 'bdk', 'Wdv', 'bdv')}
    del _L0_gnn_all

    def _L1_gnn_setup():
        import jax, jax.numpy as jnp
        import numpy as np
        N, E, D, T, R, H = (6250, 50000, 256, 3, 6, 4)
        DK = D // H
        OUT = H * DK
        LN_EPS = 1e-05
        key = jax.random.key(seed)
        ks = jax.random.split(key, 16)
        std = 0.02
        f32 = jnp.float32
        inp = {'x': jax.random.normal(ks[0], (N, D), f32), 'Wk': jax.random.normal(ks[1], (T, D, OUT), f32) * std, 'bk': jnp.zeros((T, OUT), f32), 'Wq': jax.random.normal(ks[2], (T, D, OUT), f32) * std, 'bq': jnp.zeros((T, OUT), f32), 'Wv': jax.random.normal(ks[3], (T, D, OUT), f32) * std, 'bv': jnp.zeros((T, OUT), f32), 'Wa': jax.random.normal(ks[4], (T, OUT, OUT), f32) * std, 'ba': jnp.zeros((T, OUT), f32), 'rel_pri': jnp.ones((R, H), f32), 'rel_att': jax.random.normal(ks[5], (R, H, DK, DK), f32) * (1.0 / np.sqrt(DK)), 'rel_msg': jax.random.normal(ks[6], (R, H, DK, DK), f32) * (1.0 / np.sqrt(DK)), 'skip': jnp.ones((T,), f32), 'ln_g': jnp.ones((T, OUT), f32), 'ln_b': jnp.zeros((T, OUT), f32), 'node_type': jax.random.randint(ks[7], (N,), 0, T), 'edge_src': jax.random.randint(ks[8], (E,), 0, N), 'edge_dst': jax.random.randint(ks[9], (E,), 0, N), 'edge_type': jax.random.randint(ks[10], (E,), 0, R), 'n_heads': H}
        return inp
    _L1_gnn_all = _L1_gnn_setup()
    _L1_gnn_in = {k: v for k, v in _L1_gnn_all.items() if k in ('Wk', 'bk', 'Wq', 'bq', 'Wv', 'bv', 'Wa', 'ba', 'rel_pri', 'rel_att', 'rel_msg', 'skip', 'ln_g', 'ln_b')}
    del _L1_gnn_all
    return {'x': x, 'src': src, 'dst': dst, 'edge_attr_64': edge_attr_64, 'edge_type_6': edge_type_6, 'edge_weight': edge_weight, 'node_type_3': node_type_3, 'L0_gnn_ln_g': _L0_gnn_in['ln_g'], 'L0_gnn_ln_b': _L0_gnn_in['ln_b'], 'L0_gnn_Wq': _L0_gnn_in['Wq'], 'L0_gnn_bq': _L0_gnn_in['bq'], 'L0_gnn_Wk': _L0_gnn_in['Wk'], 'L0_gnn_bk': _L0_gnn_in['bk'], 'L0_gnn_Wv': _L0_gnn_in['Wv'], 'L0_gnn_bv': _L0_gnn_in['bv'], 'L0_gnn_Wo': _L0_gnn_in['Wo'], 'L0_gnn_bo': _L0_gnn_in['bo'], 'L0_gnn_Wdk': _L0_gnn_in['Wdk'], 'L0_gnn_bdk': _L0_gnn_in['bdk'], 'L0_gnn_Wdv': _L0_gnn_in['Wdv'], 'L0_gnn_bdv': _L0_gnn_in['bdv'], 'L1_gnn_Wk': _L1_gnn_in['Wk'], 'L1_gnn_bk': _L1_gnn_in['bk'], 'L1_gnn_Wq': _L1_gnn_in['Wq'], 'L1_gnn_bq': _L1_gnn_in['bq'], 'L1_gnn_Wv': _L1_gnn_in['Wv'], 'L1_gnn_bv': _L1_gnn_in['bv'], 'L1_gnn_Wa': _L1_gnn_in['Wa'], 'L1_gnn_ba': _L1_gnn_in['ba'], 'L1_gnn_rel_pri': _L1_gnn_in['rel_pri'], 'L1_gnn_rel_att': _L1_gnn_in['rel_att'], 'L1_gnn_rel_msg': _L1_gnn_in['rel_msg'], 'L1_gnn_skip': _L1_gnn_in['skip'], 'L1_gnn_ln_g': _L1_gnn_in['ln_g'], 'L1_gnn_ln_b': _L1_gnn_in['ln_b']}

def reference(x, src, dst, edge_attr_64, edge_type_6, edge_weight, node_type_3, L0_gnn_ln_g, L0_gnn_ln_b, L0_gnn_Wq, L0_gnn_bq, L0_gnn_Wk, L0_gnn_bk, L0_gnn_Wv, L0_gnn_bv, L0_gnn_Wo, L0_gnn_bo, L0_gnn_Wdk, L0_gnn_bdk, L0_gnn_Wdv, L0_gnn_bdv, L1_gnn_Wk, L1_gnn_bk, L1_gnn_Wq, L1_gnn_bq, L1_gnn_Wv, L1_gnn_bv, L1_gnn_Wa, L1_gnn_ba, L1_gnn_rel_pri, L1_gnn_rel_att, L1_gnn_rel_msg, L1_gnn_skip, L1_gnn_ln_g, L1_gnn_ln_b):
    import jax
    import jax.numpy as jnp

    def _L0_gnn_ref(x, edge_index, edge_weight, edge_attr, ln_g, ln_b, Wq, bq, Wk, bk, Wv, bv, Wo, bo, Wdk, bdk, Wdv, bdv):
        import jax, jax.numpy as jnp
        import numpy as np
        H = 256
        R = 64
        N = 2500
        E = 40000
        CUTOFF_LO = 0.0
        CUTOFF_UP = 5.0
        LN_EPS = 1e-05

        def _layernorm(x, g, b):
            mu = jnp.mean(x, axis=-1, keepdims=True)
            var = jnp.var(x, axis=-1, keepdims=True)
            return (x - mu) * jax.lax.rsqrt(var + LN_EPS) * g + b

        def _cosine_cutoff(r):
            c = 0.5 * (jnp.cos(r * (jnp.pi / CUTOFF_UP)) + 1.0)
            return c * (r < CUTOFF_UP).astype(r.dtype)
        src = edge_index[0]
        dst = edge_index[1]
        x_norm = _layernorm(x, ln_g, ln_b)
        q = x_norm @ Wq.T + bq
        k = x_norm @ Wk.T + bk
        v = x_norm @ Wv.T + bv
        dk = jax.nn.silu(edge_attr @ Wdk.T + bdk)
        dv = jax.nn.silu(edge_attr @ Wdv.T + bdv)
        q_i = q[dst]
        k_j = k[src]
        v_j = v[src]
        attn = jnp.sum(q_i * k_j * dk, axis=1)
        attn = jax.nn.silu(attn) * _cosine_cutoff(edge_weight)
        msg = v_j * dv * attn[:, None]
        agg = jax.ops.segment_sum(msg, dst, num_segments=x.shape[0])
        out = agg @ Wo.T + bo
        return x + out

    def _L1_gnn_ref(x, Wk, bk, Wq, bq, Wv, bv, Wa, ba, rel_pri, rel_att, rel_msg, skip, ln_g, ln_b, node_type, edge_src, edge_dst, edge_type, n_heads):
        import jax, jax.numpy as jnp
        import numpy as np
        N, E, D, T, R, H = (6250, 50000, 256, 3, 6, 4)
        DK = D // H
        OUT = H * DK
        LN_EPS = 1e-05
        n, d = x.shape
        r, h = rel_pri.shape
        dk = rel_att.shape[-1]
        out_dim = h * dk
        ar = jnp.arange(n)

        def typed_linear(inp_, W, b):
            y = jnp.einsum('ni,tio->tno', inp_, W) + b[:, None, :]
            return y[node_type, ar]
        k = typed_linear(x, Wk, bk).reshape(n, h, dk)
        q = typed_linear(x, Wq, bq).reshape(n, h, dk)
        v = typed_linear(x, Wv, bv).reshape(n, h, dk)
        k_rel = jnp.einsum('nhd,rhde->rnhe', k, rel_att)
        v_rel = jnp.einsum('nhd,rhde->rnhe', v, rel_msg)
        key_e = k_rel[edge_type, edge_src]
        val_e = v_rel[edge_type, edge_src]
        att = (q[edge_dst] * key_e).sum(-1) * rel_pri[edge_type] / jnp.sqrt(jnp.float32(dk))
        seg = edge_dst * r + edge_type
        S = n * r
        amax = jax.ops.segment_max(att, seg, num_segments=S)
        amax = jax.lax.stop_gradient(jnp.where(jnp.isfinite(amax), amax, 0.0))
        ex = jnp.exp(att - amax[seg])
        denom = jax.ops.segment_sum(ex, seg, num_segments=S)
        w = ex / denom[seg]
        hsum = jax.ops.segment_sum(w[:, :, None] * val_e, seg, num_segments=S)
        cnt = jax.ops.segment_sum(jnp.ones((seg.shape[0],), x.dtype), seg, num_segments=S)
        t_rel = hsum.reshape(n, r, out_dim)
        present = cnt.reshape(n, r) > 0
        nrel = jnp.maximum(present.sum(-1), 1).astype(x.dtype)
        t = (t_rel * present[..., None].astype(x.dtype)).sum(1) / nrel[:, None]
        trans = typed_linear(t, Wa, ba)
        alpha = jax.nn.sigmoid(skip)[node_type][:, None]
        out = trans * alpha + x * (1.0 - alpha)
        mu = out.mean(-1, keepdims=True)
        var = out.var(-1, keepdims=True)
        normed = (out - mu) * jax.lax.rsqrt(var + LN_EPS) * ln_g[node_type] + ln_b[node_type]
        has_msg = present.any(-1)[:, None]
        return jnp.where(has_msg, normed, x)
    edge_index = jnp.stack([src, dst])
    h = jnp.maximum(_layernorm(x, axis=-1), 0.0)
    x = x + _L0_gnn_ref(h, edge_index, edge_weight, edge_attr_64, L0_gnn_ln_g, L0_gnn_ln_b, L0_gnn_Wq, L0_gnn_bq, L0_gnn_Wk, L0_gnn_bk, L0_gnn_Wv, L0_gnn_bv, L0_gnn_Wo, L0_gnn_bo, L0_gnn_Wdk, L0_gnn_bdk, L0_gnn_Wdv, L0_gnn_bdv)
    h = jnp.maximum(_layernorm(x, axis=-1), 0.0)
    x = x + _L1_gnn_ref(h, L1_gnn_Wk, L1_gnn_bk, L1_gnn_Wq, L1_gnn_bq, L1_gnn_Wv, L1_gnn_bv, L1_gnn_Wa, L1_gnn_ba, L1_gnn_rel_pri, L1_gnn_rel_att, L1_gnn_rel_msg, L1_gnn_skip, L1_gnn_ln_g, L1_gnn_ln_b, node_type_3, src, dst, edge_type_6, 4)
    return x

_drawn_inputs = setup_inputs


def setup_inputs(seed=0):
    import zlib

    import numpy as np

    out = dict(_drawn_inputs(seed))
    spreads = {'L0_gnn_ln_g': (1.0, 0.2),
     'L0_gnn_ln_b': (0.0, 0.1),
     'L0_gnn_bq': (0.0, 0.1),
     'L0_gnn_bk': (0.0, 0.1),
     'L0_gnn_bv': (0.0, 0.1),
     'L0_gnn_bo': (0.0, 0.33),
     'L0_gnn_bdk': (0.0, 0.1),
     'L0_gnn_bdv': (0.0, 0.1),
     'L1_gnn_bk': (0.0, 0.8),
     'L1_gnn_bq': (0.0, 0.8),
     'L1_gnn_bv': (0.0, 0.787),
     'L1_gnn_ba': (0.0, 0.1),
     'L1_gnn_rel_pri': (1.0, 0.6),
     'L1_gnn_skip': (1.0, 0.6),
     'L1_gnn_ln_g': (1.0, 0.2),
     'L1_gnn_ln_b': (0.0, 0.412)}
    factors = {'L1_gnn_Wk': 8.0, 'L1_gnn_Wq': 8.0, 'L1_gnn_rel_att': 8.0}
    for name, (base, spread) in spreads.items():
        noise = np.random.default_rng([zlib.crc32(name.encode()), seed]).standard_normal(out[name].shape)
        drawn = base * np.exp(spread * noise) if base else spread * noise
        out[name] = jnp.asarray(drawn.astype(out[name].dtype))
    for name, factor in factors.items():
        out[name] = (out[name] * factor).astype(out[name].dtype)
    return out
```

```python
from contextlib import ExitStack

import numpy as np

import concourse.bass as bass
from concourse import mybir

F32 = mybir.dt.float32
F32R = mybir.dt.float32r
BF16 = mybir.dt.bfloat16
I32 = mybir.dt.int32
ALU = mybir.AluOpType
ACT = mybir.ActivationFunctionType
AX = mybir.AxisListType.X
ds = bass.ds

P = 128
N, E, D, R = 6250, 100000, 256, 64
TYPES, RELS, HEADS = 3, 6, 4
DK = D // HEADS
HALF = D // P
EPS = 1e-5
CUTOFF = 5.0

SUB = 20
SEG = SUB * RELS
PER_GROUP = 6
GROUP = SUB * PER_GROUP
GROUPS = -(-N // GROUP)
SUBS = GROUPS * PER_GROUP
NP = GROUPS * GROUP

MINI = 32
MINIS = E // MINI
PER_PART = 800
EP = P * PER_PART
REAL_PARTS = E // PER_PART
T0, T1 = 4, 3
CH0, CH1 = T0 * P, T1 * P
U = 8
BIG = 1e30
FLOOR = -1e25
MIN_STEPS = 3
PARTS = 3
Q_ROW = PARTS * D + 2
SUB_ROWS, SUB_COLS = 106, 3
assert SUB_ROWS * SUB_COLS == SUBS and REAL_PARTS * PER_PART == E


class Item:

    def __init__(self, i, off, unroll):
        self.i, self.off, self.unroll = i, off, unroll

    def slot(self, depth):
        return self.off % depth

    def prev(self, n=1):
        return Item(self.i, self.off - n, self.unroll)

    def count(self, lag=0, per=1, extra=0):
        if isinstance(self.i, int):
            return (self.unroll * self.i + self.off + 1 - lag) * per + extra
        return self.i * (self.unroll * per) + ((self.off + 1 - lag) * per + extra)

    def round(self, ahead=1):
        return self.i + (self.off // self.unroll + ahead)

    @property
    def index(self):
        return self.i * self.unroll + self.off


def wait(eng, sem, item, lag=0, per=1, extra=0):
    value = item.count(lag, per, extra)
    if not (isinstance(value, int) and value <= 0):
        eng.wait_ge(sem, value)


def hold(eng, held, sem, value):
    eng.wait_ge(sem, value)
    eng.sem_inc(held, 1)


def wait_slot(eng, sems, item, dmas=1):
    eng.wait_ge(sems[item.slot(item.unroll)], item.round() * (16 * dmas))


def wait_pair(eng, sems, item):
    eng.wait_ge(sems[item.slot(2)], item.i * (8 * item.unroll) + 16 * (item.off // 2))


def run_stages(eng, n, stages, unroll):
    most = max(lag for lag, _ in stages)
    peel = -(-(most + unroll) // unroll)

    def step(i, u, whole):
        for lag, f in stages:
            item = Item(i, u - lag, unroll)
            if whole or 0 <= item.index < n:
                f(item)

    for s in range(peel * unroll):
        step(s // unroll, s % unroll, False)
    with eng.Fori(peel, n // unroll) as i:
        for u in range(unroll):
            step(i, u, True)
    for s in range(n // unroll * unroll, n + most):
        step(s // unroll, s % unroll, False)


def chunk_steps(eng, spare):
    return eng.value_load(spare[0:1, 0:1], min_val=0, max_val=1 << 20) + MIN_STEPS


def run_chunks(eng, steps, stages):
    most = max(lag for lag, _ in stages)
    for s in range(2 * U):
        for lag, f in stages:
            if s >= lag:
                f(Item(s // U, s % U - lag, U))
    with eng.Fori(2, steps) as i:
        for u in range(U):
            for lag, f in stages:
                f(Item(i, u - lag, U))
    for e in range(most):
        for lag, f in stages:
            if e < lag:
                f(Item(steps, e - lag, U))


def halves(ap):
    return ap.rearrange("(c p) n -> p c n", p=P)


def build(nc, x, rec, edge_feat_t, node_type, w0, out):
    with ExitStack() as top:
        def sem(name):
            return nc.alloc_semaphore(name=name)

        def sems(name, n):
            return [sem(f"{name}{k}") for k in range(n)]

        def keep(name, shape, dt=F32):
            return top.enter_context(nc.sbuf_tensor(name, shape, dt))

        def dram(name, shape, dt=F32):
            return nc.dram_tensor(name, shape, dt, kind="Internal").ap()

        rec_d = dram("edge_records", [EP, 4])
        key_d = dram("segment_keys", [1, EP])
        span_d = dram("mini_spans", [2, MINIS])
        range_d = dram("block_ranges", [2, SUBS])
        q0_d = dram("q0_table", [GROUPS * P, Q_ROW], BF16)
        kv0_d = dram("kv0_table", [NP, 2 * D])
        xh_d = dram("x_plus_h", [NP, D])
        agg_d = dram("agg0_table", [(GROUPS + 1) * GROUP, D])
        x1_d, h1_d = dram("x1", [NP, D]), dram("h1", [NP, D])
        kv1_d = dram("kv1_table", [NP, 2 * D])
        qrel_d = dram("q_by_relation", [SUBS, P, HALF * SEG])
        acc_d = dram("acc1_table", [(SUBS + 1) * SEG, D + HEADS])

        ident = keep("ident", [P, P])
        iota = keep("iota", [P, GROUP])
        eps = keep("eps", [P, 1])
        runs0, runs1 = keep("runs0", [1, GROUPS + 1, 2], I32), keep("runs1", [1, SUBS + 1, 2], I32)
        lo0, n0, lo1, n1 = runs0[:, :, 0], runs0[:, :, 1], runs1[:, :, 0], runs1[:, :, 1]
        steps0, steps1 = keep("steps0", [1, 1], I32), keep("steps1", [1, 1], I32)

        c = dict(locals())
        before = nc.snapshot_sems()
        prepare(nc, c)
        nodes_0(nc, c)
        edges_0(nc, c)
        nc.clear_and_free_semaphores(nc.allocated_since(before))
        nc.all_engine_barrier()
        nodes_1(nc, c)
        edges_1(nc, c)
        nodes_out(nc, c)


def prepare(nc, c):
    sem, dram = c["sem"], c["dram"]
    w0 = c["w0"]
    with ExitStack() as ctx:
        def sb(name, shape, dt=F32):
            return ctx.enter_context(nc.sbuf_tensor(name, shape, dt))

        rec_in = sb("rec_in", [P, PER_PART, 4], I32)
        rec_out = sb("rec_out", [P, PER_PART, 4])
        key = sb("key", [P, PER_PART])
        clip = sb("clip", [P, PER_PART])
        cosine = sb("cosine", [P, PER_PART])
        half_pi = sb("half_pi", [P, 1])
        span = sb("span", [REAL_PARTS, 2, PER_PART // MINI])
        span_all = sb("span_all", [SUB_ROWS, 2, MINIS])
        ranks = sb("ranks", [SUB_ROWS, 2, MINIS])
        begin = sb("begin", [SUB_ROWS, SUB_COLS])
        end = sb("end", [SUB_ROWS, SUB_COLS])
        inside = sb("inside", [SUB_ROWS, MINIS])
        junk = sb("junk", [SUB_ROWS, MINIS])
        edge_range = sb("edge_range", [SUB_ROWS, 2, SUB_COLS])
        row = sb("row", [1, 2, SUBS])
        lo_f, len_f = sb("lo_f", [1, SUBS]), sb("len_f", [1, SUBS])
        lo0_f, hi0_f = sb("lo0_f", [1, GROUPS]), sb("hi0_f", [1, GROUPS])
        total = sb("total", [1, 2])
        total_i = sb("total_i", [1, 2], I32)

        loaded, consts_loaded = sem("prep_loaded"), sem("prep_consts")
        filled = sem("prep_filled")
        clipped, cosine_ready = sem("prep_clipped"), sem("prep_cosine")
        span_ready, span_stored, span_back = sem("span_ready"), sem("span_stored"), sem("span_back")
        rec_ready, stored = sem("rec_ready"), sem("prep_stored")
        range_ready, range_stored, row_back = sem("range_ready"), sem("range_stored"), sem("row_back")
        link_sem = sem("prep_chain")

        with nc.Block() as block:
            @block.sync
            def _(sp):
                sp.dma_start(rec_in[:], c["rec"].rearrange("(p t) f -> p t f", p=P)).then_inc(loaded, 16)
                sp.dma_start(ranks[:], w0["ranks"].rearrange("a (o n) -> o a n", o=1)
                             .to_broadcast([SUB_ROWS, 2, MINIS])).then_inc(consts_loaded, 16)
                sp.dma_start(begin[:], w0["begin"]).then_inc(consts_loaded, 16)
                sp.dma_start(c["ident"][:], w0["ident"]).then_inc(consts_loaded, 16)
                sp.dma_start(c["iota"][:], w0["iota"].to_broadcast([P, GROUP])).then_inc(consts_loaded, 16)
                sp.wait_ge(span_ready, 2)
                sp.dma_start(c["span_d"].rearrange("a (p m) -> p a m", p=REAL_PARTS),
                             span[:]).then_inc(span_stored, 16)
                sp.wait_ge(span_stored, 16)
                sp.dma_start(span_all[:], c["span_d"].rearrange("a (o n) -> o a n", o=1)
                             .to_broadcast([SUB_ROWS, 2, MINIS])).then_inc(span_back, 16)
                sp.wait_ge(rec_ready, 1)
                sp.dma_start(c["rec_d"].rearrange("(p t) f -> p t f", p=P), rec_out[:]).then_inc(stored, 16)
                sp.dma_start(c["key_d"].rearrange("o (p t) -> (o p) t", p=P), key[:]).then_inc(stored, 16)
                sp.wait_ge(range_ready, 2 * SUB_COLS)
                with nc.allow_non_contiguous_dma(reason="a few hundred single numbers"):
                    sp.dma_start(c["range_d"].rearrange("a (q p) -> p a q", p=SUB_ROWS),
                                 edge_range[:]).then_inc(range_stored, 16)
                sp.wait_ge(range_stored, 16)
                sp.dma_start(row[:], c["range_d"].rearrange("(o a) n -> o a n", o=1)).then_inc(row_back, 16)
                sp.wait_ge(row_back, 16)
                sp.wait_ge(stored, 32)

            @block.scalar
            def _(act):
                act.wait_ge(clipped, 1)
                act.wait_ge(filled, 1)
                act.activation(cosine[:], clip[:], ACT.Sin, bias=half_pi[:],
                               scale=-float(np.pi) / CUTOFF).then_inc(cosine_ready, 1)

            @block.vector
            def _(dve):
                links = [0]

                def link(ins):
                    ins.then_inc(link_sem, 1)
                    links[0] += 1
                    dve.wait_ge(link_sem, links[0])

                dve.memset(half_pi[:], float(np.pi) / 2).then_inc(filled, 1)
                dve.memset(c["eps"][:], EPS)
                for table, fill in ((c["lo0"], MINIS), (c["lo1"], MINIS), (c["n0"], 1), (c["n1"], 1)):
                    link(dve.memset(table, fill))
                dve.wait_ge(loaded, 16)
                dst, src, kind = rec_in[:, :, 1], rec_in[:, :, 0], rec_in[:, :, 2]
                weight = rec_in[:, :, 3].bitcast(F32)
                minis = rec_in[0:REAL_PARTS, :, 1].rearrange("p (m e) -> p m e", e=MINI)
                dve.tensor_reduce(span[:, 0, :], minis, AX, ALU.max).then_inc(span_ready, 1)
                dve.tensor_reduce(span[:, 1, :], minis, AX, ALU.min).then_inc(span_ready, 1)
                link(dve.scalar_tensor_tensor(clip[:], weight, -1.0, weight, ALU.mult, ALU.max))
                dve.tensor_scalar(clip[:], clip[:], CUTOFF, None, ALU.min).then_inc(clipped, 1)
                dve.tensor_copy(rec_out[:, :, 0].bitcast(I32), src)
                dve.tensor_copy(rec_out[:, :, 1], dst)
                link(dve.scalar_tensor_tensor(key[:], kind, float(N), dst, ALU.mult, ALU.add))
                dve.tensor_copy(rec_out[:, :, 2], key[:])
                dve.wait_ge(cosine_ready, 1)
                link(dve.tensor_scalar(cosine[:], cosine[:], 0.5, 0.5, ALU.mult, ALU.add))
                dve.scalar_tensor_tensor(rec_out[:, :, 3], weight, CUTOFF, cosine[:],
                                         ALU.is_lt, ALU.mult).then_inc(rec_ready, 1)
                dve.wait_ge(consts_loaded, 64)
                link(dve.tensor_scalar(end[:], begin[:], float(SUB), None, ALU.add))
                dve.wait_ge(span_back, 16)
                for q in range(SUB_COLS):
                    link(dve.tensor_scalar(junk[:], span_all[:, 0, :], begin[:, q:q + 1], None, ALU.is_ge))
                    link(dve.scalar_tensor_tensor(inside[:], span_all[:, 1, :], end[:, q:q + 1], junk[:],
                                                  ALU.is_lt, ALU.mult))
                    for a in range(2):
                        ins = dve.tensor_tensor_reduce(junk[:], inside[:], ranks[:, a, :], 1.0, 0.0, ALU.mult,
                                                       ALU.max, edge_range[:, a, q:q + 1])
                        ins.then_inc(range_ready, 1)
                        dve.wait_ge(range_ready, 2 * q + a + 1)
                dve.wait_ge(row_back, 16)
                link(dve.tensor_scalar(lo_f[:], row[:, 0, :], -1.0, float(MINIS), ALU.mult, ALU.add))
                link(dve.tensor_tensor(len_f[:], row[:, 1, :], lo_f[:], ALU.subtract))
                dve.tensor_copy(c["lo1"][:, 0:SUBS], lo_f[:])
                dve.tensor_reduce(lo0_f[:], lo_f[:].rearrange("o (g j) -> o g j", j=PER_GROUP), AX, ALU.min)
                link(dve.tensor_reduce(hi0_f[:], row[:, 1, :].rearrange("o (g j) -> o g j", j=PER_GROUP), AX, ALU.max))
                dve.tensor_copy(c["lo0"][:, 0:GROUPS], lo0_f[:])
                link(dve.tensor_tensor(hi0_f[:], hi0_f[:], lo0_f[:], ALU.subtract))
                m0, m1 = CH0 // MINI, CH1 // MINI
                a0, a1 = c["n0"][:, 0:GROUPS], c["n1"][:, 0:SUBS]
                link(dve.tensor_scalar(a0, hi0_f[:], float(m0 - 1), None, ALU.add))
                link(dve.tensor_scalar(a0, a0, m0.bit_length() - 1, None, ALU.arith_shift_right))
                link(dve.tensor_scalar(a0, a0, 1.0, None, ALU.max))
                link(dve.tensor_scalar(a1, len_f[:], float(m1 - 1), 2731.0, ALU.add, ALU.mult))
                link(dve.tensor_scalar(a1, a1, 15, None, ALU.arith_shift_right))
                link(dve.tensor_scalar(a1, a1, 1.0, None, ALU.max))
                dve.tensor_reduce(total[:, 0:1], a0, AX, ALU.add)
                link(dve.tensor_reduce(total[:, 1:2], a1, AX, ALU.add))
                link(dve.tensor_scalar(total_i[:], total[:], float(U - 1), None, ALU.add))
                link(dve.tensor_scalar(total_i[:], total_i[:], U.bit_length() - 1, None, ALU.arith_shift_right))
                dve.tensor_scalar(c["steps0"][:], total_i[:, 0:1], float(-MIN_STEPS), None, ALU.add)
                dve.tensor_scalar(c["steps1"][:], total_i[:, 1:2], float(-MIN_STEPS), None, ALU.add)


def nodes_0(nc, c):
    sem, sems = c["sem"], c["sems"]
    w0 = c["w0"]
    UN = 4
    with ExitStack() as ctx:
        def sb(name, shape, dt=F32):
            return ctx.enter_context(nc.sbuf_tensor(name, shape, dt))

        def ps(name, shape):
            return ctx.enter_context(nc.psum_tensor(name, shape, F32))

        w_qkv = sb("w_qkv", [P, HALF, 3 * D])
        b_qkv = sb("b_qkv", [P, 3 * D])
        b_o = sb("b_o", [P, D])
        gamma_t, beta_t = sb("gamma_t", [P, HALF]), sb("beta_t", [P, HALF])
        xs = [sb(f"xs{k}", [GROUP, D]) for k in range(4)]
        hs = [sb(f"hs{k}", [GROUP, D]) for k in range(4)]
        xhs = [sb(f"xhs{k}", [GROUP, D]) for k in range(4)]
        xn = [sb(f"xn{k}", [GROUP, D]) for k in range(4)]
        xnT = [sb(f"xnT{k}", [P, HALF, GROUP]) for k in range(4)]
        q = [sb(f"q{k}", [GROUP, D]) for k in range(4)]
        q_rest = [sb(f"q_rest{k}", [GROUP, D]) for k in range(4)]
        q_parts = [sb(f"q_parts{k}", [P, Q_ROW], BF16) for k in range(4)]
        kv = [sb(f"kv0{k}", [GROUP, 2 * D]) for k in range(4)]
        stat = [[sb(f"stat{a}{k}", [GROUP, 6]) for k in range(4)] for a in range(2)]
        mv = [[sb(f"mv{a}{k}", [GROUP, 2]) for k in range(4)] for a in range(2)]
        std = [[sb(f"std{a}{k}", [GROUP, 1]) for k in range(4)] for a in range(2)]
        rstd = [[sb(f"rstd{a}{k}", [GROUP, 1]) for k in range(4)] for a in range(2)]
        shift = [[sb(f"shift{a}{k}", [GROUP, 1]) for k in range(4)] for a in range(2)]
        xnT_p = [ps(f"xnT_p{k}", [P, HALF, GROUP]) for k in range(2)]
        q_p = [ps(f"q_p{k}", [GROUP, D]) for k in range(2)]
        kv_p = [ps(f"kv_p{k}", [GROUP, 2 * D]) for k in range(2)]

        w_loaded = sem("w_qkv_loaded")
        x_loaded = sems("x_loaded", UN)
        stat_ready = [sem("stat_x"), sem("stat_h")]
        mean_ready = [sem("mean_x"), sem("mean_h")]
        std_ready = [sem("std_x"), sem("std_h")]
        rstd_ready = [sem("rstd_x"), sem("rstd_h")]
        shift_ready = [sem("shift_x"), sem("shift_h")]
        h_ready, xh_sum, xh_ready, xn_ready = sem("h_ready"), sem("xh_sum"), sem("xh_ready"), sem("xn_ready")
        xnT_turned, xnT_ready = sem("xnT_turned"), sem("xnT_ready")
        qkv_summed, qkv_ready = sem("qkv_summed"), sem("qkv_ready")
        q_filled, q_ready, q_split = sem("q_filled"), sem("q_ready"), sem("q_split")
        stored = sems("node0_stored", UN)
        held = sem("node0_held")

        with nc.Block() as block:
            @block.sync
            def _(sp):
                for dst, src in ((w_qkv[:], halves(w0["w_qkv"])), (b_qkv[:], w0["b_qkv"].to_broadcast([P, 3 * D])),
                                 (b_o[:], w0["b_o"].to_broadcast([P, D])),
                                 (gamma_t[:], w0["gamma_t"]), (beta_t[:], w0["beta_t"])):
                    sp.dma_start(dst, src).then_inc(w_loaded, 16)

                def load(it):
                    k = it.slot(4)
                    wait(sp, xh_sum, it, 4)
                    sp.dma_start(xs[k][:], c["x"][ds(it.index * GROUP, GROUP), :]).then_inc(x_loaded[k], 16)

                def store(it):
                    k = it.slot(4)
                    rows = ds(it.index * GROUP, GROUP)
                    wait(sp, qkv_ready, it)
                    wait(sp, xh_ready, it)
                    sp.dma_start(c["q0_d"][ds(it.index * P, P), :], q_parts[k][:]).then_inc(stored[k], 16)
                    sp.dma_start(c["kv0_d"][rows, :], kv[k][:]).then_inc(stored[k], 16)
                    sp.dma_start(c["xh_d"][rows, :], xhs[k][:]).then_inc(stored[k], 16)

                run_stages(sp, GROUPS, ((0, load), (7, store)), UN)
                for k in range(UN):
                    sp.wait_ge(stored[k], 48 * len(range(k, GROUPS, UN)))

            @block.gpsimd
            def _(pool):
                pool.wait_ge(w_loaded, 80)

                def residual(it):
                    k = it.slot(4)
                    wait(pool, h_ready, it)
                    if it.unroll and not (isinstance(it.i, int) and it.index < 4):
                        pool.wait_ge(stored[k], it.round(0) * 48)
                    pool.tensor_tensor(xhs[k][:], xs[k][:], hs[k][:], ALU.add).then_inc(xh_sum, 1)
                    wait(pool, xh_sum, it)
                    pool.tensor_tensor(xhs[k][:], xhs[k][:], b_o[0:GROUP, :], ALU.add).then_inc(xh_ready, 1)

                run_stages(pool, GROUPS, ((2, residual),), UN)

            @block.scalar
            def _(act):
                act.wait_ge(w_loaded, 80)

                def root(a):
                    def f(it):
                        k = it.slot(4)
                        wait(act, mean_ready[a], it)
                        wait(act, shift_ready[a], it, 4)
                        act.activation(std[a][k][:], mv[a][k][:, 1:2], ACT.Sqrt,
                                       bias=c["eps"][0:GROUP, :]).then_inc(std_ready[a], 1)
                    return f

                def relu(it):
                    k = it.slot(4)
                    wait(act, shift_ready[0], it)
                    wait(act, xn_ready, it, 4)
                    wait(act, xh_ready, it, 4)
                    act.activation(hs[k][:], xs[k][:], ACT.Relu, bias=shift[0][k][:],
                                   scale=rstd[0][k][:]).then_inc(h_ready, 1)

                def affine(it):
                    k = it.slot(4)
                    wait(act, xnT_turned, it)
                    wait(act, qkv_summed, it, 4)
                    for j in range(HALF):
                        act.activation(xnT[k][:, j, :], xnT_p[k % 2][:, j, :], ACT.Identity, bias=beta_t[:, j:j + 1],
                                       scale=gamma_t[:, j:j + 1]).then_inc(xnT_ready, 1)

                run_stages(act, GROUPS, ((0, root(0)), (1, relu), (2, root(1)), (4, affine)), UN)

            @block.vector
            def _(dve):
                def node_of(k):
                    return q_parts[k][:, PARTS * D:Q_ROW].bitcast(F32)

                for k in range(UN):
                    dve.memset(q_parts[k][:], 0.0).then_inc(q_filled, 1)
                dve.wait_ge(q_filled, UN)
                for k in range(UN):
                    dve.memset(node_of(k), float((k - UN) * GROUP)).then_inc(q_filled, 1)
                dve.wait_ge(q_filled, 2 * UN)
                dve.wait_ge(w_loaded, 80)

                def stats(a, src, lag):
                    def f(it):
                        k = it.slot(4)
                        if a == 0:
                            wait_slot(dve, x_loaded, it)
                        else:
                            wait(dve, h_ready, it)
                        dve.bn_stats(stat[a][k][:], src[k][:]).then_inc(stat_ready[a], 1)
                        dve.wait_ge(stat_ready[a], it.count())
                        wait(dve, shift_ready[a], it, 4)
                        dve.sem_inc(held, 1)
                        dve.bn_aggr(mv[a][k][:], stat[a][k][:]).then_inc(mean_ready[a], 1)
                    return f

                def scale(a):
                    def f(it):
                        k = it.slot(4)
                        wait(dve, std_ready[a], it)
                        wait(dve, h_ready if a == 0 else xn_ready, it, 4)
                        dve.reciprocal(rstd[a][k][:], std[a][k][:]).then_inc(rstd_ready[a], 1)
                        wait(dve, rstd_ready[a], it)
                        dve.scalar_tensor_tensor(shift[a][k][:], mv[a][k][:, 0:1], -1.0, rstd[a][k][:],
                                                 ALU.mult, ALU.mult).then_inc(shift_ready[a], 1)
                        if a == 1:
                            wait(dve, shift_ready[1], it)
                            wait(dve, xnT_turned, it, 4)
                            dve.tensor_scalar(xn[k][:], hs[k][:], rstd[1][k][:], shift[1][k][:],
                                              ALU.mult, ALU.add).then_inc(xn_ready, 1)
                    return f

                def bias(it):
                    k = it.slot(4)
                    wait(dve, qkv_summed, it)
                    if not (isinstance(it.i, int) and it.index < 4):
                        dve.wait_ge(stored[k], it.round(0) * 48)
                    dve.tensor_tensor(q[k][:], q_p[k % 2][:], b_qkv[0:GROUP, 0:D], ALU.add).then_inc(q_ready, 1)
                    dve.tensor_tensor(kv[k][:], kv_p[k % 2][:], b_qkv[0:GROUP, D:3 * D], ALU.add)
                    wait(dve, q_ready, it)
                    dve.tensor_scalar(node_of(k), node_of(k), float(UN * GROUP), None, ALU.add)
                    src = q[k]
                    for j in range(PARTS - 1):
                        part = q_parts[k][0:GROUP, j * D:(j + 1) * D]
                        dve.tensor_copy(part, src[:]).then_inc(q_split, 1)
                        dve.wait_ge(q_split, it.count(1, PARTS, 2 * j + 1))
                        last = j == PARTS - 2
                        left = q_parts[k][0:GROUP, (j + 1) * D:(j + 2) * D] if last else q_rest[k][:]
                        ins = dve.tensor_tensor(left, src[:], part, ALU.subtract)
                        if not last:
                            ins.then_inc(q_split, 1)
                            dve.wait_ge(q_split, it.count(1, PARTS, 2 * j + 2))
                        src = q_rest[k]
                    ins.then_inc(qkv_ready, 1)

                run_stages(dve, GROUPS, ((0, stats(0, xs, 0)), (1, scale(0)), (2, stats(1, hs, 2)), (3, scale(1)),
                                         (6, bias)), UN)

            @block.tensor
            def _(pe):
                pe.wait_ge(w_loaded, 80)

                def turn(it):
                    k = it.slot(4)
                    wait(pe, xn_ready, it)
                    wait(pe, xnT_ready, it, 2, per=HALF)
                    for j in range(HALF):
                        ins = pe.transpose(xnT_p[k % 2][:, j, :], xn[k][:, j * P:(j + 1) * P],
                                           c["ident"][0:GROUP, 0:GROUP])
                    ins.then_inc(xnT_turned, 1)

                def project(it):
                    k = it.slot(4)
                    wait(pe, xnT_ready, it, per=HALF)
                    wait(pe, qkv_ready, it, 2)
                    for j in range(HALF):
                        pe.matmul(q_p[k % 2][:], xnT[k][:, j, :], w_qkv[:, j, 0:D], start=j == 0, stop=j == HALF - 1)
                    for j in range(HALF):
                        ins = pe.matmul(kv_p[k % 2][:], xnT[k][:, j, :], w_qkv[:, j, D:3 * D],
                                        start=j == 0, stop=j == HALF - 1)
                    ins.then_inc(qkv_summed, 1)

                run_stages(pe, GROUPS, ((4, turn), (5, project)), UN)


def edges_0(nc, c):
    sem, sems = c["sem"], c["sems"]
    w0 = c["w0"]
    with ExitStack() as ctx:
        def sb(name, shape, dt=F32):
            return ctx.enter_context(nc.sbuf_tensor(name, shape, dt))

        def ps(name, shape):
            return ctx.enter_context(nc.psum_tensor(name, shape, F32))

        LAST = 96
        w_raw = sb("w_edge_raw", [LAST + 1, 2 * D])
        w_lead = sb("w_edge_lead", [P, 2 * D], F32R)
        w_rest = sb("w_edge_rest", [LAST + 1, 2 * D], F32R)
        b_lead = sb("b_edge_lead", [LAST + 1, 2 * D], F32R)
        rec = [sb(f"rec{k}", [P, T0, 4]) for k in range(U)]
        feat = [sb(f"feat{k}", [R, CH0]) for k in range(U)]
        parts = [sb(f"parts{k}", [P, CH0], F32R) for k in range(2)]
        lead = [sb(f"feat_lead{k}", [LAST + 1, CH0], F32R) for k in range(2)]
        ones = sb("edge_ones", [LAST + 1 - R, CH0])
        q_blk = [sb(f"q_blk{k}", [P, Q_ROW], BF16) for k in range(U)]
        keep = [sb(f"keep{k}", [GROUP, 1]) for k in range(U)]
        kv = [sb(f"kv{k}", [P, T0, 2 * D]) for k in range(U)]
        local = [sb(f"local{k}", [P, T0]) for k in range(2)]
        hot = [sb(f"hot{k}", [P, T0, GROUP]) for k in range(4)]
        hotT = [sb(f"hotT{k}", [GROUP, T0, P], BF16) for k in range(2)]
        gates = [sb(f"gates{k}", [P, T0, 2 * D]) for k in range(2)]
        qk = [sb(f"qk{k}", [P, T0, D]) for k in range(2)]
        attn = [sb(f"attn{k}", [P, T0]) for k in range(2)]
        attn_act = [sb(f"attn_act{k}", [P, T0]) for k in range(2)]
        weight = [sb(f"weight{k}", [P, T0]) for k in range(2)]
        msg = [sb(f"msg{k}", [P, T0, D]) for k in range(2)]
        total = [sb(f"total{k}", [GROUP, D]) for k in range(U)]
        gates_p = [ps(f"gates_p{t}", [P, 2 * D]) for t in range(T0)]
        qe_p = ps("qe_p", [P, T0, D])
        hotT_p = ps("hotT_p", [GROUP, T0, P])
        sum_p = ps("sum_p", [GROUP, 2, D])

        w_loaded, filled = sem("w_edge_loaded"), sem("edge0_filled")
        w_lead_ready, w_ready = sem("w_lead_ready"), sem("w_edge_ready")
        lead_ready, parts_ready = sem("feat_lead_ready"), sem("feat_parts_ready")
        loaded, gathered = sems("edge0_loaded", U), sems("kv0_gathered", U)
        local_ready, hot_ready = sem("local_ready"), sem("hot_ready")
        hotT_turned, hotT_ready = sem("hotT_turned"), sem("hotT_ready")
        gates_summed, gates_ready = sem("gates_summed"), sem("gates_ready")
        qe_ready, qk_ready, attn_ready = sem("qe_ready"), sem("qk_ready"), sem("attn_ready")
        attn_act_ready, weight_ready = sem("attn_act_ready"), sem("weight_ready")
        msg_ready, msg_summed, total_ready = sem("msg_ready"), sem("msg_summed"), sem("total_ready")
        stored, held = sem("total_stored"), sem("edge0_held")
        LOADS = 3

        def first_of(s):
            return q_blk[s][:, PARTS * D:Q_ROW].bitcast(F32)

        with nc.Block() as block:
            @block.sync
            def _(sp):
                sp.wait_ge(filled, 1)
                sp.dma_start(w_raw[0:R, :], w0["w_edge"]).then_inc(w_loaded, 16)
                for row in (R, LAST):
                    sp.dma_start(w_raw[row:row + 1, :], w0["b_edge"]).then_inc(w_loaded, 16)
                steps = chunk_steps(sp, c["steps0"])
                blk, k_in, first, n, at, row, done = (
                    sp.alloc_register(name) for name in ("blk", "k_in", "first", "n", "at", "row", "done"))
                used = [sp.alloc_register(f"used{k}") for k in range(U)]
                sp.reg_mov(blk, 0)
                sp.reg_mov(k_in, 0)

                def load(it):
                    k = it.slot(U)
                    b = sp.snap(blk, min_val=0, max_val=GROUPS)
                    sp.reg_load((first, n), c["runs0"][0:1, ds(b, 1), :])
                    sp.reg_mul(at, k_in, CH0 // MINI)
                    sp.reg_add(at, at, first)
                    sp.reg_mul(at, at, MINI)
                    edge = sp.snap(at, min_val=0, max_val=EP - CH0)
                    sp.reg_alu(row, blk, GROUPS - 1, ALU.min)
                    node = sp.snap(row, min_val=0, max_val=GROUPS - 1)
                    wait(sp, total_ready, it, U - 1)
                    sp.sem_inc(held, 1)
                    sp.dma_start(rec[k][:], c["rec_d"][ds(edge, CH0), :].rearrange("(p t) f -> p t f", t=T0)
                                 ).then_inc(loaded[k], 16)
                    sp.dma_start(feat[k][:], c["edge_feat_t"][:, ds(edge, CH0)]).then_inc(loaded[k], 16)
                    sp.dma_start(q_blk[k][:], c["q0_d"][ds(node * P, P), :]).then_inc(loaded[k], 16)
                    sp.reg_mov(used[k], blk)
                    sp.reg_add(k_in, k_in, 1)
                    sp.reg_alu(done, k_in, n, ALU.is_ge)
                    sp.reg_add(blk, blk, done)
                    sp.reg_alu(blk, blk, GROUPS, ALU.min)
                    sp.reg_alu(done, 1, done, ALU.subtract)
                    sp.reg_mul(k_in, k_in, done)

                def store(it):
                    k = it.slot(U)
                    b = sp.snap(used[k], min_val=0, max_val=GROUPS)
                    wait(sp, total_ready, it)
                    sp.sem_inc(held, 1)
                    wait(sp, stored, it, 1, per=16)
                    sp.sem_inc(held, 1)
                    sp.dma_start(c["agg_d"][ds(b * GROUP, GROUP), :], total[k][:]).then_inc(stored, 16)

                run_chunks(sp, steps, ((0, load), (5, store)))
                sp.wait_ge(stored, Item(steps, -1, U).count(per=16))
                sp.sem_inc(held, 1)

            @block.gpsimd
            def _(pool):
                steps = chunk_steps(pool, c["steps0"])

                def gather(it):
                    k = it.slot(U)
                    wait_slot(pool, loaded, it, LOADS)
                    pool.sem_inc(held, 1)
                    wait(pool, msg_ready, it, U)
                    pool.sem_inc(held, 1)
                    for t in range(T0):
                        pool.indirect_dma_start(
                            kv[k][:, t, :], None, c["kv0_d"],
                            bass.IndirectOffsetOnAxis(ap=rec[k][:, t, 0:1].bitcast(I32), axis=0)
                        ).then_inc(gathered[k], 16)

                def split_rest(it):
                    k, s = it.slot(2), it.slot(U)
                    wait(pool, lead_ready, it, per=2)
                    pool.sem_inc(held, 1)
                    wait(pool, gates_summed, it, 2, per=T0)
                    pool.sem_inc(held, 1)
                    pool.tensor_tensor(parts[k][R:P, :], feat[s][:], parts[k][0:R, :],
                                       ALU.subtract).then_inc(parts_ready, 1)

                run_chunks(pool, steps, ((1, split_rest), (0, gather)))

            @block.scalar
            def _(act):
                steps = chunk_steps(act, c["steps0"])

                def split_lead(it):
                    k, s = it.slot(2), it.slot(U)
                    wait_slot(act, loaded, it, LOADS)
                    wait(act, gates_summed, it, 2, per=T0)
                    act.copy(parts[k][0:R, :], feat[s][:]).then_inc(lead_ready, 1)
                    act.copy(lead[k][0:R, :], feat[s][:]).then_inc(lead_ready, 1)

                def hot_out(it):
                    k = it.slot(2)
                    wait(act, hotT_turned, it)
                    wait(act, qe_ready, it, 2)
                    act.copy(hotT[k][:], hotT_p[:]).then_inc(hotT_ready, 1)

                def attn_silu(it):
                    k = it.slot(2)
                    wait(act, attn_ready, it)
                    wait(act, weight_ready, it, 2)
                    act.activation(attn_act[k][:], attn[k][:], ACT.Silu).then_inc(attn_act_ready, 1)

                def gates_silu(it):
                    k = it.slot(2)
                    wait(act, msg_ready, it, 2)
                    for t in range(T0):
                        act.wait_ge(gates_summed, it.count(1, T0, t + 1))
                        act.activation(gates[k][:, t, :], gates_p[t][:], ACT.Silu).then_inc(gates_ready, 1)

                run_chunks(act, steps, ((1, hot_out), (0, split_lead), (2, attn_silu), (1, gates_silu)))

            @block.vector
            def _(dve):
                dve.memset(w_raw[R:LAST + 1, :], 0.0).then_inc(filled, 1)
                dve.memset(ones[:], 1.0).then_inc(filled, 1)
                for k in range(U):
                    dve.memset(total[k][:], 0.0).then_inc(filled, 1)
                dve.wait_ge(filled, U + 2)
                for k in range(2):
                    dve.tensor_copy(lead[k][R:LAST + 1, :], ones[:])
                dve.wait_ge(w_loaded, 48)
                dve.tensor_copy(w_lead[0:R, :], w_raw[0:R, :])
                dve.tensor_copy(w_lead[R:P, :], w_raw[0:R, :])
                dve.tensor_copy(b_lead[R:LAST + 1, :], w_raw[R:LAST + 1, :]).then_inc(w_lead_ready, 1)
                dve.wait_ge(w_lead_ready, 1)
                dve.tensor_tensor(w_rest[0:R, :], w_raw[0:R, :], w_lead[0:R, :], ALU.subtract)
                dve.tensor_copy(w_rest[R:LAST, :], b_lead[R:LAST, :])
                dve.tensor_tensor(w_rest[LAST:LAST + 1, :], w_raw[LAST:LAST + 1, :], b_lead[LAST:LAST + 1, :],
                                  ALU.subtract).then_inc(w_ready, 1)
                steps = chunk_steps(dve, c["steps0"])

                def locate(it):
                    k, s = it.slot(2), it.slot(U)
                    wait_slot(dve, loaded, it, LOADS)
                    wait(dve, total_ready, it, U)
                    last = s if isinstance(it.i, int) and it.index == 0 else it.prev().slot(U)
                    dve.tensor_scalar(keep[s][:], first_of(s)[0:GROUP], first_of(last)[0:GROUP], None, ALU.is_equal)
                    wait(dve, hot_ready, it, 2)
                    dve.tensor_scalar(local[k][:], rec[s][:, :, 1], first_of(s), None,
                                      ALU.subtract).then_inc(local_ready, 1)

                def one_hot(it):
                    wait(dve, local_ready, it)
                    wait(dve, msg_summed, it, 4)
                    dve.tensor_tensor(hot[it.slot(4)][:],
                                      c["iota"][:].rearrange("p (o n) -> p o n", o=1).to_broadcast([P, T0, GROUP]),
                                      local[it.slot(2)][:].rearrange("p (t o) -> p t o", o=1).to_broadcast(
                                          [P, T0, GROUP]), ALU.is_equal).then_inc(hot_ready, 1)

                def q_times_k(it):
                    k, s = it.slot(2), it.slot(U)
                    wait(dve, qe_ready, it)
                    wait_slot(dve, gathered, it, T0)
                    dve.tensor_tensor(qk[k][:], qe_p[:], kv[s][:, :, 0:D], ALU.mult).then_inc(qk_ready, 1)

                def scores(it):
                    k = it.slot(2)
                    wait(dve, gates_ready, it, per=T0)
                    dve.sem_inc(held, 1)
                    wait(dve, qk_ready, it)
                    dve.sem_inc(held, 1)
                    for t in range(T0):
                        ins = dve.tensor_tensor_reduce(qk[k][:, t, :], qk[k][:, t, :], gates[k][:, t, 0:D], 1.0, 0.0,
                                                       ALU.mult, ALU.add, attn[k][:, t:t + 1])
                    ins.then_inc(attn_ready, 1)

                def add_total(it):
                    k, s = it.slot(2), it.slot(U)
                    wait(dve, msg_summed, it)
                    wait(dve, stored, it, U, per=16)
                    wait(dve, total_ready, it, 1)
                    dve.scalar_tensor_tensor(total[s][:], total[it.prev().slot(U)][:], keep[s][:],
                                             sum_p[:, k, :], ALU.mult, ALU.add).then_inc(total_ready, 1)

                def weights(it):
                    k, s = it.slot(2), it.slot(U)
                    wait(dve, attn_act_ready, it)
                    dve.tensor_tensor(weight[k][:], attn_act[k][:], rec[s][:, :, 3], ALU.mult).then_inc(weight_ready, 1)

                def messages(it):
                    k, s = it.slot(2), it.slot(U)
                    wait(dve, weight_ready, it)
                    wait(dve, msg_summed, it, 2)
                    for t in range(T0):
                        ins = dve.scalar_tensor_tensor(msg[k][:, t, :], kv[s][:, t, D:2 * D], weight[k][:, t:t + 1],
                                                       gates[k][:, t, D:2 * D], ALU.mult, ALU.mult)
                    ins.then_inc(msg_ready, 1)

                run_chunks(dve, steps, ((2, q_times_k), (0, locate), (2, scores), (0, one_hot), (2, weights),
                                        (3, add_total), (2, messages)))

            @block.tensor
            def _(pe):
                pe.wait_ge(w_ready, 1)
                steps = chunk_steps(pe, c["steps0"])

                def turn(it):
                    wait(pe, hot_ready, it)
                    wait(pe, hotT_ready, it, 1)
                    for t in range(T0):
                        ins = pe.transpose(hotT_p[:, t, :], hot[it.slot(4)][:, t, :], c["ident"][:])
                    ins.then_inc(hotT_turned, 1)

                def edge_gates(it):
                    k = it.slot(2)
                    wait(pe, parts_ready, it)
                    for t in range(T0):
                        if not (isinstance(it.i, int) and it.index == 0):
                            pe.wait_ge(gates_ready, it.count(2, T0, t + 1))
                        pe.matmul(gates_p[t][:], parts[k][:, t::T0], w_lead[:], start=True, stop=False)
                        pe.matmul(gates_p[t][:], lead[k][:, t::T0], w_rest[:], start=False,
                                  stop=True).then_inc(gates_summed, 1)

                def q_of_edges(it):
                    k, s = it.slot(2), it.slot(U)
                    wait(pe, hotT_ready, it)
                    wait(pe, qk_ready, it, 1)
                    for t in range(T0):
                        for j in range(PARTS):
                            ins = pe.matmul(qe_p[:, t, :], hotT[k][:, t, :], q_blk[s][0:GROUP, j * D:(j + 1) * D],
                                            start=j == 0, stop=j == PARTS - 1)
                    ins.then_inc(qe_ready, 1)

                def sum_messages(it):
                    k = it.slot(2)
                    wait(pe, msg_ready, it)
                    wait(pe, total_ready, it, 1)
                    for t in range(T0):
                        ins = pe.matmul(sum_p[:, k, :], hot[it.slot(4)][:, t, :], msg[k][:, t, :],
                                        start=t == 0, stop=t == T0 - 1)
                    ins.then_inc(msg_summed, 1)

                run_chunks(pe, steps, ((3, sum_messages), (1, q_of_edges), (1, edge_gates), (0, turn)))


def nodes_1(nc, c):
    sem, sems = c["sem"], c["sems"]
    w0 = c["w0"]
    UN = 4
    with ExitStack() as ctx:
        def sb(name, shape, dt=F32):
            return ctx.enter_context(nc.sbuf_tensor(name, shape, dt))

        def ps(name, shape):
            return ctx.enter_context(nc.psum_tensor(name, shape, F32))

        w_o = sb("w_o", [P, HALF, D])
        w_kv = sb("w_kv", [P, TYPES * HALF, 2 * D])
        w_q = sb("w_q", [P, TYPES * HALF, D])
        b_q = sb("b_q", [TYPES, D])
        a_rel = sb("a_rel", [P, RELS, HALF, P])
        prior = sb("prior", [P, RELS, HALF])
        part = sb("part", [P, 1])
        agg = [sb(f"agg{k}", [GROUP, D]) for k in range(4)]
        xh = [sb(f"xh1{k}", [GROUP, D]) for k in range(4)]
        kind_row = [sb(f"kind_row{k}", [P, GROUP], I32) for k in range(4)]
        kind_col = [sb(f"kind_col{k}", [GROUP, 1], I32) for k in range(4)]
        b_kv = [sb(f"b_kv{k}", [GROUP, 2 * D]) for k in range(4)]
        of_kind = [sb(f"of_kind{k}", [P, TYPES, GROUP]) for k in range(4)]
        kind_hot = [sb(f"kind_hot{k}", [TYPES, GROUP]) for k in range(4)]
        aggT = [sb(f"aggT{k}", [P, HALF, GROUP]) for k in range(2)]
        x1 = [sb(f"x1{k}", [GROUP, D]) for k in range(4)]
        h1 = [sb(f"h1{k}", [GROUP, D]) for k in range(4)]
        stat = [sb(f"stat_h1_{k}", [GROUP, 6]) for k in range(4)]
        mv = [sb(f"mv_h1_{k}", [GROUP, 2]) for k in range(4)]
        std = [sb(f"std_h1_{k}", [GROUP, 1]) for k in range(4)]
        rstd = [sb(f"rstd_h1_{k}", [GROUP, 1]) for k in range(4)]
        shift = [sb(f"shift_h1_{k}", [GROUP, 1]) for k in range(4)]
        hT = [sb(f"hT{k}", [P, TYPES, HALF, GROUP]) for k in range(2)]
        kv = [sb(f"kv1{k}", [GROUP, 2 * D]) for k in range(4)]
        qT = [sb(f"qT{k}", [P, HALF, GROUP]) for k in range(2)]
        qrel = [sb(f"qrel{k}", [P, PER_GROUP, HALF, RELS, SUB]) for k in range(2)]
        aggT_p, out_p, hT_p = ps("aggT_p", [P, HALF, GROUP]), ps("out_p", [GROUP, D]), ps("hT_p", [P, HALF, GROUP])
        kv_p, qT_p = ps("kv1_p", [GROUP, 2 * D]), ps("qT_p", [P, HALF, GROUP])
        WIDE = 4
        qrel_p = [ps(f"qrel_p{k}", [P, WIDE, GROUP]) for k in range(HALF)]
        qrel_p45 = ps("qrel_p45", [P, HALF, RELS - WIDE, GROUP])

        w_loaded, scaled = sem("w1_loaded"), sem("a_rel_scaled")
        loaded, bias_got = sems("node1_loaded", UN), sems("b_kv_gathered", UN)
        kinds_ready = sem("kinds_ready")
        aggT_turned, aggT_ready, out_summed = sem("aggT_turned"), sem("aggT_ready"), sem("out_summed")
        x1_ready, stat_ready, mean_ready, std_ready = sem("x1_ready"), sem("stat1"), sem("mean1"), sem("std1")
        rstd_ready, shift_ready, h1_ready = sem("rstd1"), sem("shift1"), sem("h1_ready")
        hT_turned, hT_ready = sem("hT_turned"), sem("hT_ready")
        kv_summed, kv_ready, qT_summed, qT_ready = sem("kv1_summed"), sem("kv1_ready"), sem("qT_summed"), sem("qT_ready")
        qrel_summed, qrel_act, qrel_dve = sem("qrel_summed"), sem("qrel_act"), sem("qrel_dve")
        x_stored, kv_stored, qrel_stored = sems("x1_stored", UN), sems("kv1_stored", UN), sems("qrel_stored", 2)
        held = sem("node1_held")
        LOADS, WEIGHTS = 4, 7

        with nc.Block() as block:
            @block.sync
            def _(sp):
                for dst, src in ((w_o[:], halves(w0["w_o"])),
                                 (w_kv[:], w0["w_kv1"].rearrange("(a p) n -> p a n", p=P)),
                                 (w_q[:], w0["w_q1"].rearrange("(a p) n -> p a n", p=P)), (b_q[:], w0["b_q1"]),
                                 (a_rel[:], w0["a_rel"]), (prior[:], w0["prior"]), (part[:], w0["part"])):
                    sp.dma_start(dst, src).then_inc(w_loaded, 16)

                def load(it):
                    k = it.slot(4)
                    rows = ds(it.index * GROUP, GROUP)
                    wait(sp, x1_ready, it, 4)
                    sp.sem_inc(held, 1)
                    wait(sp, kinds_ready, it, 4)
                    sp.sem_inc(held, 1)
                    if not (isinstance(it.i, int) and it.index < UN):
                        sp.wait_ge(bias_got[k], it.round(0) * 16)
                    sp.dma_start(agg[k][:], c["agg_d"][rows, :]).then_inc(loaded[k], 16)
                    sp.dma_start(xh[k][:], c["xh_d"][rows, :]).then_inc(loaded[k], 16)
                    sp.dma_start(kind_row[k][:], c["node_type"][:, rows].to_broadcast([P, GROUP])
                                 ).then_inc(loaded[k], 16)
                    sp.dma_start(kind_col[k][:], c["node_type"].rearrange("o n -> n o")[rows, :]
                                 ).then_inc(loaded[k], 16)

                def store_x(it):
                    k = it.slot(4)
                    rows = ds(it.index * GROUP, GROUP)
                    wait(sp, h1_ready, it)
                    sp.dma_start(c["x1_d"][rows, :], x1[k][:]).then_inc(x_stored[k], 16)
                    sp.dma_start(c["h1_d"][rows, :], h1[k][:]).then_inc(x_stored[k], 16)

                def store_kv(it):
                    k = it.slot(4)
                    wait(sp, kv_ready, it)
                    sp.dma_start(c["kv1_d"][ds(it.index * GROUP, GROUP), :], kv[k][:]).then_inc(kv_stored[k], 16)

                def store_qrel(it):
                    k = it.slot(2)
                    wait(sp, qrel_act, it)
                    sp.sem_inc(held, 1)
                    wait(sp, qrel_dve, it)
                    sp.dma_start(c["qrel_d"][ds(it.index * PER_GROUP, PER_GROUP)].rearrange("j p f -> p j f"),
                                 qrel[k][:].rearrange("p j a r n -> p j (a r n)")).then_inc(qrel_stored[k], 16)

                run_stages(sp, GROUPS, ((0, load), (5, store_x), (6, store_kv), (8, store_qrel)), UN)
                for k in range(UN):
                    sp.wait_ge(x_stored[k], 32 * len(range(k, GROUPS, UN)))
                    sp.wait_ge(kv_stored[k], 16 * len(range(k, GROUPS, UN)))
                for k in range(2):
                    sp.wait_ge(qrel_stored[k], 16 * len(range(k, GROUPS, 2)))

            @block.gpsimd
            def _(pool):
                def gather(it):
                    k = it.slot(4)
                    wait_slot(pool, loaded, it, LOADS)
                    pool.sem_inc(held, 1)
                    wait(pool, kv_ready, it, 4)
                    pool.sem_inc(held, 1)
                    pool.indirect_dma_start(b_kv[k][:], None, w0["b_kv1"],
                                            bass.IndirectOffsetOnAxis(ap=kind_col[k][:], axis=0)
                                            ).then_inc(bias_got[k], 16)

                run_stages(pool, GROUPS, ((1, gather),), UN)

            @block.scalar
            def _(act):
                def agg_out(it):
                    k = it.slot(2)
                    wait(act, aggT_turned, it)
                    wait(act, out_summed, it, 2)
                    act.copy(aggT[k][:], aggT_p[:]).then_inc(aggT_ready, 1)

                def root(it):
                    k = it.slot(4)
                    wait(act, mean_ready, it)
                    wait(act, shift_ready, it, 4)
                    act.activation(std[k][:], mv[k][:, 1:2], ACT.Sqrt, bias=c["eps"][0:GROUP, :]).then_inc(std_ready, 1)

                def relu(it):
                    k = it.slot(4)
                    wait(act, shift_ready, it)
                    if not (isinstance(it.i, int) and it.index < UN):
                        act.wait_ge(x_stored[k], it.round(0) * 32)
                    wait(act, hT_turned, it, 4)
                    act.activation(h1[k][:], x1[k][:], ACT.Relu, bias=shift[k][:], scale=rstd[k][:]).then_inc(h1_ready, 1)

                def q_out(it):
                    k = it.slot(2)
                    wait(act, qT_summed, it)
                    wait(act, qrel_summed, it, 2)
                    act.copy(qT[k][:], qT_p[:]).then_inc(qT_ready, 1)

                def qrel_out(it):
                    k = it.slot(2)
                    wait(act, qrel_summed, it)
                    if not (isinstance(it.i, int) and it.index < 2):
                        wait_pair(act, qrel_stored, it)
                    for a in range(HALF):
                        ins = act.copy(qrel[k][:, :, a, 0:WIDE, :].rearrange("p j r n -> p r j n"),
                                       qrel_p[a][:].rearrange("p r (j n) -> p r j n", n=SUB))
                    ins.then_inc(qrel_act, 1)

                run_stages(act, GROUPS, ((1, agg_out), (2, root), (3, relu), (5, q_out), (6, qrel_out)), UN)

            @block.vector
            def _(dve):
                dve.wait_ge(w_loaded, 16 * WEIGHTS)
                for r in range(RELS):
                    for a in range(HALF):
                        dve.tensor_scalar(a_rel[:, r, a, :], a_rel[:, r, a, :], prior[:, r, a:a + 1], DK ** -0.5,
                                          ALU.mult, ALU.mult).then_inc(scaled, 1)

                def kinds(it):
                    k = it.slot(4)
                    wait_slot(dve, loaded, it, LOADS)
                    wait(dve, qT_summed, it, 4)
                    for t in range(TYPES):
                        dve.tensor_scalar(of_kind[k][:, t, :], kind_row[k][:], float(t), None, ALU.is_equal)
                    dve.tensor_scalar(kind_hot[k][:], kind_row[k][0:TYPES, :], part[0:TYPES, :], None,
                                      ALU.is_equal).then_inc(kinds_ready, 1)

                def residual(it):
                    k = it.slot(4)
                    wait(dve, out_summed, it)
                    if not (isinstance(it.i, int) and it.index < UN):
                        dve.wait_ge(x_stored[k], it.round(0) * 32)
                    dve.tensor_tensor(x1[k][:], out_p[:], xh[k][:], ALU.add).then_inc(x1_ready, 1)
                    wait(dve, x1_ready, it)
                    dve.bn_stats(stat[k][:], x1[k][:]).then_inc(stat_ready, 1)
                    wait(dve, stat_ready, it)
                    dve.sem_inc(held, 1)
                    wait(dve, shift_ready, it, 4)
                    dve.sem_inc(held, 1)
                    dve.bn_aggr(mv[k][:], stat[k][:]).then_inc(mean_ready, 1)

                def scale(it):
                    k = it.slot(4)
                    wait(dve, std_ready, it)
                    wait(dve, h1_ready, it, 4)
                    dve.reciprocal(rstd[k][:], std[k][:]).then_inc(rstd_ready, 1)
                    wait(dve, rstd_ready, it)
                    dve.scalar_tensor_tensor(shift[k][:], mv[k][:, 0:1], -1.0, rstd[k][:],
                                             ALU.mult, ALU.mult).then_inc(shift_ready, 1)

                def split_kinds(it):
                    k = it.slot(2)
                    wait(dve, hT_turned, it)
                    wait(dve, kinds_ready, it)
                    wait(dve, qT_summed, it, 2)
                    for t in range(TYPES):
                        ins = dve.tensor_tensor(hT[k][:, t], hT_p[:], of_kind[it.slot(4)][:, t:t + 1, :].to_broadcast(
                            [P, HALF, GROUP]), ALU.mult)
                    ins.then_inc(hT_ready, 1)

                def kv_out(it):
                    k = it.slot(4)
                    wait(dve, kv_summed, it)
                    wait_slot(dve, bias_got, it)
                    if not (isinstance(it.i, int) and it.index < UN):
                        dve.wait_ge(kv_stored[k], it.round(0) * 16)
                    dve.tensor_tensor(kv[k][:], kv_p[:], b_kv[k][:], ALU.add).then_inc(kv_ready, 1)

                def qrel_out(it):
                    k = it.slot(2)
                    wait(dve, qrel_summed, it)
                    if not (isinstance(it.i, int) and it.index < 2):
                        wait_pair(dve, qrel_stored, it)
                    for a in range(HALF):
                        ins = dve.tensor_copy(qrel[k][:, :, a, WIDE:RELS, :].rearrange("p j r n -> p r j n"),
                                              qrel_p45[:, a].rearrange("p r (j n) -> p r j n", n=SUB))
                    ins.then_inc(qrel_dve, 1)

                run_stages(dve, GROUPS, ((1, kinds), (2, residual), (3, scale), (4, split_kinds), (5, kv_out),
                                         (6, qrel_out)), UN)

            @block.tensor
            def _(pe):
                pe.wait_ge(w_loaded, 16 * WEIGHTS)
                pe.wait_ge(scaled, RELS * HALF)

                def turn_agg(it):
                    k = it.slot(4)
                    wait_slot(pe, loaded, it, LOADS)
                    wait(pe, aggT_ready, it, 1)
                    for j in range(HALF):
                        ins = pe.transpose(aggT_p[:, j, :], agg[k][:, j * P:(j + 1) * P], c["ident"][0:GROUP, 0:GROUP])
                    ins.then_inc(aggT_turned, 1)

                def out_project(it):
                    k = it.slot(2)
                    wait(pe, aggT_ready, it)
                    wait(pe, x1_ready, it, 1)
                    for j in range(HALF):
                        ins = pe.matmul(out_p[:], aggT[k][:, j, :], w_o[:, j, :], start=j == 0, stop=j == HALF - 1)
                    ins.then_inc(out_summed, 1)

                def turn_h(it):
                    k = it.slot(4)
                    wait(pe, h1_ready, it)
                    wait(pe, hT_ready, it, 1)
                    for j in range(HALF):
                        ins = pe.transpose(hT_p[:, j, :], h1[k][:, j * P:(j + 1) * P], c["ident"][0:GROUP, 0:GROUP])
                    ins.then_inc(hT_turned, 1)

                def project(it):
                    k = it.slot(2)
                    wait(pe, hT_ready, it)
                    wait(pe, kv_ready, it, 1)
                    for a in range(TYPES * HALF):
                        ins = pe.matmul(kv_p[:], hT[k][:, a // HALF, a % HALF, :], w_kv[:, a, :],
                                        start=a == 0, stop=a == TYPES * HALF - 1)
                    ins.then_inc(kv_summed, 1)
                    wait(pe, qT_ready, it, 1)
                    for j in range(HALF):
                        cols = slice(j * P, (j + 1) * P)
                        for a in range(TYPES * HALF):
                            pe.matmul(qT_p[:, j, :], w_q[:, a, cols], hT[k][:, a // HALF, a % HALF, :],
                                      start=a == 0, stop=False)
                        ins = pe.matmul(qT_p[:, j, :], b_q[:, cols], kind_hot[it.slot(4)][:], start=False, stop=True)
                    ins.then_inc(qT_summed, 1)

                def relate(it):
                    k = it.slot(2)
                    wait(pe, qT_ready, it)
                    wait(pe, qrel_act, it, 1)
                    wait(pe, qrel_dve, it, 1)
                    for a in range(HALF):
                        for r in range(RELS):
                            dst = qrel_p[a][:, r, :] if r < WIDE else qrel_p45[:, a, r - WIDE, :]
                            ins = pe.matmul(dst, a_rel[:, r, a, :], qT[k][:, a, :], start=True, stop=True)
                    ins.then_inc(qrel_summed, 1)

                run_stages(pe, GROUPS, ((1, turn_agg), (2, out_project), (4, turn_h), (5, project), (6, relate)), UN)


def edges_1(nc, c):
    sem, sems = c["sem"], c["sems"]
    w0 = c["w0"]
    with ExitStack() as ctx:
        def sb(name, shape, dt=F32):
            return ctx.enter_context(nc.sbuf_tensor(name, shape, dt))

        def ps(name, shape):
            return ctx.enter_context(nc.psum_tensor(name, shape, F32))

        rec = [sb(f"rec1{k}", [P, T1, 4]) for k in range(U)]
        key = [sb(f"key{k}", [SEG, CH1]) for k in range(U)]
        qrel = [sb(f"qrel1{k}", [P, HEADS, SEG]) for k in range(U)]
        par = [sb(f"par1{k}", [SEG, 2]) for k in range(U)]
        kv = [sb(f"kv1c{k}", [P, T1, 2 * D]) for k in range(U)]
        kT = [sb(f"kT{k}", [P, HALF, CH1]) for k in range(2)]
        mask = [sb(f"mask{k}", [SEG, CH1]) for k in range(2)]
        prob = [sb(f"prob{k}", [SEG, HEADS, CH1]) for k in range(4)]
        probT = [sb(f"probT{k}", [P, T1, HEADS, SEG]) for k in range(2)]
        top = [sb(f"top{k}", [SEG, HEADS]) for k in range(U)]
        old = [sb(f"old{k}", [SEG, HEADS]) for k in range(U)]
        peak = [sb(f"peak{k}", [SEG, HEADS]) for k in range(U)]
        drop = [sb(f"drop{k}", [SEG, HEADS]) for k in range(U)]
        neg = [sb(f"neg{k}", [SEG, HEADS]) for k in range(U)]
        fade = [sb(f"fade{k}", [SEG, HEADS]) for k in range(U)]
        mass = [sb(f"mass{k}", [SEG, HEADS]) for k in range(U)]
        faded = [sb(f"faded{k}", [SEG, HEADS]) for k in range(U)]
        acc = [sb(f"acc{k}", [SEG, D + HEADS]) for k in range(U)]
        score_p = ps("score_p", [SEG, HEADS, 512])
        kT_p = ps("kT_p", [P, CH1])
        probT_p = [ps(f"probT_p{k}", [P, HEADS, SEG]) for k in range(2)]
        acc_p = ps("acc_p", [SEG, HEADS, DK])

        filled = sem("edge1_filled")
        loaded, gathered = sems("edge1_loaded", U), sems("kv1_gathered", U)
        kT_turned, kT_ready, mask_ready = sem("kT_turned"), sem("kT_ready"), sem("mask_ready")
        score_ready, top_ready = sem("score_ready"), sem("top_ready")
        old_ready, peak_ready, shift_ready = sem("old_ready"), sem("peak_ready"), sem("peak_used")
        prob_ready, fade_ready = sem("prob_ready"), sem("fade_ready")
        probT_turned, probT_act, probT_dve = sem("probT_turned"), sem("probT_act"), sem("probT_dve")
        acc_summed, faded_ready, acc_ready = sem("acc_summed"), sem("faded_ready"), sem("acc_ready")
        stored, held = sem("acc_stored"), sem("edge1_held")
        LOADS = 5

        with nc.Block() as block:
            @block.sync
            def _(sp):
                sp.wait_ge(filled, 3 * U)
                steps = chunk_steps(sp, c["steps1"])
                blk, k_in, first, n, at, row, later, done = (sp.alloc_register(name + "1") for name in (
                    "blk", "k_in", "first", "n", "at", "row", "later", "done"))
                used = [sp.alloc_register(f"used1{k}") for k in range(U)]
                sp.reg_mov(blk, 0)
                sp.reg_mov(k_in, 0)

                def load(it):
                    k = it.slot(U)
                    b = sp.snap(blk, min_val=0, max_val=SUBS)
                    sp.reg_load((first, n), c["runs1"][0:1, ds(b, 1), :])
                    sp.reg_mul(at, k_in, CH1 // MINI)
                    sp.reg_add(at, at, first)
                    sp.reg_mul(at, at, MINI)
                    edge = sp.snap(at, min_val=0, max_val=EP - CH1)
                    sp.reg_alu(row, blk, SUBS - 1, ALU.min)
                    sub = sp.snap(row, min_val=0, max_val=SUBS - 1)
                    sp.reg_alu(later, k_in, 1, ALU.min)
                    flag = sp.snap(later, min_val=0, max_val=1)
                    wait(sp, acc_ready, it, U)
                    sp.sem_inc(held, 1)
                    sp.dma_start(rec[k][:], c["rec_d"][ds(edge, CH1), :].rearrange("(p t) f -> p t f", t=T1)
                                 ).then_inc(loaded[k], 16)
                    for odd in range(2):
                        rows = slice(odd * DK, (odd + 1) * DK)
                        sp.dma_start(qrel[k][rows, odd::2, :], c["qrel_d"][ds(sub, 1), rows].rearrange(
                            "o p (a s) -> (o p) a s", a=HALF)).then_inc(loaded[k], 16)
                    sp.dma_start(key[k][:], c["key_d"][:, ds(edge, CH1)].to_broadcast([SEG, CH1])
                                 ).then_inc(loaded[k], 16)
                    sp.dma_start(par[k][:], w0["par1"][ds(flag * SEG, SEG), ds(sub * 2, 2)]).then_inc(loaded[k], 16)
                    sp.reg_mov(used[k], blk)
                    sp.reg_add(k_in, k_in, 1)
                    sp.reg_alu(done, k_in, n, ALU.is_ge)
                    sp.reg_add(blk, blk, done)
                    sp.reg_alu(blk, blk, SUBS, ALU.min)
                    sp.reg_alu(done, 1, done, ALU.subtract)
                    sp.reg_mul(k_in, k_in, done)

                def store(it):
                    k = it.slot(U)
                    b = sp.snap(used[k], min_val=0, max_val=SUBS)
                    wait(sp, acc_ready, it)
                    sp.sem_inc(held, 1)
                    wait(sp, stored, it, 1, per=16)
                    sp.sem_inc(held, 1)
                    sp.dma_start(c["acc_d"][ds(b * SEG, SEG), :], acc[k][:]).then_inc(stored, 16)

                run_chunks(sp, steps, ((0, load), (5, store)))
                sp.wait_ge(stored, Item(steps, -1, U).count(per=16))
                sp.sem_inc(held, 1)

            @block.gpsimd
            def _(pool):
                steps = chunk_steps(pool, c["steps1"])

                def gather(it):
                    k = it.slot(U)
                    wait_slot(pool, loaded, it, LOADS)
                    pool.sem_inc(held, 1)
                    wait(pool, acc_summed, it, U)
                    pool.sem_inc(held, 1)
                    for t in range(T1):
                        pool.indirect_dma_start(
                            kv[k][:, t, :], None, c["kv1_d"],
                            bass.IndirectOffsetOnAxis(ap=rec[k][:, t, 0:1].bitcast(I32), axis=0)
                        ).then_inc(gathered[k], 16)

                run_chunks(pool, steps, ((0, gather),))

            @block.scalar
            def _(act):
                steps = chunk_steps(act, c["steps1"])

                def k_out(a):
                    def f(it):
                        k = it.slot(2)
                        act.wait_ge(kT_turned, it.count(1, HALF, a + 1))
                        wait(act, score_ready, it, 2, per=HEADS)
                        act.copy(kT[k][:, a, :], kT_p[:]).then_inc(kT_ready, 1)
                    return f

                def prob_out(t):
                    def f(it):
                        act.wait_ge(probT_turned, it.count(1, T1, t + 1))
                        wait(act, acc_summed, it, 2)
                        act.copy(probT[it.slot(2)][:, t], probT_p[t % 2][:]).then_inc(probT_act, 1)
                    return f

                def exps(it):
                    k, s = it.slot(4), it.slot(U)
                    wait(act, shift_ready, it)
                    wait(act, acc_ready, it, U)
                    act.activation(fade[s][:], drop[s][:], ACT.Exp).then_inc(fade_ready, 1)
                    for h in range(HEADS):
                        ins = act.activation(prob[k][:, h, :], prob[k][:, h, :], ACT.Exp, bias=neg[s][:, h:h + 1],
                                             accum_out=mass[s][:, h:h + 1])
                    ins.then_inc(prob_ready, 1)

                run_chunks(act, steps, ((2, exps), (3, prob_out(1)), (0, k_out(0)), (3, prob_out(2)), (0, k_out(1))))

            @block.vector
            def _(dve):
                for k in range(U):
                    dve.memset(peak[k][:], 0.0).then_inc(filled, 1)
                    dve.memset(acc[k][:], 0.0).then_inc(filled, 1)
                    dve.memset(qrel[k][:], 0.0).then_inc(filled, 1)
                dve.wait_ge(filled, 3 * U)
                steps = chunk_steps(dve, c["steps1"])

                def masks(it):
                    k, s = it.slot(2), it.slot(U)
                    wait_slot(dve, loaded, it, LOADS)
                    wait(dve, top_ready, it, 2, per=HEADS)
                    dve.tensor_scalar(mask[k][:].rearrange("s (t p) -> s t p", p=P),
                                      key[s][:].rearrange("s (p t) -> s t p", p=P), par[s][:, 0:1], -BIG,
                                      ALU.not_equal, ALU.mult).then_inc(mask_ready, 1)

                def maxima(heads):
                    def f(it):
                        k, s = it.slot(2), it.slot(U)
                        wait(dve, mask_ready, it)
                        wait(dve, probT_turned, it, 4, per=T1)
                        wait(dve, peak_ready, it, U)
                        for h in heads:
                            dve.wait_ge(score_ready, it.count(1, HEADS, h + 1))
                            dve.sem_inc(held, 1)
                            dve.tensor_tensor_reduce(prob[it.slot(4)][:, h, :], score_p[:, h, 0:CH1], mask[k][:], 1.0, -BIG,
                                                     ALU.add, ALU.max, top[s][:, h:h + 1]).then_inc(top_ready, 1)
                    return f

                def peaks(it):
                    s = it.slot(U)
                    wait(dve, fade_ready, it, U)
                    wait(dve, prob_ready, it, U)
                    dve.tensor_scalar(old[s][:], peak[it.prev().slot(U)][:], par[s][:, 1:2], None,
                                      ALU.add).then_inc(old_ready, 1)
                    wait(dve, old_ready, it)
                    wait(dve, top_ready, it, per=HEADS)
                    dve.scalar_tensor_tensor(peak[s][:], top[s][:], FLOOR, old[s][:], ALU.max,
                                             ALU.max).then_inc(peak_ready, 1)
                    wait(dve, peak_ready, it)
                    dve.tensor_scalar(neg[s][:], peak[s][:], -1.0, None, ALU.mult)
                    dve.tensor_tensor(drop[s][:], old[s][:], peak[s][:], ALU.subtract).then_inc(shift_ready, 1)

                def prob_out(it):
                    dve.wait_ge(probT_turned, it.count(1, T1, 1))
                    wait(dve, acc_summed, it, 2)
                    dve.tensor_copy(probT[it.slot(2)][:, 0], probT_p[0][:]).then_inc(probT_dve, 1)

                def add_acc(it):
                    s, last = it.slot(U), it.prev().slot(U)
                    wait(dve, fade_ready, it)
                    wait(dve, prob_ready, it)
                    wait(dve, stored, it, U, per=16)
                    wait(dve, acc_ready, it, 1)
                    dve.tensor_tensor(faded[s][:], acc[last][:, D:D + HEADS], fade[s][:], ALU.mult).then_inc(faded_ready, 1)
                    wait(dve, acc_summed, it)
                    for h in range(HEADS):
                        cols = slice(h * DK, (h + 1) * DK)
                        dve.scalar_tensor_tensor(acc[s][:, cols], acc[last][:, cols], fade[s][:, h:h + 1],
                                                 acc_p[:, h, :], ALU.mult, ALU.add)
                    wait(dve, faded_ready, it)
                    dve.tensor_tensor(acc[s][:, D:D + HEADS], faded[s][:], mass[s][:], ALU.add).then_inc(acc_ready, 1)

                run_chunks(dve, steps, ((0, masks), (4, add_acc), (1, maxima((0, 1))), (3, prob_out),
                                        (1, maxima((2, 3))), (1, peaks)))

            @block.tensor
            def _(pe):
                pe.wait_ge(filled, 3 * U)
                steps = chunk_steps(pe, c["steps1"])

                def turn_k(a):
                    def f(it):
                        s = it.slot(U)
                        wait_slot(pe, gathered, it, T1)
                        pe.wait_ge(kT_ready, it.count(1, HALF, a)) if a or not (
                            isinstance(it.i, int) and it.index == 0) else None
                        for t in range(T1):
                            ins = pe.transpose(kT_p[:, t * P:(t + 1) * P], kv[s][:, t, a * P:(a + 1) * P], c["ident"][:])
                        ins.then_inc(kT_turned, 1)
                    return f

                def scores(heads):
                    def f(it):
                        k, s = it.slot(2), it.slot(U)
                        for h in heads:
                            pe.wait_ge(kT_ready, it.count(1, HALF, h // 2 + 1))
                            if not (isinstance(it.i, int) and it.index == 0):
                                pe.wait_ge(top_ready, it.count(2, HEADS, h + 1))
                            pe.matmul(score_p[:, h, 0:CH1], qrel[s][:, h, :], kT[k][:, h // 2, :],
                                      start=True, stop=True).then_inc(score_ready, 1)
                    return f

                def turn_prob(t):
                    def f(it):
                        k = it.slot(4)
                        wait(pe, prob_ready, it)
                        if t == 0:
                            wait(pe, probT_act, it, 1, per=2)
                        elif t == 1:
                            wait(pe, probT_act, it, 1, per=2, extra=-1)
                        else:
                            wait(pe, probT_dve, it)
                        for h in range(HEADS):
                            ins = pe.transpose(probT_p[t % 2][:, h, :], prob[k][:, h, t * P:(t + 1) * P],
                                               c["ident"][0:SEG, 0:SEG])
                        ins.then_inc(probT_turned, 1)
                    return f

                def weigh(t):
                    def f(it):
                        k, s = it.slot(2), it.slot(U)
                        if t == 0:
                            wait(pe, probT_dve, it)
                            wait(pe, acc_ready, it, 1)
                        else:
                            pe.wait_ge(probT_act, it.count(1, 2, t))
                        for h in range(HEADS):
                            ins = pe.matmul(acc_p[:, h, :], probT[k][:, t, h, :],
                                            kv[s][:, t, D + h * DK:D + (h + 1) * DK],
                                            start=t == 0 and h == 0, stop=t == T1 - 1 and h == HEADS - 1,
                                            skip_group_check=True)
                        if t == T1 - 1:
                            ins.then_inc(acc_summed, 1)
                    return f

                run_chunks(pe, steps, ((1, scores((0, 1))), (3, turn_prob(0)), (3, turn_prob(1)), (0, turn_k(0)),
                                       (1, scores((2, 3))), (3, turn_prob(2)), (0, turn_k(1)), (3, weigh(0)),
                                       (3, weigh(1)), (3, weigh(2))))


def nodes_out(nc, c):
    sem, sems = c["sem"], c["sems"]
    w0 = c["w0"]
    UN = 8
    with ExitStack() as ctx:
        def sb(name, shape, dt=F32):
            return ctx.enter_context(nc.sbuf_tensor(name, shape, dt))

        def ps(name, shape):
            return ctx.enter_context(nc.psum_tensor(name, shape, F32))

        m_rel = sb("m_rel", [P, RELS, HALF, P])
        w_a = sb("w_a", [P, TYPES * HALF, D])
        same_node = sb("same_node", [SEG, SUB])
        ones = sb("ones", [SEG, 1])
        skip = sb("skip", [P, TYPES])
        gain = sb("gain", [P, TYPES])
        acc = [sb(f"acc_in{k}", [SEG, PER_GROUP, D + HEADS]) for k in range(2)]
        x1 = [sb(f"x1o{k}", [GROUP, D]) for k in range(UN)]
        h1 = [sb(f"h1o{k}", [GROUP, D]) for k in range(UN)]
        kind_row = [sb(f"kind_row_o{k}", [P, GROUP], I32) for k in range(UN)]
        kind_col = [sb(f"kind_col_o{k}", [GROUP, 1], I32) for k in range(UN)]
        typed = [sb(f"typed{k}", [GROUP, 3 * D]) for k in range(UN)]
        of_kind = [sb(f"of_kind_o{k}", [P, TYPES, GROUP]) for k in range(UN)]
        row_kind = [sb(f"row_kind{k}", [GROUP, TYPES]) for k in range(UN)]
        alpha = [sb(f"alpha{k}", [GROUP, 1]) for k in range(UN)]
        mass = [sb(f"mass_o{k}", [SEG, PER_GROUP, HEADS]) for k in range(2)]
        inv = [sb(f"inv{k}", [SEG, PER_GROUP, HEADS]) for k in range(2)]
        here = [sb(f"here{k}", [SEG, PER_GROUP]) for k in range(2)]
        spread = [sb(f"spread{k}", [SEG, PER_GROUP, SUB]) for k in range(2)]
        mean = [sb(f"mean{k}", [SEG, PER_GROUP, D]) for k in range(2)]
        meanT = [sb(f"meanT{k}", [P, HALF, RELS, PER_GROUP, SUB]) for k in range(2)]
        tT = [sb(f"tT{k}", [P, TYPES, HALF, GROUP]) for k in range(2)]
        count = [sb(f"count{k}", [GROUP, 2]) for k in range(UN)]
        per_rel = [sb(f"per_rel{k}", [GROUP, 1]) for k in range(UN)]
        trans = [sb(f"trans{k}", [GROUP, D]) for k in range(UN)]
        mixed = [sb(f"mixed{k}", [GROUP, D]) for k in range(UN)]
        stat = [sb(f"stat_o{k}", [GROUP, 6]) for k in range(UN)]
        mv = [sb(f"mv_o{k}", [GROUP, 2]) for k in range(UN)]
        std = [sb(f"std_o{k}", [GROUP, 1]) for k in range(UN)]
        rstd = [sb(f"rstd_o{k}", [GROUP, 1]) for k in range(UN)]
        shift = [sb(f"shift_o{k}", [GROUP, 1]) for k in range(UN)]
        normed = [sb(f"normed{k}", [GROUP, D]) for k in range(UN)]
        xh = [sb(f"xh_o{k}", [GROUP, D]) for k in range(UN)]
        res = [sb(f"res{k}", [GROUP, D]) for k in range(UN)]
        meanT_p = [ps(f"meanT_p{k}", [P, 2, HALF, SEG]) for k in range(2)]
        tT_p = ps("tT_p", [P, HALF, GROUP])
        trans_p = ps("trans_p", [GROUP, D])
        count_p = ps("count_p", [GROUP, 1])

        w_loaded, gain_ready, filled = sem("w_out_loaded"), sem("gain_ready"), sem("out_filled")
        loaded, typed_got = sems("out_loaded", UN), sems("typed_gathered", UN)
        mass_ready, inv_ready, here_ready, mean_ready = sem("mass_o"), sem("inv_o"), sem("here_o"), sem("mean_o")
        spread_ready, count_summed, count_ready = sem("spread_o"), sem("count_summed"), sem("count_ready")
        meanT_turned, meanT_act, meanT_dve = sem("meanT_turned"), sem("meanT_act"), sem("meanT_dve")
        kinds_ready, row_kind_ready, alpha_ready = sem("kinds_o"), sem("row_kind_o"), sem("alpha_o")
        tT_summed, tT_ready, trans_summed = sem("tT_summed"), sem("tT_ready"), sem("trans_summed")
        per_rel_ready, trans_ready, less_ready, mixed_ready = sem("per_rel"), sem("trans_o"), sem("less_o"), sem("mixed_o")
        stat_ready, var_ready, std_ready = sem("stat_o"), sem("var_o"), sem("std_o")
        rstd_ready, shift_ready, normed_ready = sem("rstd_o"), sem("shift_o"), sem("normed_o")
        scaled_ready, affine_ready, xh_ready = sem("scaled_o"), sem("affine_o"), sem("xh_o")
        diff_ready, res_ready = sem("diff_o"), sem("res_o")
        stored, held = sems("out_stored", UN), sem("out_held")
        LOADS, WEIGHTS = 5, 4
        PAIRS = PER_GROUP // 2

        with nc.Block() as block:
            @block.sync
            def _(sp):
                for dst, src in ((m_rel[:], w0["m_rel"]), (w_a[:], w0["w_a"].rearrange("(a p) n -> p a n", p=P)),
                                 (same_node[:], w0["same_node"]), (skip[:], w0["skip"].to_broadcast([P, TYPES]))):
                    sp.dma_start(dst, src).then_inc(w_loaded, 16)

                def load(it):
                    k = it.slot(UN)
                    rows = ds(it.index * GROUP, GROUP)
                    wait(sp, mean_ready, it, 2)
                    sp.sem_inc(held, 1)
                    wait(sp, res_ready, it, UN)
                    sp.dma_start(acc[it.slot(2)][:], c["acc_d"].rearrange("(b s) f -> s b f", s=SEG)[
                        :, ds(it.index * PER_GROUP, PER_GROUP), :]).then_inc(loaded[k], 16)
                    sp.dma_start(x1[k][:], c["x1_d"][rows, :]).then_inc(loaded[k], 16)
                    sp.dma_start(h1[k][:], c["h1_d"][rows, :]).then_inc(loaded[k], 16)
                    sp.dma_start(kind_row[k][:], c["node_type"][:, rows].to_broadcast([P, GROUP])
                                 ).then_inc(loaded[k], 16)
                    sp.dma_start(kind_col[k][:], c["node_type"].rearrange("o n -> n o")[rows, :]
                                 ).then_inc(loaded[k], 16)

                def store(it):
                    k = it.slot(UN)
                    wait(sp, res_ready, it)
                    sp.dma_start(c["out"][ds(it.index * GROUP, GROUP), :], res[k][:]).then_inc(stored[k], 16)

                run_stages(sp, GROUPS, ((0, load), (7, store)), UN)
                for k in range(UN):
                    sp.wait_ge(stored[k], 16 * len(range(k, GROUPS, UN)))

            @block.gpsimd
            def _(pool):
                def gather(it):
                    k = it.slot(UN)
                    wait_slot(pool, loaded, it, LOADS)
                    pool.sem_inc(held, 1)
                    wait(pool, affine_ready, it, UN)
                    pool.sem_inc(held, 1)
                    pool.indirect_dma_start(typed[k][:], None, w0["typed"],
                                            bass.IndirectOffsetOnAxis(ap=kind_col[k][:], axis=0)
                                            ).then_inc(typed_got[k], 16)
                    wait(pool, res_ready, it, UN)
                    pool.tensor_tensor(xh[k][:], x1[k][:], h1[k][:], ALU.add).then_inc(xh_ready, 1)

                def affine(it):
                    k = it.slot(UN)
                    wait(pool, normed_ready, it)
                    pool.tensor_tensor(normed[k][:], normed[k][:], typed[k][:, D:2 * D], ALU.mult).then_inc(scaled_ready, 1)
                    wait(pool, scaled_ready, it)
                    pool.tensor_tensor(normed[k][:], normed[k][:], typed[k][:, 2 * D:3 * D], ALU.add).then_inc(affine_ready, 1)

                run_stages(pool, GROUPS, ((0, gather), (5, affine)), UN)

            @block.scalar
            def _(act):
                act.wait_ge(w_loaded, 16 * WEIGHTS)
                act.activation(gain[:], skip[:], ACT.Sigmoid).then_inc(gain_ready, 1)

                def turn_out(it):
                    k = it.slot(2)
                    wait(act, tT_summed, it, 2)
                    for pair in range(0, PAIRS, 2):
                        act.wait_ge(meanT_turned, it.count(1, PAIRS, pair + 1))
                        for j in range(2):
                            ins = act.copy(meanT[k][:, :, :, 2 * pair + j, :],
                                           meanT_p[0][:, j].rearrange("p a (r n) -> p a r n", n=SUB))
                        ins.then_inc(meanT_act, 1)

                def root(it):
                    k = it.slot(UN)
                    wait(act, var_ready, it)
                    wait(act, shift_ready, it, UN)
                    act.activation(std[k][:], mv[k][:, 1:2], ACT.Sqrt, bias=c["eps"][0:GROUP, :]).then_inc(std_ready, 1)

                run_stages(act, GROUPS, ((1, turn_out), (4, root)), UN)

            @block.vector
            def _(dve):
                dve.memset(ones[:], 1.0).then_inc(filled, 1)
                dve.wait_ge(w_loaded, 16 * WEIGHTS)
                dve.wait_ge(gain_ready, 1)

                def kinds(it):
                    k = it.slot(UN)
                    wait_slot(dve, loaded, it, LOADS)
                    wait(dve, mixed_ready, it, UN)
                    for t in range(TYPES):
                        dve.tensor_scalar(of_kind[k][:, t, :], kind_row[k][:], float(t), None, ALU.is_equal)
                    dve.tensor_scalar(row_kind[k][:], c["iota"][0:GROUP, 0:TYPES], kind_col[k][:], None,
                                      ALU.is_equal).then_inc(row_kind_ready, 1)
                    wait(dve, row_kind_ready, it)
                    dve.sem_inc(held, 1)
                    dve.tensor_tensor_reduce(row_kind[k][:], row_kind[k][:], gain[0:GROUP, :], 1.0, 0.0, ALU.mult,
                                             ALU.add, alpha[k][:]).then_inc(alpha_ready, 1)

                def means(it):
                    k = it.slot(2)
                    wait(dve, mean_ready, it, 2)
                    dve.tensor_scalar(mass[k][:], acc[k][:, :, D:D + HEADS], 0.5, None, ALU.max).then_inc(mass_ready, 1)
                    wait(dve, count_summed, it, 2)
                    dve.tensor_scalar(here[k][:], acc[k][:, :, D], 0.5, None, ALU.is_gt).then_inc(here_ready, 1)
                    wait(dve, mass_ready, it)
                    dve.reciprocal(inv[k][:], mass[k][:]).then_inc(inv_ready, 1)
                    wait(dve, here_ready, it)
                    dve.tensor_tensor(spread[k][:], same_node[:].rearrange("s (o n) -> s o n", o=1).to_broadcast(
                        [SEG, PER_GROUP, SUB]), here[k][:].rearrange("s (j o) -> s j o", o=1).to_broadcast(
                        [SEG, PER_GROUP, SUB]), ALU.mult).then_inc(spread_ready, 1)
                    wait(dve, inv_ready, it)
                    wait(dve, meanT_turned, it, 2, per=PAIRS)
                    dve.tensor_tensor(mean[k][:].rearrange("s j (h e) -> s j h e", h=HEADS),
                                      acc[k][:, :, 0:D].rearrange("s j (h e) -> s j h e", h=HEADS),
                                      inv[k][:].rearrange("s j (h o) -> s j h o", o=1).to_broadcast(
                                          [SEG, PER_GROUP, HEADS, DK]), ALU.mult).then_inc(mean_ready, 1)

                def turn_out(it):
                    k = it.slot(2)
                    wait(dve, tT_summed, it, 2)
                    dve.wait_ge(meanT_turned, it.count(1, PAIRS, 2))
                    for j in range(2):
                        ins = dve.tensor_copy(meanT[k][:, :, :, 2 + j, :],
                                              meanT_p[1][:, j].rearrange("p a (r n) -> p a r n", n=SUB))
                    ins.then_inc(meanT_dve, 1)

                def split_kinds(it):
                    k = it.slot(2)
                    wait(dve, tT_summed, it)
                    wait(dve, alpha_ready, it)
                    wait(dve, trans_summed, it, 2)
                    for t in range(TYPES):
                        ins = dve.tensor_tensor(tT[k][:, t], tT_p[:], of_kind[it.slot(UN)][:, t:t + 1, :].to_broadcast(
                            [P, HALF, GROUP]), ALU.mult)
                    ins.then_inc(tT_ready, 1)

                def counts(it):
                    k = it.slot(UN)
                    wait(dve, count_summed, it)
                    wait(dve, res_ready, it, UN)
                    dve.tensor_scalar(count[k][:, 0:1], count_p[:], 1.0, None, ALU.max)
                    dve.tensor_scalar(count[k][:, 1:2], count_p[:], 0.5, None, ALU.is_gt).then_inc(count_ready, 1)
                    wait(dve, count_ready, it)
                    dve.reciprocal(per_rel[k][:], count[k][:, 0:1]).then_inc(per_rel_ready, 1)

                def mix(it):
                    k = it.slot(UN)
                    wait(dve, trans_summed, it)
                    wait(dve, per_rel_ready, it)
                    wait_slot(dve, typed_got, it)
                    dve.scalar_tensor_tensor(trans[k][:], trans_p[:], per_rel[k][:], typed[k][:, 0:D],
                                             ALU.mult, ALU.add).then_inc(trans_ready, 1)
                    wait(dve, trans_ready, it)
                    dve.tensor_tensor(trans[k][:], trans[k][:], h1[k][:], ALU.subtract).then_inc(less_ready, 1)
                    wait(dve, less_ready, it)
                    wait(dve, normed_ready, it, UN)
                    dve.scalar_tensor_tensor(mixed[k][:], trans[k][:], alpha[k][:], h1[k][:],
                                             ALU.mult, ALU.add).then_inc(mixed_ready, 1)
                    wait(dve, mixed_ready, it)
                    dve.bn_stats(stat[k][:], mixed[k][:]).then_inc(stat_ready, 1)
                    wait(dve, stat_ready, it)
                    dve.sem_inc(held, 1)
                    wait(dve, shift_ready, it, UN)
                    dve.sem_inc(held, 1)
                    dve.bn_aggr(mv[k][:], stat[k][:]).then_inc(var_ready, 1)

                def norm(it):
                    k = it.slot(UN)
                    wait(dve, std_ready, it)
                    wait(dve, normed_ready, it, UN)
                    dve.reciprocal(rstd[k][:], std[k][:]).then_inc(rstd_ready, 1)
                    wait(dve, rstd_ready, it)
                    dve.scalar_tensor_tensor(shift[k][:], mv[k][:, 0:1], -1.0, rstd[k][:],
                                             ALU.mult, ALU.mult).then_inc(shift_ready, 1)
                    wait(dve, shift_ready, it)
                    wait(dve, diff_ready, it, UN)
                    dve.tensor_scalar(normed[k][:], mixed[k][:], rstd[k][:], shift[k][:],
                                      ALU.mult, ALU.add).then_inc(normed_ready, 1)

                def finish(it):
                    k = it.slot(UN)
                    wait(dve, affine_ready, it)
                    wait(dve, res_ready, it, UN)
                    dve.tensor_tensor(normed[k][:], normed[k][:], h1[k][:], ALU.subtract).then_inc(diff_ready, 1)
                    wait(dve, diff_ready, it)
                    wait(dve, xh_ready, it)
                    if not (isinstance(it.i, int) and it.index < UN):
                        dve.wait_ge(stored[k], it.round(0) * 16)
                    dve.scalar_tensor_tensor(res[k][:], normed[k][:], count[k][:, 1:2], xh[k][:],
                                             ALU.mult, ALU.add).then_inc(res_ready, 1)

                run_stages(dve, GROUPS, ((0, kinds), (0, means), (1, turn_out), (2, split_kinds), (1, counts), (4, mix),
                                         (5, norm), (6, finish)), UN)

            @block.tensor
            def _(pe):
                pe.wait_ge(w_loaded, 16 * WEIGHTS)
                pe.wait_ge(filled, 1)

                def turn(it):
                    k = it.slot(2)
                    wait(pe, spread_ready, it)
                    wait(pe, count_ready, it, 1)
                    pe.matmul(count_p[:], spread[k][:].rearrange("s j n -> s (j n)"), ones[:], start=True,
                              stop=True).then_inc(count_summed, 1)
                    wait(pe, mean_ready, it)
                    for pair in range(PAIRS):
                        if pair == 0:
                            wait(pe, meanT_act, it, 1, per=2)
                        elif pair == 1:
                            wait(pe, meanT_dve, it, 1)
                        else:
                            pe.wait_ge(meanT_act, it.count(1, 2, 1))
                        for j in range(2):
                            for a in range(HALF):
                                ins = pe.transpose(meanT_p[pair % 2][:, j, a, :],
                                                   mean[k][:, 2 * pair + j, a * P:(a + 1) * P],
                                                   c["ident"][0:SEG, 0:SEG])
                        ins.then_inc(meanT_turned, 1)

                def relate(it):
                    k = it.slot(2)
                    wait(pe, meanT_act, it, per=2)
                    wait(pe, meanT_dve, it)
                    wait(pe, tT_ready, it, 1)
                    for a in range(HALF):
                        for r in range(RELS):
                            ins = pe.matmul(tT_p[:, a, :], m_rel[:, r, a, :],
                                            meanT[k][:, a, r].rearrange("p j n -> p (j n)"),
                                            start=r == 0, stop=r == RELS - 1)
                    ins.then_inc(tT_summed, 1)

                def project(it):
                    k = it.slot(2)
                    wait(pe, tT_ready, it)
                    wait(pe, trans_ready, it, 1)
                    for a in range(TYPES * HALF):
                        ins = pe.matmul(trans_p[:], tT[k][:, a // HALF, a % HALF, :], w_a[:, a, :],
                                        start=a == 0, stop=a == TYPES * HALF - 1)
                    ins.then_inc(trans_summed, 1)

                run_stages(pe, GROUPS, ((1, turn), (2, relate), (3, project)), UN)


def device_arrays(a):
    def f(name):
        return np.ascontiguousarray(a[name])

    def padded(v, n, fill=0):
        out = np.full((n,) + v.shape[1:], fill, v.dtype)
        out[:v.shape[0]] = v
        return out

    rec = np.empty((EP, 4), np.int32)
    rec[:, 0] = padded(f("src").astype(np.int32, copy=False), EP)
    rec[:, 1] = padded(f("dst").astype(np.int32, copy=False), EP, RELS * N)
    rec[:, 2] = padded(f("edge_type_6").astype(np.int32, copy=False), EP)
    rec[:, 3] = padded(f("edge_weight"), EP).view(np.int32)
    ranks = np.arange(MINIS, dtype=np.float32)
    a_rel, m_rel = (np.zeros((P, RELS, HALF, P), np.float32) for _ in range(2))
    prior = np.empty((P, RELS, HALF), np.float32)
    for h in range(HEADS):
        rows = slice(h % 2 * DK, h % 2 * DK + DK)
        for r in range(RELS):
            a_rel[rows, r, h // 2, rows] = f("L1_gnn_rel_att")[r, h].T
            m_rel[rows, r, h // 2, rows] = f("L1_gnn_rel_msg")[r, h]
            prior[rows, r, h // 2] = f("L1_gnn_rel_pri")[r, h]
    seg = np.arange(SEG)
    par1 = np.zeros((2, SEG, SUBS, 2), np.float32)
    par1[:, :, :, 0] = (seg // SUB * N + seg % SUB)[:, None] + SUB * np.arange(SUBS)
    par1[0, :, :, 1] = -BIG
    return {
        "x": padded(f("x"), NP),
        "rec": rec,
        "edge_feat_t": np.ascontiguousarray(padded(f("edge_attr_64"), EP).T),
        "node_type": padded(f("node_type_3").astype(np.int32, copy=False), NP)[None, :],
        "w_qkv": np.concatenate([f("L0_gnn_Wq").T, f("L0_gnn_Wk").T, f("L0_gnn_Wv").T], 1),
        "b_qkv": np.concatenate([f("L0_gnn_bq"), f("L0_gnn_bk"), f("L0_gnn_bv")])[None, :],
        "b_o": f("L0_gnn_bo")[None, :],
        "gamma_t": np.ascontiguousarray(f("L0_gnn_ln_g").reshape(HALF, P).T),
        "beta_t": np.ascontiguousarray(f("L0_gnn_ln_b").reshape(HALF, P).T),
        "w_edge": np.concatenate([f("L0_gnn_Wdk").T, f("L0_gnn_Wdv").T], 1),
        "b_edge": np.concatenate([f("L0_gnn_bdk"), f("L0_gnn_bdv")])[None, :],
        "ident": np.eye(P, dtype=np.float32),
        "iota": np.arange(GROUP, dtype=np.float32)[None, :],
        "ranks": np.stack([MINIS - ranks, ranks + 1.0]),
        "begin": np.ascontiguousarray((SUB * np.arange(SUBS, dtype=np.float32)).reshape(SUB_COLS, SUB_ROWS).T),
        "w_o": f("L0_gnn_Wo").T,
        "w_kv1": np.concatenate([f("L1_gnn_Wk"), f("L1_gnn_Wv")], 2).reshape(TYPES * D, 2 * D),
        "w_q1": f("L1_gnn_Wq").reshape(TYPES * D, D),
        "b_q1": f("L1_gnn_bq"),
        "b_kv1": np.concatenate([f("L1_gnn_bk"), f("L1_gnn_bv")], 1),
        "a_rel": a_rel,
        "m_rel": m_rel,
        "prior": prior,
        "part": np.arange(P, dtype=np.float32)[:, None],
        "par1": par1.reshape(2 * SEG, 2 * SUBS),
        "w_a": f("L1_gnn_Wa").reshape(TYPES * D, D),
        "typed": np.concatenate([f("L1_gnn_ba"), f("L1_gnn_ln_g"), f("L1_gnn_ln_b")], 1),
        "skip": f("L1_gnn_skip")[None, :],
        "same_node": (np.arange(SEG)[:, None] % SUB == np.arange(SUB)).astype(np.float32),
    }


def kernel(**inputs):
    import concourse.bacc as bacc
    from concourse.bass_utils import run_bass_kernel_spmd

    nc = bacc.Bacc("TRN2", target_bir_lowering=False, num_devices=1)
    arrays, aps = {}, {}
    for name, v in device_arrays(inputs).items():
        v = np.ascontiguousarray(v)
        arrays["in_" + name] = v
        aps[name] = nc.dram_tensor("in_" + name, v.shape, mybir.dt.from_np(v.dtype), kind="ExternalInput").ap()
    out = nc.dram_tensor("out_0", (NP, D), F32, kind="ExternalOutput").ap()
    build(nc, aps.pop("x"), aps.pop("rec"), aps.pop("edge_feat_t"), aps.pop("node_type"), aps, out)
    r = run_bass_kernel_spmd(nc, [arrays], core_ids=[0])
    return r.results[0]["out_0"][:N]
```

```python
from contextlib import ExitStack

import numpy as np

import concourse.bass as bass
from concourse import mybir

F32 = mybir.dt.float32
F32R = mybir.dt.float32r
BF16 = mybir.dt.bfloat16
I32 = mybir.dt.int32
ALU = mybir.AluOpType
ACT = mybir.ActivationFunctionType
AX = mybir.AxisListType.X
ds = bass.ds

P = 128
N, E, D, R = 6250, 100000, 256, 64
TYPES, RELS, HEADS = 3, 6, 4
DK = D // HEADS
HALF = D // P
EPS = 1e-5
CUTOFF = 5.0

SUB = 21
SEG = SUB * RELS
PER_GROUP = 6
GROUP = SUB * PER_GROUP
GROUPS = -(-N // GROUP)
SUBS = GROUPS * PER_GROUP
NP = GROUPS * GROUP

MINI = 16
MINIS = E // MINI
PER_PART = 800
EP = P * PER_PART
REAL_PARTS = E // PER_PART
T0, T1 = 4, 3
CH0, CH1 = T0 * P, T1 * P
U = 8
BIG = 2.0 ** 100
FLOOR = -1e25
MIN_STEPS = 3
PARTS = 3
Q_ROW = PARTS * D + 2
SUB_ROWS, SUB_COLS = 100, 3
assert SUB_ROWS * SUB_COLS == SUBS and REAL_PARTS * PER_PART == E


class Item:

    def __init__(self, i, off, unroll):
        self.i, self.off, self.unroll = i, off, unroll

    def slot(self, depth):
        return self.off % depth

    def prev(self, n=1):
        return Item(self.i, self.off - n, self.unroll)

    def count(self, lag=0, per=1, extra=0):
        if isinstance(self.i, int):
            return (self.unroll * self.i + self.off + 1 - lag) * per + extra
        return self.i * (self.unroll * per) + ((self.off + 1 - lag) * per + extra)

    def round(self, ahead=1):
        return self.i + (self.off // self.unroll + ahead)

    @property
    def index(self):
        return self.i * self.unroll + self.off


def wait(eng, sem, item, lag=0, per=1, extra=0):
    value = item.count(lag, per, extra)
    if not (isinstance(value, int) and value <= 0):
        eng.wait_ge(sem, value)


def hold(eng, held, sem, value):
    eng.wait_ge(sem, value)
    eng.sem_inc(held, 1)


def wait_slot(eng, sems, item, dmas=1):
    eng.wait_ge(sems[item.slot(item.unroll)], item.round() * (16 * dmas))


def wait_pair(eng, sems, item):
    eng.wait_ge(sems[item.slot(2)], item.i * (8 * item.unroll) + 16 * (item.off // 2))


def run_stages(eng, n, stages, unroll):
    most = max(lag for lag, _ in stages)
    peel = -(-(most + unroll) // unroll)

    def step(i, u, whole):
        for lag, f in stages:
            item = Item(i, u - lag, unroll)
            if whole or 0 <= item.index < n:
                f(item)

    for s in range(peel * unroll):
        step(s // unroll, s % unroll, False)
    with eng.Fori(peel, n // unroll) as i:
        for u in range(unroll):
            step(i, u, True)
    for s in range(n // unroll * unroll, n + most):
        step(s // unroll, s % unroll, False)


def chunk_steps(eng, spare):
    return eng.value_load(spare[0:1, 0:1], min_val=0, max_val=1 << 20) + MIN_STEPS


def run_chunks(eng, steps, stages):
    most = max(lag for lag, _ in stages)
    for s in range(2 * U):
        for lag, f in stages:
            if s >= lag:
                f(Item(s // U, s % U - lag, U))
    with eng.Fori(2, steps) as i:
        for u in range(U):
            for lag, f in stages:
                f(Item(i, u - lag, U))
    for e in range(most):
        for lag, f in stages:
            if e < lag:
                f(Item(steps, e - lag, U))


def halves(ap):
    return ap.rearrange("(c p) n -> p c n", p=P)


def build(nc, x, rec, edge_feat_t, node_type, w0, out):
    with ExitStack() as top:
        def sem(name):
            return nc.alloc_semaphore(name=name)

        def sems(name, n):
            return [sem(f"{name}{k}") for k in range(n)]

        def keep(name, shape, dt=F32):
            return top.enter_context(nc.sbuf_tensor(name, shape, dt))

        def dram(name, shape, dt=F32):
            return nc.dram_tensor(name, shape, dt, kind="Internal").ap()

        rec_d = dram("edge_records", [EP, 4])
        key_d = dram("segment_keys", [1, EP])
        span_d = dram("mini_spans", [2, MINIS])
        range_d = dram("block_ranges", [2, SUBS])
        q0_d = dram("q0_table", [GROUPS * P, Q_ROW], BF16)
        kv0_d = dram("kv0_table", [NP, 2 * D])
        xh_d = dram("x_plus_h", [NP, D])
        agg_d = dram("agg0_table", [(GROUPS + 1) * GROUP, D])
        x1_d, h1_d = dram("x1", [NP, D]), dram("h1", [NP, D])
        kv1_d = dram("kv1_table", [NP, 2 * D])
        qrel_d = dram("q_by_relation", [NP * RELS, D])
        acc_d = dram("acc1_table", [(SUBS + 1) * SEG, HEADS * (DK + 1)])

        ident = keep("ident", [P, P])
        iota = keep("iota", [P, GROUP])
        eps, one, minus_big = keep("eps", [P, 1]), keep("one", [P, 1]), keep("minus_big", [P, 1])
        runs0, runs1 = keep("runs0", [1, GROUPS + 1, 2], I32), keep("runs1", [1, SUBS + 1, 2], I32)
        lo0, n0, lo1, n1 = runs0[:, :, 0], runs0[:, :, 1], runs1[:, :, 0], runs1[:, :, 1]
        steps0, steps1 = keep("steps0", [1, 1], I32), keep("steps1", [1, 1], I32)

        c = dict(locals())
        before = nc.snapshot_sems()
        prepare(nc, c)
        nodes_0(nc, c)
        w1_loaded = sem("w1_loaded")
        w1 = {"w_o": keep("w_o", [P, HALF, D]), "w_kvq1": keep("w1_raw", [P, TYPES * HALF, 3 * D]),
              "a_rel": keep("a_rel", [P, HALF, RELS, P]), "prior": keep("prior", [P, HALF, RELS])}
        c.update(w1=w1, w1_loaded=w1_loaded)
        edges_0(nc, c)
        nc.clear_and_free_semaphores(nc.allocated_since(before))
        nc.all_engine_barrier()
        nodes_1(nc, c)
        edges_1(nc, c)
        nodes_out(nc, c)


def prepare(nc, c):
    sem = c["sem"]
    w0 = c["w0"]
    with ExitStack() as ctx:
        def sb(name, shape, dt=F32):
            return ctx.enter_context(nc.sbuf_tensor(name, shape, dt))

        rec_in = sb("rec_in", [P, PER_PART, 4], I32)
        rec_out = sb("rec_out", [P, PER_PART, 4])
        key = sb("key", [P, PER_PART])
        clip = sb("clip", [P, PER_PART])
        cosine = sb("cosine", [P, PER_PART])
        half_pi = sb("half_pi", [P, 1])
        span = sb("span", [REAL_PARTS, 2, PER_PART // MINI])
        span_all = sb("span_all", [SUB_ROWS, 2, MINIS])
        begin = sb("begin", [SUB_ROWS, SUB_COLS])
        end = sb("end", [SUB_ROWS, SUB_COLS])
        reach = sb("reach", [SUB_ROWS, MINIS])
        junk = sb("junk", [SUB_ROWS, MINIS])
        edge_range = sb("edge_range", [SUB_ROWS, 2, SUB_COLS])
        row = sb("row", [1, 2, SUBS])
        lo_f, hi_f, len_f = row[:, 0, :], sb("hi_f", [1, SUBS]), sb("len_f", [1, SUBS])
        lo0_f, hi0_f = sb("lo0_f", [1, GROUPS]), sb("hi0_f", [1, GROUPS])
        total = sb("total", [1, 2])
        total_i = sb("total_i", [1, 2], I32)

        loaded, consts_loaded = sem("prep_loaded"), sem("prep_consts")
        filled = sem("prep_filled")
        clipped, cosine_ready = sem("prep_clipped"), sem("prep_cosine")
        span_ready, span_stored, span_back = sem("span_ready"), sem("span_stored"), sem("span_back")
        rec_ready, stored = sem("rec_ready"), sem("prep_stored")
        range_ready, range_stored, row_back = sem("range_ready"), sem("range_stored"), sem("row_back")
        link_sem = sem("prep_chain")

        with nc.Block() as block:
            @block.sync
            def _(sp):
                sp.dma_start(rec_in[:], c["rec"].rearrange("(p t) f -> p t f", p=P)).then_inc(loaded, 16)
                sp.dma_start(begin[:], w0["begin"]).then_inc(consts_loaded, 16)
                sp.dma_start(c["ident"][:], w0["ident"]).then_inc(consts_loaded, 16)
                sp.dma_start(c["iota"][:], w0["iota"].to_broadcast([P, GROUP])).then_inc(consts_loaded, 16)
                sp.wait_ge(span_ready, 2)
                sp.dma_start(c["span_d"].rearrange("a (p m) -> p a m", p=REAL_PARTS),
                             span[:]).then_inc(span_stored, 16)
                sp.wait_ge(span_stored, 16)
                sp.dma_start(span_all[:], c["span_d"].rearrange("a (o n) -> o a n", o=1)
                             .to_broadcast([SUB_ROWS, 2, MINIS])).then_inc(span_back, 16)
                sp.wait_ge(rec_ready, 1)
                sp.dma_start(c["rec_d"].rearrange("(p t) f -> p t f", p=P), rec_out[:]).then_inc(stored, 16)
                sp.dma_start(c["key_d"].rearrange("o (p t) -> (o p) t", p=P), key[:]).then_inc(stored, 16)
                sp.wait_ge(range_ready, SUB_COLS)
                with nc.allow_non_contiguous_dma(reason="a few hundred single numbers"):
                    sp.dma_start(c["range_d"].rearrange("a (q p) -> p a q", p=SUB_ROWS),
                                 edge_range[:]).then_inc(range_stored, 16)
                sp.wait_ge(range_stored, 16)
                sp.dma_start(row[:], c["range_d"].rearrange("(o a) n -> o a n", o=1)).then_inc(row_back, 16)
                sp.wait_ge(row_back, 16)
                sp.wait_ge(stored, 32)

            @block.scalar
            def _(act):
                act.wait_ge(clipped, 1)
                act.wait_ge(filled, 1)
                act.activation(cosine[:], clip[:], ACT.Sin, bias=half_pi[:],
                               scale=-float(np.pi) / CUTOFF).then_inc(cosine_ready, 1)

            @block.vector
            def _(dve):
                links = [0]

                def link(ins):
                    ins.then_inc(link_sem, 1)
                    links[0] += 1
                    dve.wait_ge(link_sem, links[0])

                dve.memset(half_pi[:], float(np.pi) / 2).then_inc(filled, 1)
                dve.memset(c["eps"][:], EPS)
                dve.memset(c["one"][:], 1.0)
                dve.memset(c["minus_big"][:], -BIG)
                for table, fill in ((c["lo0"], MINIS), (c["lo1"], MINIS), (c["n0"], 1), (c["n1"], 1)):
                    link(dve.memset(table, fill))
                dve.wait_ge(loaded, 16)
                dst, src, kind = rec_in[:, :, 1], rec_in[:, :, 0], rec_in[:, :, 2]
                weight = rec_in[:, :, 3].bitcast(F32)
                minis = rec_in[0:REAL_PARTS, :, 1].rearrange("p (m e) -> p m e", e=MINI)
                dve.tensor_reduce(span[:, 0, :], minis, AX, ALU.max).then_inc(span_ready, 1)
                dve.tensor_reduce(span[:, 1, :], minis, AX, ALU.min).then_inc(span_ready, 1)
                link(dve.scalar_tensor_tensor(clip[:], weight, -1.0, weight, ALU.mult, ALU.max))
                dve.tensor_scalar(clip[:], clip[:], CUTOFF, None, ALU.min).then_inc(clipped, 1)
                dve.tensor_copy(rec_out[:, :, 0].bitcast(I32), src)
                dve.tensor_copy(rec_out[:, :, 1], dst)
                link(dve.scalar_tensor_tensor(key[:], dst, float(RELS), kind, ALU.mult, ALU.add))
                dve.tensor_copy(rec_out[:, :, 2], key[:])
                dve.wait_ge(cosine_ready, 1)
                link(dve.tensor_scalar(cosine[:], cosine[:], 0.5, 0.5, ALU.mult, ALU.add))
                dve.scalar_tensor_tensor(rec_out[:, :, 3], weight, CUTOFF, cosine[:],
                                         ALU.is_lt, ALU.mult).then_inc(rec_ready, 1)
                dve.wait_ge(consts_loaded, 48)
                link(dve.tensor_scalar(end[:], begin[:], float(SUB), None, ALU.add))
                dve.wait_ge(span_back, 16)
                link(dve.tensor_tensor_scan(reach[:], span_all[:, 0, :], span_all[:, 0, :], -1.0, ALU.max, ALU.max))
                for col in range(SUB_COLS):
                    ins = dve.tensor_scalar(junk[:], reach[:], begin[:, col:col + 1], 0.0, ALU.is_lt, ALU.add,
                                            accum_out=edge_range[:, 0, col:col + 1])
                    link(ins)
                back = span_all[:, 1, ::-1]
                link(dve.tensor_tensor_scan(reach[:], back, back, 1e9, ALU.min, ALU.min))
                for col in range(SUB_COLS):
                    ins = dve.tensor_scalar(junk[:], reach[:], end[:, col:col + 1], 0.0, ALU.is_ge, ALU.add,
                                            accum_out=edge_range[:, 1, col:col + 1])
                    ins.then_inc(range_ready, 1)
                    dve.wait_ge(range_ready, col + 1)
                dve.wait_ge(row_back, 16)
                link(dve.tensor_scalar(hi_f[:], row[:, 1, :], -1.0, float(MINIS), ALU.mult, ALU.add))
                link(dve.tensor_tensor(len_f[:], hi_f[:], lo_f, ALU.subtract))
                dve.tensor_copy(c["lo1"][:, 0:SUBS], lo_f)
                dve.tensor_reduce(lo0_f[:], lo_f.rearrange("o (g j) -> o g j", j=PER_GROUP), AX, ALU.min)
                link(dve.tensor_reduce(hi0_f[:], hi_f[:].rearrange("o (g j) -> o g j", j=PER_GROUP), AX, ALU.max))
                dve.tensor_copy(c["lo0"][:, 0:GROUPS], lo0_f[:])
                link(dve.tensor_tensor(hi0_f[:], hi0_f[:], lo0_f[:], ALU.subtract))
                m0, m1 = CH0 // MINI, CH1 // MINI
                a0, a1 = c["n0"][:, 0:GROUPS], c["n1"][:, 0:SUBS]
                link(dve.tensor_scalar(a0, hi0_f[:], float(m0 - 1), None, ALU.add))
                link(dve.tensor_scalar(a0, a0, m0.bit_length() - 1, None, ALU.arith_shift_right))
                link(dve.tensor_scalar(a0, a0, 1.0, None, ALU.max))
                link(dve.tensor_scalar(a1, len_f[:], float(m1 - 1), 2731.0, ALU.add, ALU.mult))
                link(dve.tensor_scalar(a1, a1, 16, None, ALU.arith_shift_right))
                link(dve.tensor_scalar(a1, a1, 1.0, None, ALU.max))
                dve.tensor_reduce(total[:, 0:1], a0, AX, ALU.add)
                link(dve.tensor_reduce(total[:, 1:2], a1, AX, ALU.add))
                link(dve.tensor_scalar(total_i[:], total[:], float(U - 1), None, ALU.add))
                link(dve.tensor_scalar(total_i[:], total_i[:], U.bit_length() - 1, None, ALU.arith_shift_right))
                dve.tensor_scalar(c["steps0"][:], total_i[:, 0:1], float(-MIN_STEPS), None, ALU.add)
                dve.tensor_scalar(c["steps1"][:], total_i[:, 1:2], float(-MIN_STEPS), None, ALU.add)


def nodes_0(nc, c):
    sem, sems = c["sem"], c["sems"]
    w0 = c["w0"]
    UN = 4
    with ExitStack() as ctx:
        def sb(name, shape, dt=F32):
            return ctx.enter_context(nc.sbuf_tensor(name, shape, dt))

        def ps(name, shape):
            return ctx.enter_context(nc.psum_tensor(name, shape, F32))

        w_qkv = sb("w_qkv", [P, HALF, 3 * D])
        b_qkv = sb("b_qkv", [P, 3 * D])
        b_o = sb("b_o", [P, D])
        gamma_t, beta_t = sb("gamma_t", [P, HALF]), sb("beta_t", [P, HALF])
        xs = [sb(f"xs{k}", [GROUP, D]) for k in range(4)]
        hs = [sb(f"hs{k}", [GROUP, D]) for k in range(4)]
        xhs = [sb(f"xhs{k}", [GROUP, D]) for k in range(4)]
        xn = [sb(f"xn{k}", [GROUP, D]) for k in range(4)]
        xnT = [sb(f"xnT{k}", [P, HALF, GROUP]) for k in range(4)]
        q = [sb(f"q{k}", [GROUP, D]) for k in range(4)]
        q_rest = [sb(f"q_rest{k}", [GROUP, D]) for k in range(4)]
        q_parts = [sb(f"q_parts{k}", [P, Q_ROW], BF16) for k in range(4)]
        kv = [sb(f"kv0{k}", [GROUP, 2 * D]) for k in range(4)]
        stat = [[sb(f"stat{a}{k}", [GROUP, 6]) for k in range(4)] for a in range(2)]
        mv = [[sb(f"mv{a}{k}", [GROUP, 2]) for k in range(4)] for a in range(2)]
        std = [[sb(f"std{a}{k}", [GROUP, 1]) for k in range(4)] for a in range(2)]
        rstd = [[sb(f"rstd{a}{k}", [GROUP, 1]) for k in range(4)] for a in range(2)]
        shift = [[sb(f"shift{a}{k}", [GROUP, 1]) for k in range(4)] for a in range(2)]
        xnT_p = [ps(f"xnT_p{k}", [P, HALF, GROUP]) for k in range(2)]
        q_p = [ps(f"q_p{k}", [GROUP, D]) for k in range(2)]
        kv_p = [ps(f"kv_p{k}", [GROUP, 2 * D]) for k in range(2)]

        w_loaded = sem("w_qkv_loaded")
        x_loaded = sems("x_loaded", UN)
        stat_ready = [sem("stat_x"), sem("stat_h")]
        mean_ready = [sem("mean_x"), sem("mean_h")]
        std_ready = [sem("std_x"), sem("std_h")]
        rstd_ready = [sem("rstd_x"), sem("rstd_h")]
        shift_ready = [sem("shift_x"), sem("shift_h")]
        h_ready, xh_sum, xh_ready, xn_ready = sem("h_ready"), sem("xh_sum"), sem("xh_ready"), sem("xn_ready")
        xnT_turned, xnT_ready = sem("xnT_turned"), sem("xnT_ready")
        qkv_summed, q_ready, kv_ready = sem("qkv0_summed"), sem("q0_ready"), sem("kv0_ready")
        q_filled, q_first, q_left = sem("q0_filled"), sem("q0_first"), sem("q0_left")
        q_second, q_last = sem("q0_second"), sem("q0_last")
        q_stored, kv_stored, xh_stored = sems("q0_stored", UN), sems("kv0_stored", UN), sems("xh_stored", UN)
        held = sem("node0_held")

        with nc.Block() as block:
            @block.sync
            def _(sp):
                for dst, src in ((w_qkv[:], halves(w0["w_qkv"])), (b_qkv[:], w0["b_qkv"].to_broadcast([P, 3 * D])),
                                 (b_o[:], w0["b_o"].to_broadcast([P, D])),
                                 (gamma_t[:], w0["gamma_t"]), (beta_t[:], w0["beta_t"])):
                    sp.dma_start(dst, src).then_inc(w_loaded, 16)

                def load(it):
                    k = it.slot(4)
                    wait(sp, xh_sum, it, 4)
                    sp.dma_start(xs[k][:], c["x"][ds(it.index * GROUP, GROUP), :]).then_inc(x_loaded[k], 16)

                def store_kv(it):
                    k = it.slot(4)
                    wait(sp, kv_ready, it)
                    sp.dma_start(c["kv0_d"][ds(it.index * GROUP, GROUP), :], kv[k][:]).then_inc(kv_stored[k], 16)

                def store_q(it):
                    k = it.slot(4)
                    wait(sp, q_last, it)
                    sp.dma_start(c["q0_d"][ds(it.index * P, P), :], q_parts[k][:]).then_inc(q_stored[k], 16)

                def store_xh(it):
                    k = it.slot(4)
                    wait(sp, xh_ready, it)
                    sp.dma_start(c["xh_d"][ds(it.index * GROUP, GROUP), :], xhs[k][:]).then_inc(xh_stored[k], 16)

                run_stages(sp, GROUPS, ((0, load), (4, store_xh), (7, store_kv), (9, store_q)), UN)
                for k in range(UN):
                    sp.wait_ge(q_stored[k], 16 * len(range(k, GROUPS, UN)))
                    sp.wait_ge(kv_stored[k], 16 * len(range(k, GROUPS, UN)))
                    sp.wait_ge(xh_stored[k], 16 * len(range(k, GROUPS, UN)))

            @block.gpsimd
            def _(pool):
                pool.wait_ge(w_loaded, 80)

                def residual(it):
                    k = it.slot(4)
                    wait(pool, h_ready, it)
                    if not (isinstance(it.i, int) and it.index < UN):
                        pool.wait_ge(xh_stored[k], it.round(0) * 16)
                    pool.tensor_tensor(xhs[k][:], xs[k][:], hs[k][:], ALU.add).then_inc(xh_sum, 1)
                    wait(pool, xh_sum, it)
                    pool.tensor_tensor(xhs[k][:], xhs[k][:], b_o[0:GROUP, :], ALU.add).then_inc(xh_ready, 1)

                def last_part(it):
                    k = it.slot(4)
                    wait(pool, q_second, it)
                    pool.tensor_tensor(q_parts[k][0:GROUP, 2 * D:3 * D], q_rest[k][:], q_parts[k][0:GROUP, D:2 * D],
                                       ALU.subtract).then_inc(q_last, 1)

                run_stages(pool, GROUPS, ((2, residual), (8, last_part)), UN)

            @block.scalar
            def _(act):
                act.wait_ge(w_loaded, 80)

                def root(a):
                    def f(it):
                        k = it.slot(4)
                        wait(act, mean_ready[a], it)
                        wait(act, shift_ready[a], it, 4)
                        act.activation(std[a][k][:], mv[a][k][:, 1:2], ACT.Sqrt,
                                       bias=c["eps"][0:GROUP, :]).then_inc(std_ready[a], 1)
                    return f

                def relu(it):
                    k = it.slot(4)
                    wait(act, shift_ready[0], it)
                    wait(act, xn_ready, it, 4)
                    wait(act, xh_ready, it, 4)
                    act.activation(hs[k][:], xs[k][:], ACT.Relu, bias=shift[0][k][:],
                                   scale=rstd[0][k][:]).then_inc(h_ready, 1)

                def norm(it):
                    k = it.slot(4)
                    wait(act, shift_ready[1], it)
                    wait(act, xnT_turned, it, 4)
                    act.activation(xn[k][:], hs[k][:], ACT.Identity, bias=shift[1][k][:],
                                   scale=rstd[1][k][:]).then_inc(xn_ready, 1)

                def affine(it):
                    k = it.slot(4)
                    wait(act, xnT_turned, it)
                    wait(act, qkv_summed, it, 4)
                    for j in range(HALF):
                        act.activation(xnT[k][:, j, :], xnT_p[k % 2][:, j, :], ACT.Identity, bias=beta_t[:, j:j + 1],
                                       scale=gamma_t[:, j:j + 1]).then_inc(xnT_ready, 1)

                def first_part(it):
                    k = it.slot(4)
                    wait(act, q_ready, it)
                    if not (isinstance(it.i, int) and it.index < UN):
                        act.wait_ge(q_stored[k], it.round(0) * 16)
                    act.copy(q_parts[k][0:GROUP, 0:D], q[k][:]).then_inc(q_first, 1)

                def second_part(it):
                    k = it.slot(4)
                    wait(act, q_left, it)
                    act.copy(q_parts[k][0:GROUP, D:2 * D], q_rest[k][:]).then_inc(q_second, 1)

                run_stages(act, GROUPS, ((3, root(1)), (1, root(0)), (4, affine), (8, second_part), (6, first_part),
                                         (3, norm), (1, relu)), UN)

            @block.vector
            def _(dve):
                def node_of(k):
                    return q_parts[k][:, PARTS * D:Q_ROW].bitcast(F32)

                for k in range(UN):
                    dve.memset(q_parts[k][:], 0.0).then_inc(q_filled, 1)
                dve.wait_ge(q_filled, UN)
                for k in range(UN):
                    dve.memset(node_of(k), float((k - UN) * GROUP)).then_inc(q_filled, 1)
                dve.wait_ge(q_filled, 2 * UN)
                dve.wait_ge(w_loaded, 80)

                def stats(a, src):
                    def f(it):
                        k = it.slot(4)
                        if a == 0:
                            wait_slot(dve, x_loaded, it)
                        else:
                            wait(dve, h_ready, it)
                        dve.bn_stats(stat[a][k][:], src[k][:]).then_inc(stat_ready[a], 1)
                    return f

                def moments(a):
                    def f(it):
                        k = it.slot(4)
                        wait(dve, stat_ready[a], it)
                        dve.sem_inc(held, 1)
                        wait(dve, shift_ready[a], it, 4)
                        dve.sem_inc(held, 1)
                        dve.bn_aggr(mv[a][k][:], stat[a][k][:]).then_inc(mean_ready[a], 1)
                    return f

                def inverse(a):
                    def f(it):
                        k = it.slot(4)
                        wait(dve, std_ready[a], it)
                        wait(dve, h_ready if a == 0 else xn_ready, it, 4)
                        dve.reciprocal(rstd[a][k][:], std[a][k][:]).then_inc(rstd_ready[a], 1)
                    return f

                def offset(a):
                    def f(it):
                        k = it.slot(4)
                        wait(dve, rstd_ready[a], it)
                        dve.scalar_tensor_tensor(shift[a][k][:], mv[a][k][:, 0:1], -1.0, rstd[a][k][:],
                                                 ALU.mult, ALU.mult).then_inc(shift_ready[a], 1)
                    return f

                def bias_q(it):
                    k = it.slot(4)
                    wait(dve, qkv_summed, it)
                    dve.tensor_tensor(q[k][:], q_p[k % 2][:], b_qkv[0:GROUP, 0:D], ALU.add).then_inc(q_ready, 1)

                def bias_kv(it):
                    k = it.slot(4)
                    if not (isinstance(it.i, int) and it.index < UN):
                        dve.wait_ge(kv_stored[k], it.round(0) * 16)
                    dve.tensor_tensor(kv[k][:], kv_p[k % 2][:], b_qkv[0:GROUP, D:3 * D], ALU.add).then_inc(kv_ready, 1)

                def left(it):
                    k = it.slot(4)
                    wait(dve, q_first, it)
                    dve.tensor_scalar(node_of(k), node_of(k), float(UN * GROUP), None, ALU.add)
                    wait(dve, q_last, it, 4)
                    dve.tensor_tensor(q_rest[k][:], q[k][:], q_parts[k][0:GROUP, 0:D], ALU.subtract).then_inc(q_left, 1)

                run_stages(dve, GROUPS, ((0, stats(0, xs)), (2, stats(1, hs)), (6, bias_q), (3, inverse(1)),
                                         (1, inverse(0)), (6, bias_kv), (3, offset(1)), (1, offset(0)),
                                         (0, moments(0)), (2, moments(1)), (7, left)), UN)

            @block.tensor
            def _(pe):
                pe.wait_ge(w_loaded, 80)

                def turn(it):
                    k = it.slot(4)
                    wait(pe, xn_ready, it)
                    wait(pe, xnT_ready, it, 2, per=HALF)
                    for j in range(HALF):
                        ins = pe.transpose(xnT_p[k % 2][:, j, :], xn[k][:, j * P:(j + 1) * P],
                                           c["ident"][0:GROUP, 0:GROUP])
                    ins.then_inc(xnT_turned, 1)

                def project(it):
                    k = it.slot(4)
                    wait(pe, xnT_ready, it, per=HALF)
                    wait(pe, q_ready, it, 2)
                    wait(pe, kv_ready, it, 2)
                    for j in range(HALF):
                        pe.matmul(q_p[k % 2][:], xnT[k][:, j, :], w_qkv[:, j, 0:D], start=j == 0, stop=j == HALF - 1)
                    for j in range(HALF):
                        ins = pe.matmul(kv_p[k % 2][:], xnT[k][:, j, :], w_qkv[:, j, D:3 * D],
                                        start=j == 0, stop=j == HALF - 1)
                    ins.then_inc(qkv_summed, 1)

                run_stages(pe, GROUPS, ((4, turn), (5, project)), UN)


def edges_0(nc, c):
    sem, sems = c["sem"], c["sems"]
    w0 = c["w0"]
    with ExitStack() as ctx:
        def sb(name, shape, dt=F32):
            return ctx.enter_context(nc.sbuf_tensor(name, shape, dt))

        def ps(name, shape):
            return ctx.enter_context(nc.psum_tensor(name, shape, F32))

        LAST = 96
        w_raw = sb("w_edge_raw", [LAST + 1, 2 * D])
        w_lead = sb("w_edge_lead", [P, 2 * D], F32R)
        w_rest = sb("w_edge_rest", [LAST + 1, 2 * D], F32R)
        b_lead = sb("b_edge_lead", [LAST + 1, 2 * D], F32R)
        rec = [sb(f"rec{k}", [P, T0, 4]) for k in range(U)]
        feat = [sb(f"feat{k}", [R, CH0]) for k in range(U)]
        parts = [sb(f"parts{k}", [P, CH0], F32R) for k in range(2)]
        lead = [sb(f"feat_lead{k}", [LAST + 1, CH0], F32R) for k in range(2)]
        ones = sb("edge_ones", [LAST + 1 - R, CH0])
        q_blk = [sb(f"q_blk{k}", [P, Q_ROW], BF16) for k in range(U)]
        keep = [sb(f"keep{k}", [GROUP, 1]) for k in range(U)]
        kv = [sb(f"kv{k}", [P, T0, 2 * D]) for k in range(U)]
        local = [sb(f"local{k}", [P, T0]) for k in range(2)]
        hot = [sb(f"hot{k}", [P, T0, GROUP]) for k in range(4)]
        hotT = [sb(f"hotT{k}", [GROUP, T0, P], BF16) for k in range(2)]
        gates = [sb(f"gates{k}", [P, T0, 2 * D]) for k in range(2)]
        qk = [sb(f"qk{k}", [P, T0, D]) for k in range(2)]
        attn = [sb(f"attn{k}", [P, T0]) for k in range(2)]
        attn_act = [sb(f"attn_act{k}", [P, T0]) for k in range(2)]
        weight = [sb(f"weight{k}", [P, T0]) for k in range(2)]
        msg = [sb(f"msg{k}", [P, T0, D]) for k in range(2)]
        total = [sb(f"total{k}", [GROUP, D]) for k in range(U)]
        gates_p = [ps(f"gates_p{t}", [P, 2 * D]) for t in range(T0)]
        qe_p = ps("qe_p", [P, T0, D])
        hotT_p = ps("hotT_p", [GROUP, T0, P])
        sum_p = ps("sum_p", [GROUP, 2, D])

        w_loaded, filled = sem("w_edge_loaded"), sem("edge0_filled")
        w_lead_ready, w_ready = sem("w_lead_ready"), sem("w_edge_ready")
        lead_ready, parts_ready = sem("feat_lead_ready"), sem("feat_parts_ready")
        loaded, gathered = sems("edge0_loaded", U), sems("kv0_gathered", U)
        local_ready, hot_ready = sem("local_ready"), sem("hot_ready")
        hotT_turned, hotT_ready = sem("hotT_turned"), sem("hotT_ready")
        gates_summed, gates_ready = sem("gates_summed"), sem("gates_ready")
        qe_ready, qk_ready, attn_ready = sem("qe_ready"), sem("qk_ready"), sem("attn_ready")
        attn_act_ready, weight_ready = sem("attn_act_ready"), sem("weight_ready")
        msg_ready, msg_summed, total_ready = sem("msg_ready"), sem("msg_summed"), sem("total_ready")
        stored, held = sem("total_stored"), sem("edge0_held")
        LOADS = 3

        def first_of(s):
            return q_blk[s][:, PARTS * D:Q_ROW].bitcast(F32)

        with nc.Block() as block:
            @block.sync
            def _(sp):
                sp.wait_ge(filled, 1)
                sp.dma_start(w_raw[0:R, :], w0["w_edge"]).then_inc(w_loaded, 16)
                for row in (R, LAST):
                    sp.dma_start(w_raw[row:row + 1, :], w0["b_edge"]).then_inc(w_loaded, 16)
                steps = chunk_steps(sp, c["steps0"])
                blk, k_in, first, n, at, row, done = (
                    sp.alloc_register(name) for name in ("blk", "k_in", "first", "n", "at", "row", "done"))
                used = [sp.alloc_register(f"used{k}") for k in range(U)]
                sp.reg_mov(blk, 0)
                sp.reg_mov(k_in, 0)

                def load(it):
                    k = it.slot(U)
                    b = sp.snap(blk, min_val=0, max_val=GROUPS)
                    sp.reg_load((first, n), c["runs0"][0:1, ds(b, 1), :])
                    sp.reg_mul(at, k_in, CH0 // MINI)
                    sp.reg_add(at, at, first)
                    sp.reg_mul(at, at, MINI)
                    edge = sp.snap(at, min_val=0, max_val=EP - CH0)
                    sp.reg_alu(row, blk, GROUPS - 1, ALU.min)
                    node = sp.snap(row, min_val=0, max_val=GROUPS - 1)
                    wait(sp, total_ready, it, U - 1)
                    sp.sem_inc(held, 1)
                    sp.dma_start(rec[k][:], c["rec_d"][ds(edge, CH0), :].rearrange("(p t) f -> p t f", t=T0)
                                 ).then_inc(loaded[k], 16)
                    sp.dma_start(feat[k][:], c["edge_feat_t"][:, ds(edge, CH0)]).then_inc(loaded[k], 16)
                    sp.dma_start(q_blk[k][:], c["q0_d"][ds(node * P, P), :]).then_inc(loaded[k], 16)
                    if isinstance(it.i, int) and it.index == U:
                        w1 = c["w1"]
                        for dst, src in ((w1["w_o"][:], halves(w0["w_o"])),
                                         (w1["w_kvq1"][:], w0["w_kvq1"].rearrange("(a p) n -> p a n", p=P)),
                                         (w1["a_rel"][:], w0["a_rel"]), (w1["prior"][:], w0["prior"])):
                            sp.dma_start(dst, src).then_inc(c["w1_loaded"], 16)
                    sp.reg_mov(used[k], blk)
                    sp.reg_add(k_in, k_in, 1)
                    sp.reg_alu(done, k_in, n, ALU.is_ge)
                    sp.reg_add(blk, blk, done)
                    sp.reg_alu(blk, blk, GROUPS, ALU.min)
                    sp.reg_alu(done, 1, done, ALU.subtract)
                    sp.reg_mul(k_in, k_in, done)

                def store(it):
                    k = it.slot(U)
                    b = sp.snap(used[k], min_val=0, max_val=GROUPS)
                    wait(sp, total_ready, it)
                    sp.sem_inc(held, 1)
                    wait(sp, stored, it, 1, per=16)
                    sp.sem_inc(held, 1)
                    sp.dma_start(c["agg_d"][ds(b * GROUP, GROUP), :], total[k][:]).then_inc(stored, 16)

                run_chunks(sp, steps, ((0, load), (5, store)))
                sp.wait_ge(stored, Item(steps, -1, U).count(per=16))
                sp.sem_inc(held, 1)
                sp.wait_ge(c["w1_loaded"], 16 * len(c["w1"]))

            @block.gpsimd
            def _(pool):
                steps = chunk_steps(pool, c["steps0"])

                def gather(it):
                    k = it.slot(U)
                    wait_slot(pool, loaded, it, LOADS)
                    pool.sem_inc(held, 1)
                    wait(pool, msg_ready, it, U)
                    pool.sem_inc(held, 1)
                    for t in range(T0):
                        pool.indirect_dma_start(
                            kv[k][:, t, :], None, c["kv0_d"],
                            bass.IndirectOffsetOnAxis(ap=rec[k][:, t, 0:1].bitcast(I32), axis=0)
                        ).then_inc(gathered[k], 16)

                def split_rest(it):
                    k, s = it.slot(2), it.slot(U)
                    wait(pool, lead_ready, it, per=2)
                    pool.sem_inc(held, 1)
                    wait(pool, gates_summed, it, 2, per=T0)
                    pool.sem_inc(held, 1)
                    pool.tensor_tensor(parts[k][R:P, :], feat[s][:], parts[k][0:R, :],
                                       ALU.subtract).then_inc(parts_ready, 1)

                run_chunks(pool, steps, ((1, split_rest), (0, gather)))

            @block.scalar
            def _(act):
                steps = chunk_steps(act, c["steps0"])

                def split_lead(it):
                    k, s = it.slot(2), it.slot(U)
                    wait_slot(act, loaded, it, LOADS)
                    wait(act, gates_summed, it, 2, per=T0)
                    act.copy(parts[k][0:R, :], feat[s][:]).then_inc(lead_ready, 1)
                    act.copy(lead[k][0:R, :], feat[s][:]).then_inc(lead_ready, 1)

                def hot_out(it):
                    k = it.slot(2)
                    wait(act, hotT_turned, it)
                    wait(act, qe_ready, it, 2)
                    act.copy(hotT[k][:], hotT_p[:]).then_inc(hotT_ready, 1)

                def attn_silu(it):
                    k = it.slot(2)
                    wait(act, attn_ready, it)
                    wait(act, weight_ready, it, 2)
                    act.activation(attn_act[k][:], attn[k][:], ACT.Silu).then_inc(attn_act_ready, 1)

                def gates_silu(it):
                    k = it.slot(2)
                    wait(act, msg_ready, it, 2)
                    for t in range(T0):
                        act.wait_ge(gates_summed, it.count(1, T0, t + 1))
                        act.activation(gates[k][:, t, :], gates_p[t][:], ACT.Silu).then_inc(gates_ready, 1)

                run_chunks(act, steps, ((1, hot_out), (0, split_lead), (2, attn_silu), (1, gates_silu)))

            @block.vector
            def _(dve):
                dve.memset(w_raw[R:LAST + 1, :], 0.0).then_inc(filled, 1)
                dve.memset(ones[:], 1.0).then_inc(filled, 1)
                for k in range(U):
                    dve.memset(total[k][:], 0.0).then_inc(filled, 1)
                dve.wait_ge(filled, U + 2)
                for k in range(2):
                    dve.tensor_copy(lead[k][R:LAST + 1, :], ones[:])
                dve.wait_ge(w_loaded, 48)
                dve.tensor_copy(w_lead[0:R, :], w_raw[0:R, :])
                dve.tensor_copy(w_lead[R:P, :], w_raw[0:R, :])
                dve.tensor_copy(b_lead[R:LAST + 1, :], w_raw[R:LAST + 1, :]).then_inc(w_lead_ready, 1)
                dve.wait_ge(w_lead_ready, 1)
                dve.tensor_tensor(w_rest[0:R, :], w_raw[0:R, :], w_lead[0:R, :], ALU.subtract)
                dve.tensor_copy(w_rest[R:LAST, :], b_lead[R:LAST, :])
                dve.tensor_tensor(w_rest[LAST:LAST + 1, :], w_raw[LAST:LAST + 1, :], b_lead[LAST:LAST + 1, :],
                                  ALU.subtract).then_inc(w_ready, 1)
                steps = chunk_steps(dve, c["steps0"])

                def locate(it):
                    k, s = it.slot(2), it.slot(U)
                    wait_slot(dve, loaded, it, LOADS)
                    wait(dve, total_ready, it, U)
                    last = s if isinstance(it.i, int) and it.index == 0 else it.prev().slot(U)
                    dve.tensor_scalar(keep[s][:], first_of(s)[0:GROUP], first_of(last)[0:GROUP], None, ALU.is_equal)
                    wait(dve, hot_ready, it, 2)
                    dve.tensor_scalar(local[k][:], rec[s][:, :, 1], first_of(s), None,
                                      ALU.subtract).then_inc(local_ready, 1)

                def one_hot(it):
                    wait(dve, local_ready, it)
                    wait(dve, msg_summed, it, 4)
                    dve.tensor_tensor(hot[it.slot(4)][:],
                                      c["iota"][:].rearrange("p (o n) -> p o n", o=1).to_broadcast([P, T0, GROUP]),
                                      local[it.slot(2)][:].rearrange("p (t o) -> p t o", o=1).to_broadcast(
                                          [P, T0, GROUP]), ALU.is_equal).then_inc(hot_ready, 1)

                def q_times_k(it):
                    k, s = it.slot(2), it.slot(U)
                    wait(dve, qe_ready, it)
                    wait_slot(dve, gathered, it, T0)
                    dve.tensor_tensor(qk[k][:], qe_p[:], kv[s][:, :, 0:D], ALU.mult).then_inc(qk_ready, 1)

                def scores(it):
                    k = it.slot(2)
                    wait(dve, gates_ready, it, per=T0)
                    dve.sem_inc(held, 1)
                    wait(dve, qk_ready, it)
                    dve.sem_inc(held, 1)
                    for t in range(T0):
                        ins = dve.tensor_tensor_reduce(qk[k][:, t, :], qk[k][:, t, :], gates[k][:, t, 0:D], 1.0, 0.0,
                                                       ALU.mult, ALU.add, attn[k][:, t:t + 1])
                    ins.then_inc(attn_ready, 1)

                def add_total(it):
                    k, s = it.slot(2), it.slot(U)
                    wait(dve, msg_summed, it)
                    wait(dve, stored, it, U, per=16)
                    wait(dve, total_ready, it, 1)
                    dve.scalar_tensor_tensor(total[s][:], total[it.prev().slot(U)][:], keep[s][:],
                                             sum_p[:, k, :], ALU.mult, ALU.add).then_inc(total_ready, 1)

                def weights(it):
                    k, s = it.slot(2), it.slot(U)
                    wait(dve, attn_act_ready, it)
                    dve.tensor_tensor(weight[k][:], attn_act[k][:], rec[s][:, :, 3], ALU.mult).then_inc(weight_ready, 1)

                def messages(it):
                    k, s = it.slot(2), it.slot(U)
                    wait(dve, weight_ready, it)
                    wait(dve, msg_summed, it, 2)
                    for t in range(T0):
                        ins = dve.scalar_tensor_tensor(msg[k][:, t, :], kv[s][:, t, D:2 * D], weight[k][:, t:t + 1],
                                                       gates[k][:, t, D:2 * D], ALU.mult, ALU.mult)
                    ins.then_inc(msg_ready, 1)

                run_chunks(dve, steps, ((2, q_times_k), (0, locate), (2, scores), (0, one_hot), (2, weights),
                                        (3, add_total), (2, messages)))

            @block.tensor
            def _(pe):
                pe.wait_ge(w_ready, 1)
                steps = chunk_steps(pe, c["steps0"])

                def turn(it):
                    wait(pe, hot_ready, it)
                    wait(pe, hotT_ready, it, 1)
                    for t in range(T0):
                        ins = pe.transpose(hotT_p[:, t, :], hot[it.slot(4)][:, t, :], c["ident"][:])
                    ins.then_inc(hotT_turned, 1)

                def edge_gates(it):
                    k = it.slot(2)
                    wait(pe, parts_ready, it)
                    for t in range(T0):
                        if not (isinstance(it.i, int) and it.index == 0):
                            pe.wait_ge(gates_ready, it.count(2, T0, t + 1))
                        pe.matmul(gates_p[t][:], parts[k][:, t::T0], w_lead[:], start=True, stop=False)
                        pe.matmul(gates_p[t][:], lead[k][:, t::T0], w_rest[:], start=False,
                                  stop=True).then_inc(gates_summed, 1)

                def q_of_edges(it):
                    k, s = it.slot(2), it.slot(U)
                    wait(pe, hotT_ready, it)
                    wait(pe, qk_ready, it, 1)
                    for t in range(T0):
                        for j in range(PARTS):
                            ins = pe.matmul(qe_p[:, t, :], hotT[k][:, t, :], q_blk[s][0:GROUP, j * D:(j + 1) * D],
                                            start=j == 0, stop=j == PARTS - 1)
                    ins.then_inc(qe_ready, 1)

                def sum_messages(it):
                    k = it.slot(2)
                    wait(pe, msg_ready, it)
                    wait(pe, total_ready, it, 1)
                    for t in range(T0):
                        ins = pe.matmul(sum_p[:, k, :], hot[it.slot(4)][:, t, :], msg[k][:, t, :],
                                        start=t == 0, stop=t == T0 - 1)
                    ins.then_inc(msg_summed, 1)

                run_chunks(pe, steps, ((3, sum_messages), (1, q_of_edges), (1, edge_gates), (0, turn)))


def nodes_1(nc, c):
    sem, sems = c["sem"], c["sems"]
    w0 = c["w0"]
    UN = 4
    KINDS = TYPES * HALF
    with ExitStack() as ctx:
        def sb(name, shape, dt=F32):
            return ctx.enter_context(nc.sbuf_tensor(name, shape, dt))

        def ps(name, shape):
            return ctx.enter_context(nc.psum_tensor(name, shape, F32))

        w_o, w_raw, a_raw, prior = (c["w1"][name] for name in ("w_o", "w_kvq1", "a_rel", "prior"))
        w_lead, w_rest = sb("w1_lead", [P, KINDS, 3 * D], F32R), sb("w1_rest", [P, KINDS, 3 * D], F32R)
        a_lead, a_rest = sb("a_lead", [P, HALF, RELS, P], F32R), sb("a_rest", [P, HALF, RELS, P], F32R)
        agg = [sb(f"agg{k}", [GROUP, D]) for k in range(4)]
        xh = [sb(f"xh1{k}", [GROUP, D]) for k in range(4)]
        kind_row = [sb(f"kind_row{k}", [P, GROUP], I32) for k in range(4)]
        kind_col = [sb(f"kind_col{k}", [GROUP, 1], I32) for k in range(4)]
        bias = [sb(f"b_kvq{k}", [GROUP, 3 * D]) for k in range(4)]
        of_kind = [sb(f"of_kind{k}", [P, TYPES, GROUP]) for k in range(4)]
        aggT = [sb(f"aggT{k}", [P, HALF, GROUP]) for k in range(2)]
        x1 = [sb(f"x1{k}", [GROUP, D]) for k in range(4)]
        h1 = [sb(f"h1{k}", [GROUP, D]) for k in range(4)]
        stat = [sb(f"stat_h1_{k}", [GROUP, 6]) for k in range(4)]
        mv = [sb(f"mv_h1_{k}", [GROUP, 2]) for k in range(4)]
        std = [sb(f"std_h1_{k}", [GROUP, 1]) for k in range(4)]
        rstd = [sb(f"rstd_h1_{k}", [GROUP, 1]) for k in range(4)]
        shift = [sb(f"shift_h1_{k}", [GROUP, 1]) for k in range(4)]
        hT = [sb(f"hT{k}", [P, TYPES, HALF, GROUP]) for k in range(2)]
        hT_lead = [sb(f"hT_lead{k}", [P, TYPES, HALF, GROUP], F32R) for k in range(2)]
        hT_rest = [sb(f"hT_rest{k}", [P, TYPES, HALF, GROUP], F32R) for k in range(2)]
        kv = [sb(f"kv1{k}", [GROUP, 2 * D]) for k in range(4)]
        q = [sb(f"q1{k}", [GROUP, D]) for k in range(2)]
        qT_lead = [sb(f"qT_lead{k}", [P, HALF, GROUP], F32R) for k in range(2)]
        qT_rest = [sb(f"qT_rest{k}", [P, HALF, GROUP], F32R) for k in range(2)]
        qrel = [sb(f"qrel{k}", [GROUP, RELS, D]) for k in range(2)]
        agg_p = ps("agg_out_p", [P, 2, D])
        hT_p = ps("hT_p", [P, HALF, GROUP])
        kv_p = ps("kv1_p", [GROUP, 2 * D])
        q_p = ps("q1_p", [P, 2, D])
        PAIRS = RELS // 2
        rel_p = [ps(f"rel_p{k}", [GROUP, 2, D]) for k in range(PAIRS)]
        aggT_p = agg_p[:, 0, 0:HALF * GROUP].rearrange("p (a n) -> p a n", a=HALF)
        qT_p = q_p[:, 1, 0:HALF * GROUP].rearrange("p (a n) -> p a n", a=HALF)

        scaled, w_lead_ready, w_ready = sem("a_rel_scaled"), sem("w1_leads"), sem("w1_split")
        loaded, bias_got = sems("node1_loaded", UN), sems("b_kvq_gathered", UN)
        kinds_ready = sem("kinds_ready")
        aggT_turned, aggT_ready, out_summed = sem("aggT_turned"), sem("aggT_ready"), sem("out_summed")
        x1_ready, stat_ready, mean_ready, std_ready = sem("x1_ready"), sem("stat1"), sem("mean1"), sem("std1")
        rstd_ready, shift_ready, h1_ready = sem("rstd1"), sem("shift1"), sem("h1_ready")
        hT_turned, hT_ready, hT_lead_ready, hT_split = sem("hT_turned"), sem("hT_ready"), sem("hT_lead"), sem("hT_split")
        kv_summed, kv_ready, q_summed, q_ready = sem("kv1_summed"), sem("kv1_ready"), sem("q1_summed"), sem("q1_ready")
        qT_turned, qT_lead_ready, qT_split = sem("qT_turned"), sem("qT_lead"), sem("qT_split")
        rel_summed, rel_act, rel_dve = sem("rel_summed"), sem("rel_act"), sem("rel_dve")
        x_stored, kv_stored, rel_stored = sems("x1_stored", UN), sems("kv1_stored", UN), sems("qrel_stored", 2)
        held = sem("node1_held")
        LOADS = 4

        with nc.Block() as block:
            @block.sync
            def _(sp):
                def load(it):
                    k = it.slot(4)
                    rows = ds(it.index * GROUP, GROUP)
                    wait(sp, x1_ready, it, 4)
                    sp.sem_inc(held, 1)
                    wait(sp, kinds_ready, it, 4)
                    sp.sem_inc(held, 1)
                    if not (isinstance(it.i, int) and it.index < UN):
                        sp.wait_ge(bias_got[k], it.round(0) * 16)
                    sp.dma_start(agg[k][:], c["agg_d"][rows, :]).then_inc(loaded[k], 16)
                    sp.dma_start(xh[k][:], c["xh_d"][rows, :]).then_inc(loaded[k], 16)
                    sp.dma_start(kind_row[k][:], c["node_type"][:, rows].to_broadcast([P, GROUP])
                                 ).then_inc(loaded[k], 16)
                    sp.dma_start(kind_col[k][:], c["node_type"].rearrange("o n -> n o")[rows, :]
                                 ).then_inc(loaded[k], 16)

                def store_x(it):
                    k = it.slot(4)
                    rows = ds(it.index * GROUP, GROUP)
                    wait(sp, h1_ready, it)
                    sp.dma_start(c["x1_d"][rows, :], x1[k][:]).then_inc(x_stored[k], 16)
                    sp.dma_start(c["h1_d"][rows, :], h1[k][:]).then_inc(x_stored[k], 16)

                def store_kv(it):
                    k = it.slot(4)
                    wait(sp, kv_ready, it)
                    sp.dma_start(c["kv1_d"][ds(it.index * GROUP, GROUP), :], kv[k][:]).then_inc(kv_stored[k], 16)

                def store_rel(it):
                    k = it.slot(2)
                    wait(sp, rel_act, it)
                    sp.sem_inc(held, 1)
                    wait(sp, rel_dve, it)
                    sp.dma_start(c["qrel_d"].rearrange("(n r) d -> n (r d)", r=RELS)[ds(it.index * GROUP, GROUP), :],
                                 qrel[k][:].rearrange("n r d -> n (r d)")).then_inc(rel_stored[k], 16)

                run_stages(sp, GROUPS, ((0, load), (5, store_x), (6, store_kv), (8, store_rel)), UN)
                for k in range(UN):
                    sp.wait_ge(x_stored[k], 32 * len(range(k, GROUPS, UN)))
                    sp.wait_ge(kv_stored[k], 16 * len(range(k, GROUPS, UN)))
                for k in range(2):
                    sp.wait_ge(rel_stored[k], 16 * len(range(k, GROUPS, 2)))

            @block.gpsimd
            def _(pool):
                def gather(it):
                    k = it.slot(4)
                    wait_slot(pool, loaded, it, LOADS)
                    pool.sem_inc(held, 1)
                    wait(pool, q_ready, it, 4)
                    pool.sem_inc(held, 1)
                    pool.indirect_dma_start(bias[k][:], None, w0["b_kvq1"],
                                            bass.IndirectOffsetOnAxis(ap=kind_col[k][:], axis=0)
                                            ).then_inc(bias_got[k], 16)

                run_stages(pool, GROUPS, ((1, gather),), UN)

            @block.scalar
            def _(act):
                act.copy(w_lead[:], w_raw[:]).then_inc(w_lead_ready, 1)
                act.wait_ge(scaled, RELS * HALF)
                act.copy(a_lead[:], a_raw[:]).then_inc(w_lead_ready, 1)

                def agg_out(it):
                    k = it.slot(2)
                    wait(act, aggT_turned, it)
                    wait(act, out_summed, it, 2)
                    act.copy(aggT[k][:], aggT_p).then_inc(aggT_ready, 1)

                def root(it):
                    k = it.slot(4)
                    wait(act, mean_ready, it)
                    wait(act, shift_ready, it, 4)
                    act.activation(std[k][:], mv[k][:, 1:2], ACT.Sqrt, bias=c["eps"][0:GROUP, :]).then_inc(std_ready, 1)

                def relu(it):
                    k = it.slot(4)
                    wait(act, shift_ready, it)
                    if not (isinstance(it.i, int) and it.index < UN):
                        act.wait_ge(x_stored[k], it.round(0) * 32)
                    wait(act, hT_turned, it, 4)
                    act.activation(h1[k][:], x1[k][:], ACT.Relu, bias=shift[k][:], scale=rstd[k][:]).then_inc(h1_ready, 1)

                def h_lead(it):
                    k = it.slot(2)
                    wait(act, hT_ready, it)
                    wait(act, q_summed, it, 2)
                    act.copy(hT_lead[k][:], hT[k][:]).then_inc(hT_lead_ready, 1)

                def q_lead(it):
                    k = it.slot(2)
                    wait(act, qT_turned, it)
                    wait(act, rel_summed, it, 2)
                    act.copy(qT_lead[k][:], qT_p).then_inc(qT_lead_ready, 1)

                def rel_out(it):
                    k = it.slot(2)
                    wait(act, rel_summed, it)
                    if not (isinstance(it.i, int) and it.index < 2):
                        wait_pair(act, rel_stored, it)
                    for pair in range(1, PAIRS):
                        ins = act.copy(qrel[k][:, 2 * pair:2 * pair + 2, :], rel_p[pair][:])
                    ins.then_inc(rel_act, 1)

                run_stages(act, GROUPS, ((6, q_lead), (2, root), (3, relu), (4, h_lead), (1, agg_out), (7, rel_out)), UN)

            @block.vector
            def _(dve):
                for r in range(RELS):
                    for a in range(HALF):
                        dve.tensor_scalar(a_raw[:, a, r, :], a_raw[:, a, r, :], prior[:, a, r:r + 1], DK ** -0.5,
                                          ALU.mult, ALU.mult).then_inc(scaled, 1)
                dve.wait_ge(w_lead_ready, 1)
                dve.tensor_tensor(w_rest[:], w_raw[:], w_lead[:], ALU.subtract).then_inc(w_ready, 1)
                dve.wait_ge(scaled, RELS * HALF)
                dve.wait_ge(w_lead_ready, 2)
                dve.tensor_tensor(a_rest[:], a_raw[:], a_lead[:], ALU.subtract).then_inc(w_ready, 1)

                def kinds(it):
                    k = it.slot(4)
                    wait_slot(dve, loaded, it, LOADS)
                    wait(dve, hT_ready, it, 4)
                    for t in range(TYPES):
                        ins = dve.tensor_scalar(of_kind[k][:, t, :], kind_row[k][:], float(t), None, ALU.is_equal)
                    ins.then_inc(kinds_ready, 1)

                def residual(it):
                    k = it.slot(4)
                    wait(dve, out_summed, it)
                    if not (isinstance(it.i, int) and it.index < UN):
                        dve.wait_ge(x_stored[k], it.round(0) * 32)
                    dve.tensor_tensor(x1[k][:], agg_p[0:GROUP, 1, :], xh[k][:], ALU.add).then_inc(x1_ready, 1)
                    wait(dve, x1_ready, it)
                    dve.bn_stats(stat[k][:], x1[k][:]).then_inc(stat_ready, 1)
                    wait(dve, stat_ready, it)
                    dve.sem_inc(held, 1)
                    wait(dve, shift_ready, it, 4)
                    dve.sem_inc(held, 1)
                    dve.bn_aggr(mv[k][:], stat[k][:]).then_inc(mean_ready, 1)

                def scale(it):
                    k = it.slot(4)
                    wait(dve, std_ready, it)
                    wait(dve, h1_ready, it, 4)
                    dve.reciprocal(rstd[k][:], std[k][:]).then_inc(rstd_ready, 1)
                    wait(dve, rstd_ready, it)
                    dve.scalar_tensor_tensor(shift[k][:], mv[k][:, 0:1], -1.0, rstd[k][:],
                                             ALU.mult, ALU.mult).then_inc(shift_ready, 1)

                def split_kinds(it):
                    k = it.slot(2)
                    wait(dve, hT_turned, it)
                    wait(dve, kinds_ready, it)
                    wait(dve, hT_split, it, 2)
                    for t in range(TYPES):
                        ins = dve.tensor_tensor(hT[k][:, t], hT_p[:], of_kind[it.slot(4)][:, t:t + 1, :].to_broadcast(
                            [P, HALF, GROUP]), ALU.mult)
                    ins.then_inc(hT_ready, 1)

                def h_rest(it):
                    k = it.slot(2)
                    wait(dve, hT_lead_ready, it)
                    wait(dve, q_summed, it, 2)
                    dve.tensor_tensor(hT_rest[k][:], hT[k][:], hT_lead[k][:], ALU.subtract).then_inc(hT_split, 1)

                def kvq_out(it):
                    k = it.slot(4)
                    wait(dve, kv_summed, it)
                    wait_slot(dve, bias_got, it)
                    if not (isinstance(it.i, int) and it.index < UN):
                        dve.wait_ge(kv_stored[k], it.round(0) * 16)
                    dve.tensor_tensor(kv[k][:], kv_p[:], bias[k][:, 0:2 * D], ALU.add).then_inc(kv_ready, 1)
                    wait(dve, q_summed, it)
                    wait(dve, qT_turned, it, 2)
                    dve.tensor_tensor(q[it.slot(2)][:], q_p[0:GROUP, 0, :], bias[k][:, 2 * D:3 * D],
                                      ALU.add).then_inc(q_ready, 1)

                def q_rest(it):
                    k = it.slot(2)
                    wait(dve, qT_lead_ready, it)
                    wait(dve, rel_summed, it, 2)
                    dve.tensor_tensor(qT_rest[k][:], qT_p, qT_lead[k][:], ALU.subtract).then_inc(qT_split, 1)

                def rel_out(it):
                    k = it.slot(2)
                    wait(dve, rel_summed, it)
                    if not (isinstance(it.i, int) and it.index < 2):
                        wait_pair(dve, rel_stored, it)
                    dve.tensor_copy(qrel[k][:, 0:2, :], rel_p[0][:]).then_inc(rel_dve, 1)

                run_stages(dve, GROUPS, ((6, q_rest), (2, residual), (1, kinds), (3, scale), (4, split_kinds),
                                         (4, h_rest), (5, kvq_out), (7, rel_out)), UN)

            @block.tensor
            def _(pe):
                def turn_agg(it):
                    k = it.slot(4)
                    wait_slot(pe, loaded, it, LOADS)
                    wait(pe, x1_ready, it, 1)
                    for j in range(HALF):
                        ins = pe.transpose(aggT_p[:, j, :], agg[k][:, j * P:(j + 1) * P], c["ident"][0:GROUP, 0:GROUP])
                    ins.then_inc(aggT_turned, 1)

                def out_project(it):
                    k = it.slot(2)
                    wait(pe, aggT_ready, it)
                    for j in range(HALF):
                        ins = pe.matmul(agg_p[0:GROUP, 1, :], aggT[k][:, j, :], w_o[:, j, :],
                                        start=j == 0, stop=j == HALF - 1)
                    ins.then_inc(out_summed, 1)

                def turn_h(it):
                    k = it.slot(4)
                    wait(pe, h1_ready, it)
                    wait(pe, hT_ready, it, 1)
                    for j in range(HALF):
                        ins = pe.transpose(hT_p[:, j, :], h1[k][:, j * P:(j + 1) * P], c["ident"][0:GROUP, 0:GROUP])
                    ins.then_inc(hT_turned, 1)

                def project(it):
                    k = it.slot(2)
                    wait(pe, hT_split, it)
                    if isinstance(it.i, int) and it.index == 0:
                        pe.wait_ge(w_ready, 2)

                    def sum_parts(dst, cols):
                        for a in range(KINDS):
                            lead, rest = (x[k][:, a // HALF, a % HALF, :] for x in (hT_lead, hT_rest))
                            pe.matmul(dst, lead, w_lead[:, a, cols], start=a == 0, stop=False)
                            pe.matmul(dst, lead, w_rest[:, a, cols], start=False, stop=False)
                            ins = pe.matmul(dst, rest, w_lead[:, a, cols], start=False, stop=a == KINDS - 1)
                        return ins

                    wait(pe, kv_ready, it, 1)
                    sum_parts(kv_p[:], slice(0, 2 * D)).then_inc(kv_summed, 1)
                    wait(pe, qT_split, it, 1)
                    sum_parts(q_p[0:GROUP, 0, :], slice(2 * D, 3 * D)).then_inc(q_summed, 1)

                def turn_q(it):
                    wait(pe, q_ready, it)
                    for j in range(HALF):
                        ins = pe.transpose(qT_p[:, j, :], q[it.slot(2)][:, j * P:(j + 1) * P],
                                           c["ident"][0:GROUP, 0:GROUP])
                    ins.then_inc(qT_turned, 1)

                def relate(it):
                    k = it.slot(2)
                    wait(pe, qT_split, it)
                    wait(pe, rel_act, it, 1)
                    wait(pe, rel_dve, it, 1)
                    for pair in range(PAIRS):
                        rels = slice(2 * pair, 2 * pair + 2)
                        for a in range(HALF):
                            dst = rel_p[pair][:, :, a * P:(a + 1) * P]
                            pe.matmul(dst, qT_lead[k][:, a, :], a_lead[:, a, rels, :], start=True, stop=False)
                            pe.matmul(dst, qT_lead[k][:, a, :], a_rest[:, a, rels, :], start=False, stop=False)
                            ins = pe.matmul(dst, qT_rest[k][:, a, :], a_lead[:, a, rels, :], start=False, stop=True)
                    ins.then_inc(rel_summed, 1)

                run_stages(pe, GROUPS, ((6, turn_q), (2, out_project), (4, turn_h), (5, project), (1, turn_agg),
                                        (7, relate)), UN)


def edges_1(nc, c):
    sem, sems = c["sem"], c["sems"]
    w0 = c["w0"]
    with ExitStack() as ctx:
        def sb(name, shape, dt=F32):
            return ctx.enter_context(nc.sbuf_tensor(name, shape, dt))

        def ps(name, shape, dt=F32):
            return ctx.enter_context(nc.psum_tensor(name, shape, dt))

        spread_head = sb("spread_head", [HEADS * PARTS, HEADS, SEG], BF16)
        identity = sb("ident_bf16", [P, P], BF16)
        rec = [sb(f"rec1{k}", [P, T1, 4]) for k in range(U)]
        key = [sb(f"key{k}", [SEG, CH1]) for k in range(U)]
        qrel = [sb(f"qrel1{k}", [SEG, D]) for k in range(U)]
        par = [sb(f"par1{k}", [P, 3]) for k in range(U)]
        kv = [sb(f"kv1c{k}", [P, T1, 2 * D]) for k in range(U)]
        dist = [sb(f"dist{k}", [SEG, CH1]) for k in range(2)]
        mask = [sb(f"mask{k}", [SEG, CH1]) for k in range(4)]
        local = [sb(f"local1{k}", [P, T1]) for k in range(2)]
        hot = [sb(f"hot1{k}", [P, T1, SEG]) for k in range(U)]
        hotT = [sb(f"hotT1{k}", [SEG, CH1]) for k in range(4)]
        qk = [sb(f"qk1{k}", [P, T1, HEADS, DK]) for k in range(2)]
        score = [sb(f"score{k}", [P, T1, HEADS]) for k in range(4)]
        rest = [[sb(f"score_rest{k}{j}", [P, T1, HEADS]) for j in range(PARTS - 1)] for k in range(2)]
        parts = [sb(f"score_parts{k}", [P, T1, PARTS, HEADS], BF16) for k in range(2)]
        partsT = [sb(f"score_partsT{k}", [PARTS * HEADS, CH1], BF16) for k in range(2)]
        junk = [sb(f"masked_scores{k}", [SEG, HEADS, CH1]) for k in range(2)]
        top = [sb(f"top{k}", [SEG, HEADS]) for k in range(U)]
        old = [sb(f"old{k}", [SEG, HEADS]) for k in range(U)]
        peak = [sb(f"peak{k}", [SEG, HEADS]) for k in range(U)]
        drop = [sb(f"drop{k}", [SEG, HEADS]) for k in range(U)]
        fade = [sb(f"fade{k}", [SEG, HEADS]) for k in range(U)]
        diff = [sb(f"diff{k}", [P, T1, HEADS]) for k in range(2)]
        capped = [sb(f"capped{k}", [P, T1, HEADS]) for k in range(2)]
        wv = [sb(f"wv{k}", [P, T1, HEADS, DK + 1]) for k in range(2)]
        faded = [sb(f"faded{k}", [SEG, HEADS, DK + 1]) for k in range(2)]
        acc = [sb(f"acc{k}", [SEG, HEADS, DK + 1]) for k in range(U)]
        qe_p = ps("qe1_p", [P, 4, D])
        score_p = ps("score_p", [SEG, HEADS, CH1])
        partsT_p = ps("partsT_p", [PARTS * HEADS, CH1], BF16)
        peak_p = ps("peak_p", [P, T1, HEADS])
        sum_p = ps("sum1_p", [SEG, HEADS, DK + 1])

        const_loaded, filled = sem("edge1_consts"), sem("edge1_filled")
        loaded, gathered = sems("edge1_loaded", U), sems("kv1_gathered", U)
        dist_ready, mask_ready, local_ready, hot_ready, hotT_ready = sem("dist1"), sem("mask1"), sem("local1"), sem("hot1"), sem("hotT1")
        qe_ready, qk_ready, score_ready = sem("qe1"), sem("qk1"), sem("score1")
        split_ready = sem("score_split")
        partsT_turned, partsT_ready, spread_ready = sem("partsT_turned"), sem("partsT_ready"), sem("score_spread")
        top_ready, old_ready, peak_ready, drop_ready = sem("top_ready"), sem("old_ready"), sem("peak_ready"), sem("drop_ready")
        of_edge_ready, diff_ready, capped_ready = sem("peak_of_edge"), sem("diff_ready"), sem("capped_ready")
        weight_ready, fade_ready, wv_ready = sem("weight1"), sem("fade_ready"), sem("wv_ready")
        summed, faded_ready, acc_ready = sem("wv_summed"), sem("faded_ready"), sem("acc_ready")
        stored, held = sem("acc_stored"), sem("edge1_held")
        LOADS = 4

        with nc.Block() as block:
            @block.sync
            def _(sp):
                sp.dma_start(spread_head[:], w0["spread_head"]).then_inc(const_loaded, 16)
                steps = chunk_steps(sp, c["steps1"])
                blk, k_in, first, n, at, row, later, done = (sp.alloc_register(name + "1") for name in (
                    "blk", "k_in", "first", "n", "at", "row", "later", "done"))
                used = [sp.alloc_register(f"used1{k}") for k in range(U)]
                sp.reg_mov(blk, 0)
                sp.reg_mov(k_in, 0)

                def load(it):
                    k = it.slot(U)
                    b = sp.snap(blk, min_val=0, max_val=SUBS)
                    sp.reg_load((first, n), c["runs1"][0:1, ds(b, 1), :])
                    sp.reg_mul(at, k_in, CH1 // MINI)
                    sp.reg_add(at, at, first)
                    sp.reg_mul(at, at, MINI)
                    edge = sp.snap(at, min_val=0, max_val=EP - CH1)
                    sp.reg_alu(row, blk, SUBS - 1, ALU.min)
                    sub = sp.snap(row, min_val=0, max_val=SUBS - 1)
                    sp.reg_alu(later, k_in, 1, ALU.min)
                    flag = sp.snap(later, min_val=0, max_val=1)
                    wait(sp, acc_ready, it, U)
                    sp.sem_inc(held, 1)
                    sp.dma_start(rec[k][:], c["rec_d"][ds(edge, CH1), :].rearrange("(p t) f -> p t f", t=T1)
                                 ).then_inc(loaded[k], 16)
                    sp.dma_start(qrel[k][:], c["qrel_d"][ds(sub * SEG, SEG), :]).then_inc(loaded[k], 16)
                    sp.dma_start(key[k][:], c["key_d"][:, ds(edge, CH1)].to_broadcast([SEG, CH1])
                                 ).then_inc(loaded[k], 16)
                    sp.dma_start(par[k][:], w0["par1"][ds(flag * P, P), ds(sub * 3, 3)]).then_inc(loaded[k], 16)
                    sp.reg_mov(used[k], blk)
                    sp.reg_add(k_in, k_in, 1)
                    sp.reg_alu(done, k_in, n, ALU.is_ge)
                    sp.reg_add(blk, blk, done)
                    sp.reg_alu(blk, blk, SUBS, ALU.min)
                    sp.reg_alu(done, 1, done, ALU.subtract)
                    sp.reg_mul(k_in, k_in, done)

                def store(it):
                    k = it.slot(U)
                    b = sp.snap(used[k], min_val=0, max_val=SUBS)
                    wait(sp, acc_ready, it)
                    sp.sem_inc(held, 1)
                    wait(sp, stored, it, 1, per=16)
                    sp.sem_inc(held, 1)
                    sp.dma_start(c["acc_d"][ds(b * SEG, SEG), :], acc[k][:].rearrange("s h e -> s (h e)")
                                 ).then_inc(stored, 16)

                run_chunks(sp, steps, ((0, load), (6, store)))
                sp.wait_ge(stored, Item(steps, -1, U).count(per=16))
                sp.sem_inc(held, 1)

            @block.gpsimd
            def _(pool):
                pool.wait_ge(filled, U + 1)
                steps = chunk_steps(pool, c["steps1"])

                def one_hot(it):
                    hold(pool, held, local_ready, it.count())
                    wait(pool, summed, it, U)
                    pool.sem_inc(held, 1)
                    for t in range(T1):
                        ins = pool.tensor_scalar(hot[it.slot(U)][:, t, :], c["iota"][:],
                                                 local[it.slot(2)][:, t:t + 1], None, ALU.is_equal)
                    ins.then_inc(hot_ready, 1)

                def gather(it):
                    k = it.slot(U)
                    wait_slot(pool, loaded, it, LOADS)
                    pool.sem_inc(held, 1)
                    wait(pool, wv_ready, it, U)
                    pool.sem_inc(held, 1)
                    for t in range(T1):
                        pool.indirect_dma_start(
                            kv[k][:, t, :], None, c["kv1_d"],
                            bass.IndirectOffsetOnAxis(ap=rec[k][:, t, 0:1].bitcast(I32), axis=0)
                        ).then_inc(gathered[k], 16)

                def fade_acc(it):
                    s, last = it.slot(U), it.prev().slot(U)
                    hold(pool, held, fade_ready, it.count())
                    wait(pool, acc_ready, it, 1)
                    pool.sem_inc(held, 1)
                    pool.tensor_tensor(faded[it.slot(2)][:], acc[last][:], fade[s][:].rearrange(
                        "s (h o) -> s h o", o=1).to_broadcast([SEG, HEADS, DK + 1]), ALU.mult).then_inc(faded_ready, 1)

                run_chunks(pool, steps, ((5, fade_acc), (1, one_hot), (0, gather)))

            @block.scalar
            def _(act):
                steps = chunk_steps(act, c["steps1"])

                def distances(it):
                    s = it.slot(U)
                    wait_slot(act, loaded, it, LOADS)
                    wait(act, hotT_ready, it, 2)
                    act.activation(dist[it.slot(2)][:].rearrange("s (t p) -> s t p", p=P),
                                   key[s][:].rearrange("s (p t) -> s t p", t=T1), ACT.Abs,
                                   bias=par[s][0:SEG, 0:1]).then_inc(dist_ready, 1)

                def transposed_hot(it):
                    wait(act, dist_ready, it)
                    wait(act, of_edge_ready, it, 4)
                    wait(act, mask_ready, it, 4)
                    act.activation(hotT[it.slot(4)][:], dist[it.slot(2)][:], ACT.Relu, bias=c["one"][0:SEG, :],
                                   scale=-1.0).then_inc(hotT_ready, 1)

                def masks(it):
                    k = it.slot(4)
                    wait(act, hotT_ready, it)
                    wait(act, top_ready, it, 4, per=HEADS)
                    act.activation(mask[k][:], hotT[k][:], ACT.Identity, bias=c["minus_big"][0:SEG, :],
                                   scale=BIG).then_inc(mask_ready, 1)

                def weights(it):
                    k, s = it.slot(2), it.slot(U)
                    wait(act, capped_ready, it)
                    wait(act, summed, it, 2)
                    act.activation(wv[k][:, :, :, DK], capped[k][:], ACT.Exp).then_inc(weight_ready, 1)
                    wait(act, drop_ready, it)
                    wait(act, faded_ready, it, U)
                    act.activation(fade[s][:], drop[s][:], ACT.Exp).then_inc(fade_ready, 1)
                    wait(act, weight_ready, it)
                    wait_slot(act, gathered, it, T1)
                    for t in range(T1):
                        for h in range(HEADS):
                            ins = act.activation(wv[k][:, t, h, 0:DK], kv[s][:, t, D + h * DK:D + (h + 1) * DK],
                                                 ACT.Copy, scale=wv[k][:, t, h, DK:DK + 1])
                    ins.then_inc(wv_ready, 1)

                def partsT_out(it):
                    wait(act, partsT_turned, it)
                    wait(act, spread_ready, it, 2)
                    act.copy(partsT[it.slot(2)][:], partsT_p[:]).then_inc(partsT_ready, 1)

                run_chunks(act, steps, ((1, transposed_hot), (2, masks), (0, distances), (4, weights), (2, partsT_out)))

            @block.vector
            def _(dve):
                for k in range(U):
                    dve.memset(peak[k][:], 0.0)
                    dve.memset(acc[k][:], 0.0).then_inc(filled, 1)
                dve.tensor_copy(identity[:], c["ident"][:]).then_inc(filled, 1)
                dve.wait_ge(filled, U + 1)
                steps = chunk_steps(dve, c["steps1"])

                def locate(it):
                    s = it.slot(U)
                    wait_slot(dve, loaded, it, LOADS)
                    wait(dve, hot_ready, it, 2)
                    dve.tensor_scalar(local[it.slot(2)][:], rec[s][:, :, 2], par[s][:, 1:2], None,
                                      ALU.subtract).then_inc(local_ready, 1)

                def q_times_k(it):
                    k, s = it.slot(2), it.slot(U)
                    wait(dve, qe_ready, it)
                    wait_slot(dve, gathered, it, T1)
                    wait(dve, score_ready, it, 2)
                    dve.tensor_tensor(qk[k][:].rearrange("p t h e -> p t (h e)"), qe_p[:, 0:T1, :], kv[s][:, :, 0:D],
                                      ALU.mult).then_inc(qk_ready, 1)

                def scores(it):
                    wait(dve, qk_ready, it)
                    wait(dve, diff_ready, it, 4)
                    dve.tensor_reduce(score[it.slot(4)][:], qk[it.slot(2)][:], AX, ALU.add).then_inc(score_ready, 1)

                def lead_part(j):
                    def f(it):
                        k = it.slot(2)
                        if j == 0:
                            wait(dve, score_ready, it)
                            wait(dve, partsT_turned, it, 2)
                        else:
                            dve.wait_ge(split_ready, it.count(1, 4, 2 * j))
                        src = score[it.slot(4)] if j == 0 else rest[k][j - 1]
                        dve.tensor_copy(parts[k][:, :, j, :], src[:]).then_inc(split_ready, 1)
                    return f

                def rest_part(j):
                    def f(it):
                        k = it.slot(2)
                        dve.wait_ge(split_ready, it.count(1, 4, 2 * j + 1))
                        src = score[it.slot(4)] if j == 0 else rest[k][j - 1]
                        if j == 0:
                            dve.tensor_tensor(rest[k][0][:], src[:], parts[k][:, :, j, :],
                                              ALU.subtract).then_inc(split_ready, 1)
                        else:
                            dve.tensor_tensor(parts[k][:, :, j + 1, :], src[:], parts[k][:, :, j, :],
                                              ALU.subtract).then_inc(split_ready, 1)
                    return f

                def maxima(h):
                    def f(it):
                        k, s = it.slot(2), it.slot(U)
                        if h == 0:
                            wait(dve, spread_ready, it)
                            dve.sem_inc(held, 1)
                            wait(dve, mask_ready, it)
                            dve.sem_inc(held, 1)
                            wait(dve, top_ready, it, 2, per=HEADS)
                            dve.sem_inc(held, 1)
                            wait(dve, peak_ready, it, U)
                            dve.sem_inc(held, 1)
                        dve.tensor_tensor_reduce(junk[k][:, h, :], score_p[:, h, :], mask[it.slot(4)][:], 1.0, -BIG,
                                                 ALU.add, ALU.max, top[s][:, h:h + 1]).then_inc(top_ready, 1)
                    return f

                def old_peak(it):
                    s = it.slot(U)
                    wait(dve, drop_ready, it, U)
                    wait(dve, peak_ready, it, 1)
                    dve.tensor_scalar(old[s][:], peak[it.prev().slot(U)][:], par[s][0:SEG, 2:3], None,
                                      ALU.add).then_inc(old_ready, 1)

                def new_peak(it):
                    s = it.slot(U)
                    wait(dve, old_ready, it)
                    wait(dve, top_ready, it, per=HEADS)
                    wait(dve, of_edge_ready, it, U)
                    dve.scalar_tensor_tensor(peak[s][:], top[s][:], FLOOR, old[s][:], ALU.max,
                                             ALU.max).then_inc(peak_ready, 1)

                def peak_drop(it):
                    s = it.slot(U)
                    wait(dve, peak_ready, it)
                    wait(dve, fade_ready, it, U)
                    dve.tensor_tensor(drop[s][:], old[s][:], peak[s][:], ALU.subtract).then_inc(drop_ready, 1)

                def below_peak(it):
                    wait(dve, of_edge_ready, it)
                    wait(dve, capped_ready, it, 2)
                    dve.tensor_tensor(diff[it.slot(2)][:], score[it.slot(4)][:], peak_p[:],
                                      ALU.subtract).then_inc(diff_ready, 1)

                def cap(it):
                    wait(dve, diff_ready, it)
                    wait(dve, weight_ready, it, 2)
                    dve.tensor_scalar(capped[it.slot(2)][:], diff[it.slot(2)][:], 0.0, None,
                                      ALU.min).then_inc(capped_ready, 1)

                def add_acc(it):
                    wait(dve, summed, it)
                    wait(dve, faded_ready, it)
                    wait(dve, stored, it, U, per=16)
                    dve.tensor_tensor(acc[it.slot(U)][:], faded[it.slot(2)][:], sum_p[:], ALU.add).then_inc(acc_ready, 1)

                run_chunks(dve, steps, ((2, q_times_k), (4, below_peak), (2, scores), (4, cap), (0, locate),
                                        (3, maxima(0)), (2, lead_part(0)), (3, maxima(1)), (2, rest_part(0)),
                                        (3, maxima(2)), (2, lead_part(1)), (3, maxima(3)), (2, rest_part(1)),
                                        (3, old_peak), (5, add_acc), (3, new_peak), (3, peak_drop)))

            @block.tensor
            def _(pe):
                pe.wait_ge(const_loaded, 16)
                pe.wait_ge(filled, U + 1)
                steps = chunk_steps(pe, c["steps1"])

                def q_of_edges(it):
                    k, s = it.slot(4), it.slot(U)
                    wait(pe, hotT_ready, it)
                    wait(pe, qk_ready, it, 1)
                    for t in range(T1):
                        ins = pe.matmul(qe_p[:, t, :], hotT[k][:, t * P:(t + 1) * P], qrel[s][:], start=True, stop=True)
                    ins.then_inc(qe_ready, 1)

                def turn_parts(it):
                    k = it.slot(2)
                    wait(pe, split_ready, it, per=4)
                    wait(pe, partsT_ready, it, 1)
                    for t in range(T1):
                        ins = pe.transpose(partsT_p[:, t * P:(t + 1) * P],
                                           parts[k][:, t].rearrange("p j h -> p (j h)"), identity[:])
                    ins.then_inc(partsT_turned, 1)

                def spread(it):
                    k = it.slot(2)
                    wait(pe, partsT_ready, it)
                    wait(pe, top_ready, it, 1, per=HEADS)
                    for h in range(HEADS):
                        for t in range(T1):
                            cols = slice(t * P, (t + 1) * P)
                            ins = pe.matmul(score_p[:, h, cols], spread_head[:, h, :], partsT[k][:, cols],
                                            start=True, stop=True)
                    ins.then_inc(spread_ready, 1)

                def peaks_of_edges(it):
                    k = it.slot(4)
                    wait(pe, peak_ready, it)
                    wait(pe, diff_ready, it, 1)
                    for t in range(T1):
                        ins = pe.matmul(peak_p[:, t, :], hotT[k][:, t * P:(t + 1) * P], peak[it.slot(U)][:],
                                        start=True, stop=True)
                    ins.then_inc(of_edge_ready, 1)

                def sum_values(it):
                    k, s = it.slot(2), it.slot(U)
                    wait(pe, wv_ready, it)
                    wait(pe, hot_ready, it)
                    wait(pe, acc_ready, it, 1)
                    for t in range(T1):
                        ins = pe.matmul(sum_p[:], hot[s][:, t, :], wv[k][:, t].rearrange("p h e -> p (h e)"),
                                        start=t == 0, stop=t == T1 - 1)
                    ins.then_inc(summed, 1)

                run_chunks(pe, steps, ((5, sum_values), (1, q_of_edges), (2, turn_parts), (3, peaks_of_edges),
                                       (2, spread)))


def nodes_out(nc, c):
    sem, sems = c["sem"], c["sems"]
    w0 = c["w0"]
    UN = 8
    with ExitStack() as ctx:
        def sb(name, shape, dt=F32):
            return ctx.enter_context(nc.sbuf_tensor(name, shape, dt))

        def ps(name, shape):
            return ctx.enter_context(nc.psum_tensor(name, shape, F32))

        m_rel = sb("m_rel", [P, RELS, HALF, P])
        w_a = sb("w_a", [P, TYPES * HALF, D])
        same_node = sb("same_node", [SEG, SUB])
        ones = sb("ones", [SEG, 1])
        skip = sb("skip", [P, TYPES])
        gain = sb("gain", [P, TYPES])
        acc = [sb(f"acc_in{k}", [SEG, PER_GROUP, HEADS, DK + 1]) for k in range(2)]
        x1 = [sb(f"x1o{k}", [GROUP, D]) for k in range(UN)]
        h1 = [sb(f"h1o{k}", [GROUP, D]) for k in range(UN)]
        kind_row = [sb(f"kind_row_o{k}", [P, GROUP], I32) for k in range(UN)]
        kind_col = [sb(f"kind_col_o{k}", [GROUP, 1], I32) for k in range(UN)]
        typed = [sb(f"typed{k}", [GROUP, 3 * D]) for k in range(UN)]
        of_kind = [sb(f"of_kind_o{k}", [P, TYPES, GROUP]) for k in range(UN)]
        row_kind = [sb(f"row_kind{k}", [GROUP, TYPES]) for k in range(UN)]
        alpha = [sb(f"alpha{k}", [GROUP, 1]) for k in range(UN)]
        mass = [sb(f"mass_o{k}", [SEG, PER_GROUP, HEADS]) for k in range(2)]
        inv = [sb(f"inv{k}", [SEG, PER_GROUP, HEADS]) for k in range(2)]
        here = [sb(f"here{k}", [SEG, PER_GROUP]) for k in range(2)]
        spread = [sb(f"spread{k}", [SEG, PER_GROUP, SUB]) for k in range(2)]
        mean = [sb(f"mean{k}", [SEG, PER_GROUP, D]) for k in range(2)]
        meanT = [sb(f"meanT{k}", [P, HALF, RELS, PER_GROUP, SUB]) for k in range(2)]
        tT = [sb(f"tT{k}", [P, TYPES, HALF, GROUP]) for k in range(2)]
        count = [sb(f"count{k}", [GROUP, 2]) for k in range(UN)]
        per_rel = [sb(f"per_rel{k}", [GROUP, 1]) for k in range(UN)]
        trans = [sb(f"trans{k}", [GROUP, D]) for k in range(UN)]
        mixed = [sb(f"mixed{k}", [GROUP, D]) for k in range(UN)]
        stat = [sb(f"stat_o{k}", [GROUP, 6]) for k in range(UN)]
        mv = [sb(f"mv_o{k}", [GROUP, 2]) for k in range(UN)]
        std = [sb(f"std_o{k}", [GROUP, 1]) for k in range(UN)]
        rstd = [sb(f"rstd_o{k}", [GROUP, 1]) for k in range(UN)]
        shift = [sb(f"shift_o{k}", [GROUP, 1]) for k in range(UN)]
        normed = [sb(f"normed{k}", [GROUP, D]) for k in range(UN)]
        xh = [sb(f"xh_o{k}", [GROUP, D]) for k in range(UN)]
        ba_less = [sb(f"ba_less{k}", [GROUP, D]) for k in range(UN)]
        beta_less = [sb(f"beta_less{k}", [GROUP, D]) for k in range(UN)]
        res = [sb(f"res{k}", [GROUP, D]) for k in range(UN)]
        meanT_p = [ps(f"meanT_p{k}", [P, 2, HALF, SEG]) for k in range(2)]
        tT_p = ps("tT_p", [P, HALF, GROUP])
        trans_p = ps("trans_p", [GROUP, D])
        count_p = ps("count_p", [GROUP, 1])

        w_loaded, gain_ready, filled = sem("w_out_loaded"), sem("gain_ready"), sem("out_filled")
        loaded, typed_got = sems("out_loaded", UN), sems("typed_gathered", UN)
        mass_ready, inv_ready, here_ready, mean_ready = sem("mass_o"), sem("inv_o"), sem("here_o"), sem("mean_o")
        spread_ready, count_summed, count_ready = sem("spread_o"), sem("count_summed"), sem("count_ready")
        meanT_turned, meanT_act, meanT_dve = sem("meanT_turned"), sem("meanT_act"), sem("meanT_dve")
        row_kind_ready, alpha_ready = sem("row_kind_o"), sem("alpha_o")
        tT_summed, tT_ready, trans_summed = sem("tT_summed"), sem("tT_ready"), sem("trans_summed")
        per_rel_ready, trans_ready, mixed_ready = sem("per_rel"), sem("trans_o"), sem("mixed_o")
        stat_ready, var_ready, std_ready = sem("stat_o"), sem("var_o"), sem("std_o")
        rstd_ready, shift_ready, normed_ready = sem("rstd_o"), sem("shift_o"), sem("normed_o")
        scaled_ready, affine_ready, xh_ready = sem("scaled_o"), sem("affine_o"), sem("xh_o")
        mean_pool, pool_less, res_ready = sem("mean_pool"), sem("pool_less"), sem("res_o")
        stored, held = sems("out_stored", UN), sem("out_held")
        LOADS, WEIGHTS = 5, 4
        PAIRS = PER_GROUP // 2

        DVE_SUBS = 4

        def weigh(eng, k, subs):
            n = len(range(*subs.indices(PER_GROUP)))
            return eng.tensor_tensor(mean[k][:, subs].rearrange("s j (h e) -> s j h e", h=HEADS),
                                     acc[k][:, subs, :, 0:DK],
                                     inv[k][:, subs].rearrange("s j (h o) -> s j h o", o=1).to_broadcast(
                                         [SEG, n, HEADS, DK]), ALU.mult)

        with nc.Block() as block:
            @block.sync
            def _(sp):
                for dst, src in ((m_rel[:], w0["m_rel"]), (w_a[:], w0["w_a"].rearrange("(a p) n -> p a n", p=P)),
                                 (same_node[:], w0["same_node"]), (skip[:], w0["skip"].to_broadcast([P, TYPES]))):
                    sp.dma_start(dst, src).then_inc(w_loaded, 16)

                def load(it):
                    k = it.slot(UN)
                    rows = ds(it.index * GROUP, GROUP)
                    wait(sp, mean_ready, it, 2)
                    sp.sem_inc(held, 1)
                    wait(sp, mean_pool, it, 2)
                    sp.sem_inc(held, 1)
                    wait(sp, res_ready, it, UN)
                    sp.dma_start(acc[it.slot(2)][:].rearrange("s j h e -> s j (h e)"),
                                 c["acc_d"].rearrange("(b s) f -> s b f", s=SEG)[
                                     :, ds(it.index * PER_GROUP, PER_GROUP), :]).then_inc(loaded[k], 16)
                    sp.dma_start(x1[k][:], c["x1_d"][rows, :]).then_inc(loaded[k], 16)
                    sp.dma_start(h1[k][:], c["h1_d"][rows, :]).then_inc(loaded[k], 16)
                    sp.dma_start(kind_row[k][:], c["node_type"][:, rows].to_broadcast([P, GROUP])
                                 ).then_inc(loaded[k], 16)
                    sp.dma_start(kind_col[k][:], c["node_type"].rearrange("o n -> n o")[rows, :]
                                 ).then_inc(loaded[k], 16)

                def store(it):
                    k = it.slot(UN)
                    wait(sp, res_ready, it)
                    sp.dma_start(c["out"][ds(it.index * GROUP, GROUP), :], res[k][:]).then_inc(stored[k], 16)

                run_stages(sp, GROUPS, ((0, load), (7, store)), UN)
                for k in range(UN):
                    sp.wait_ge(stored[k], 16 * len(range(k, GROUPS, UN)))

            @block.gpsimd
            def _(pool):
                def gather(it):
                    k = it.slot(UN)
                    wait_slot(pool, loaded, it, LOADS)
                    pool.sem_inc(held, 1)
                    wait(pool, affine_ready, it, UN)
                    pool.sem_inc(held, 1)
                    pool.indirect_dma_start(typed[k][:], None, w0["typed"],
                                            bass.IndirectOffsetOnAxis(ap=kind_col[k][:], axis=0)
                                            ).then_inc(typed_got[k], 16)
                    wait(pool, res_ready, it, UN)
                    pool.tensor_tensor(xh[k][:], x1[k][:], h1[k][:], ALU.add).then_inc(xh_ready, 1)

                def less_h(it):
                    k = it.slot(UN)
                    wait_slot(pool, typed_got, it)
                    wait(pool, mixed_ready, it, UN)
                    pool.tensor_tensor(ba_less[k][:], typed[k][:, 0:D], h1[k][:], ALU.subtract)
                    wait(pool, affine_ready, it, UN)
                    pool.tensor_tensor(beta_less[k][:], typed[k][:, 2 * D:3 * D], h1[k][:],
                                       ALU.subtract).then_inc(pool_less, 1)

                def means(it):
                    k = it.slot(2)
                    wait(pool, inv_ready, it)
                    wait(pool, meanT_turned, it, 2, per=PAIRS)
                    weigh(pool, k, slice(DVE_SUBS, PER_GROUP)).then_inc(mean_pool, 1)

                def affine(it):
                    k = it.slot(UN)
                    wait(pool, normed_ready, it)
                    pool.tensor_tensor(normed[k][:], normed[k][:], typed[k][:, D:2 * D], ALU.mult).then_inc(scaled_ready, 1)
                    wait(pool, scaled_ready, it)
                    pool.tensor_tensor(normed[k][:], normed[k][:], beta_less[k][:], ALU.add).then_inc(affine_ready, 1)

                run_stages(pool, GROUPS, ((5, affine), (0, gather), (0, means), (2, less_h)), UN)

            @block.scalar
            def _(act):
                act.wait_ge(w_loaded, 16 * WEIGHTS)
                act.activation(gain[:], skip[:], ACT.Sigmoid).then_inc(gain_ready, 1)

                def turn_out(it):
                    k = it.slot(2)
                    wait(act, tT_summed, it, 2)
                    for pair in range(0, PAIRS, 2):
                        act.wait_ge(meanT_turned, it.count(1, PAIRS, pair + 1))
                        for j in range(2):
                            ins = act.copy(meanT[k][:, :, :, 2 * pair + j, :],
                                           meanT_p[0][:, j].rearrange("p a (n r) -> p a r n", r=RELS))
                        ins.then_inc(meanT_act, 1)

                def root(it):
                    k = it.slot(UN)
                    wait(act, var_ready, it)
                    wait(act, shift_ready, it, UN)
                    act.activation(std[k][:], mv[k][:, 1:2], ACT.Sqrt, bias=c["eps"][0:GROUP, :]).then_inc(std_ready, 1)

                def norm(it):
                    k = it.slot(UN)
                    wait(act, shift_ready, it)
                    wait(act, res_ready, it, UN)
                    act.activation(normed[k][:], mixed[k][:], ACT.Identity, bias=shift[k][:],
                                   scale=rstd[k][:]).then_inc(normed_ready, 1)

                run_stages(act, GROUPS, ((1, turn_out), (4, norm), (3, root)), UN)

            @block.vector
            def _(dve):
                dve.memset(ones[:], 1.0).then_inc(filled, 1)
                dve.wait_ge(w_loaded, 16 * WEIGHTS)
                dve.wait_ge(gain_ready, 1)

                def kinds(it):
                    k = it.slot(UN)
                    wait_slot(dve, loaded, it, LOADS)
                    wait(dve, mixed_ready, it, UN)
                    for t in range(TYPES):
                        dve.tensor_scalar(of_kind[k][:, t, :], kind_row[k][:], float(t), None, ALU.is_equal)
                    dve.tensor_scalar(row_kind[k][:], c["iota"][0:GROUP, 0:TYPES], kind_col[k][:], None,
                                      ALU.is_equal).then_inc(row_kind_ready, 1)
                    wait(dve, row_kind_ready, it)
                    dve.sem_inc(held, 1)
                    dve.tensor_tensor_reduce(row_kind[k][:], row_kind[k][:], gain[0:GROUP, :], 1.0, 0.0, ALU.mult,
                                             ALU.add, alpha[k][:]).then_inc(alpha_ready, 1)

                def inverses(it):
                    k = it.slot(2)
                    wait_slot(dve, loaded, it, LOADS)
                    wait(dve, mean_ready, it, 2)
                    dve.tensor_scalar(mass[k][:], acc[k][:, :, :, DK], 0.5, None, ALU.max).then_inc(mass_ready, 1)
                    wait(dve, count_summed, it, 2)
                    dve.tensor_scalar(here[k][:], acc[k][:, :, 0, DK], 0.5, None, ALU.is_gt).then_inc(here_ready, 1)

                def means(it):
                    k = it.slot(2)
                    wait(dve, mass_ready, it)
                    wait(dve, mean_pool, it, 2)
                    dve.reciprocal(inv[k][:], mass[k][:]).then_inc(inv_ready, 1)
                    wait(dve, here_ready, it)
                    dve.tensor_tensor(spread[k][:], same_node[:].rearrange("s (o n) -> s o n", o=1).to_broadcast(
                        [SEG, PER_GROUP, SUB]), here[k][:].rearrange("s (j o) -> s j o", o=1).to_broadcast(
                        [SEG, PER_GROUP, SUB]), ALU.mult).then_inc(spread_ready, 1)
                    wait(dve, inv_ready, it)
                    wait(dve, meanT_turned, it, 2, per=PAIRS)
                    weigh(dve, k, slice(0, DVE_SUBS)).then_inc(mean_ready, 1)

                def turn_out(it):
                    k = it.slot(2)
                    wait(dve, tT_summed, it, 2)
                    dve.wait_ge(meanT_turned, it.count(1, PAIRS, 2))
                    for j in range(2):
                        ins = dve.tensor_copy(meanT[k][:, :, :, 2 + j, :],
                                              meanT_p[1][:, j].rearrange("p a (n r) -> p a r n", r=RELS))
                    ins.then_inc(meanT_dve, 1)

                def split_kinds(it):
                    k = it.slot(2)
                    wait(dve, tT_summed, it)
                    wait(dve, alpha_ready, it)
                    wait(dve, trans_summed, it, 2)
                    for t in range(TYPES):
                        ins = dve.tensor_tensor(tT[k][:, t], tT_p[:], of_kind[it.slot(UN)][:, t:t + 1, :].to_broadcast(
                            [P, HALF, GROUP]), ALU.mult)
                    ins.then_inc(tT_ready, 1)

                def counts(it):
                    k = it.slot(UN)
                    wait(dve, count_summed, it)
                    wait(dve, res_ready, it, UN)
                    dve.tensor_scalar(count[k][:, 0:1], count_p[:], 1.0, None, ALU.max)
                    dve.tensor_scalar(count[k][:, 1:2], count_p[:], 0.5, None, ALU.is_gt).then_inc(count_ready, 1)

                def per_relation(it):
                    k = it.slot(UN)
                    wait(dve, count_ready, it)
                    dve.reciprocal(per_rel[k][:], count[k][:, 0:1]).then_inc(per_rel_ready, 1)

                def transform(it):
                    k = it.slot(UN)
                    wait(dve, trans_summed, it)
                    wait(dve, per_rel_ready, it)
                    wait(dve, pool_less, it)
                    dve.scalar_tensor_tensor(trans[k][:], trans_p[:], per_rel[k][:], ba_less[k][:],
                                             ALU.mult, ALU.add).then_inc(trans_ready, 1)

                def mix(it):
                    k = it.slot(UN)
                    wait(dve, trans_ready, it)
                    wait(dve, normed_ready, it, UN)
                    dve.scalar_tensor_tensor(mixed[k][:], trans[k][:], alpha[k][:], h1[k][:],
                                             ALU.mult, ALU.add).then_inc(mixed_ready, 1)

                def stats(it):
                    k = it.slot(UN)
                    wait(dve, mixed_ready, it)
                    dve.bn_stats(stat[k][:], mixed[k][:]).then_inc(stat_ready, 1)

                def variance(it):
                    k = it.slot(UN)
                    wait(dve, stat_ready, it)
                    dve.sem_inc(held, 1)
                    wait(dve, shift_ready, it, UN)
                    dve.sem_inc(held, 1)
                    dve.bn_aggr(mv[k][:], stat[k][:]).then_inc(var_ready, 1)

                def scale(it):
                    k = it.slot(UN)
                    wait(dve, std_ready, it)
                    wait(dve, normed_ready, it, UN)
                    dve.reciprocal(rstd[k][:], std[k][:]).then_inc(rstd_ready, 1)

                def shifts(it):
                    k = it.slot(UN)
                    wait(dve, rstd_ready, it)
                    dve.scalar_tensor_tensor(shift[k][:], mv[k][:, 0:1], -1.0, rstd[k][:],
                                             ALU.mult, ALU.mult).then_inc(shift_ready, 1)

                def finish(it):
                    k = it.slot(UN)
                    wait(dve, affine_ready, it)
                    wait(dve, xh_ready, it)
                    if not (isinstance(it.i, int) and it.index < UN):
                        dve.wait_ge(stored[k], it.round(0) * 16)
                    dve.scalar_tensor_tensor(res[k][:], normed[k][:], count[k][:, 1:2], xh[k][:],
                                             ALU.mult, ALU.add).then_inc(res_ready, 1)

                run_stages(dve, GROUPS, ((3, split_kinds), (0, inverses), (4, scale), (0, kinds), (4, shifts), (0, means),
                                         (1, turn_out), (3, transform), (1, counts), (3, mix), (1, per_relation),
                                         (3, stats), (6, finish), (3, variance)), UN)

            @block.tensor
            def _(pe):
                pe.wait_ge(w_loaded, 16 * WEIGHTS)
                pe.wait_ge(filled, 1)

                def turn(it):
                    k = it.slot(2)
                    wait(pe, spread_ready, it)
                    wait(pe, count_ready, it, 1)
                    pe.matmul(count_p[:], spread[k][:].rearrange("s j n -> s (j n)"), ones[:], start=True,
                              stop=True).then_inc(count_summed, 1)
                    wait(pe, mean_ready, it)
                    wait(pe, mean_pool, it)
                    for pair in range(PAIRS):
                        if pair == 0:
                            wait(pe, meanT_act, it, 1, per=2)
                        elif pair == 1:
                            wait(pe, meanT_dve, it, 1)
                        else:
                            pe.wait_ge(meanT_act, it.count(1, 2, 1))
                        for j in range(2):
                            for a in range(HALF):
                                ins = pe.transpose(meanT_p[pair % 2][:, j, a, :],
                                                   mean[k][:, 2 * pair + j, a * P:(a + 1) * P],
                                                   c["ident"][0:SEG, 0:SEG])
                        ins.then_inc(meanT_turned, 1)

                def relate(it):
                    k = it.slot(2)
                    wait(pe, meanT_act, it, per=2)
                    wait(pe, meanT_dve, it)
                    wait(pe, tT_ready, it, 1)
                    for a in range(HALF):
                        for r in range(RELS):
                            ins = pe.matmul(tT_p[:, a, :], m_rel[:, r, a, :],
                                            meanT[k][:, a, r].rearrange("p j n -> p (j n)"),
                                            start=r == 0, stop=r == RELS - 1)
                    ins.then_inc(tT_summed, 1)

                def project(it):
                    k = it.slot(2)
                    wait(pe, tT_ready, it)
                    wait(pe, trans_ready, it, 1)
                    for a in range(TYPES * HALF):
                        ins = pe.matmul(trans_p[:], tT[k][:, a // HALF, a % HALF, :], w_a[:, a, :],
                                        start=a == 0, stop=a == TYPES * HALF - 1)
                    ins.then_inc(trans_summed, 1)

                run_stages(pe, GROUPS, ((1, turn), (3, project), (2, relate)), UN)


def device_arrays(a):
    def f(name):
        return np.ascontiguousarray(a[name])

    def padded(v, n, fill=0):
        out = np.full((n,) + v.shape[1:], fill, v.dtype)
        out[:v.shape[0]] = v
        return out

    rec = np.empty((EP, 4), np.int32)
    rec[:, 0] = padded(f("src").astype(np.int32, copy=False), EP)
    rec[:, 1] = padded(f("dst").astype(np.int32, copy=False), EP, RELS * N)
    rec[:, 2] = padded(f("edge_type_6").astype(np.int32, copy=False), EP)
    rec[:, 3] = padded(f("edge_weight"), EP).view(np.int32)
    a_rel, m_rel = np.zeros((P, HALF, RELS, P), np.float32), np.zeros((P, RELS, HALF, P), np.float32)
    prior = np.empty((P, HALF, RELS), np.float32)
    for h in range(HEADS):
        rows = slice(h % 2 * DK, h % 2 * DK + DK)
        for r in range(RELS):
            a_rel[rows, h // 2, r, rows] = f("L1_gnn_rel_att")[r, h].T
            m_rel[rows, r, h // 2, rows] = f("L1_gnn_rel_msg")[r, h]
            prior[rows, h // 2, r] = f("L1_gnn_rel_pri")[r, h]
    par1 = np.zeros((2, P, SUBS, 3), np.float32)
    par1[:, :, :, 0] = -(np.arange(P)[:, None] + SEG * np.arange(SUBS))
    par1[:, :, :, 1] = SEG * np.arange(SUBS)
    par1[0, :, :, 2] = -BIG
    spread_head = np.zeros((PARTS, HEADS, HEADS, SEG), np.float32)
    for h in range(HEADS):
        spread_head[:, h, h, :] = 1.0
    return {
        "x": padded(f("x"), NP),
        "rec": rec,
        "edge_feat_t": np.ascontiguousarray(padded(f("edge_attr_64"), EP).T),
        "node_type": padded(f("node_type_3").astype(np.int32, copy=False), NP)[None, :],
        "w_qkv": np.concatenate([f("L0_gnn_Wq").T, f("L0_gnn_Wk").T, f("L0_gnn_Wv").T], 1),
        "b_qkv": np.concatenate([f("L0_gnn_bq"), f("L0_gnn_bk"), f("L0_gnn_bv")])[None, :],
        "b_o": f("L0_gnn_bo")[None, :],
        "gamma_t": np.ascontiguousarray(f("L0_gnn_ln_g").reshape(HALF, P).T),
        "beta_t": np.ascontiguousarray(f("L0_gnn_ln_b").reshape(HALF, P).T),
        "w_edge": np.concatenate([f("L0_gnn_Wdk").T, f("L0_gnn_Wdv").T], 1),
        "b_edge": np.concatenate([f("L0_gnn_bdk"), f("L0_gnn_bdv")])[None, :],
        "ident": np.eye(P, dtype=np.float32),
        "iota": np.arange(GROUP, dtype=np.float32)[None, :],
        "begin": np.ascontiguousarray((SUB * np.arange(SUBS, dtype=np.float32)).reshape(SUB_COLS, SUB_ROWS).T),
        "w_o": f("L0_gnn_Wo").T,
        "w_kvq1": np.concatenate([f("L1_gnn_Wk"), f("L1_gnn_Wv"), f("L1_gnn_Wq")], 2).reshape(TYPES * D, 3 * D),
        "b_kvq1": np.concatenate([f("L1_gnn_bk"), f("L1_gnn_bv"), f("L1_gnn_bq")], 1),
        "a_rel": a_rel,
        "m_rel": m_rel,
        "prior": prior,
        "par1": par1.reshape(2 * P, 3 * SUBS),
        "spread_head": spread_head.reshape(PARTS * HEADS, HEADS, SEG).astype(mybir.dt.np(BF16)),
        "w_a": f("L1_gnn_Wa").reshape(TYPES * D, D),
        "typed": np.concatenate([f("L1_gnn_ba"), f("L1_gnn_ln_g"), f("L1_gnn_ln_b")], 1),
        "skip": f("L1_gnn_skip")[None, :],
        "same_node": (np.arange(SEG)[:, None] // RELS == np.arange(SUB)).astype(np.float32),
    }


def kernel(**inputs):
    import concourse.bacc as bacc
    from concourse.bass_utils import run_bass_kernel_spmd

    nc = bacc.Bacc("TRN2", target_bir_lowering=False, num_devices=1)
    arrays, aps = {}, {}
    for name, v in device_arrays(inputs).items():
        v = np.ascontiguousarray(v)
        arrays["in_" + name] = v
        aps[name] = nc.dram_tensor("in_" + name, v.shape, mybir.dt.from_np(v.dtype), kind="ExternalInput").ap()
    out = nc.dram_tensor("out_0", (NP, D), F32, kind="ExternalOutput").ap()
    build(nc, aps.pop("x"), aps.pop("rec"), aps.pop("edge_feat_t"), aps.pop("node_type"), aps, out)
    r = run_bass_kernel_spmd(nc, [arrays], core_ids=[0])
    return r.results[0]["out_0"][:N]
```
